# Optimizing a Trainium2 kernel written in Bass

```python
import numpy as np
import jax
import jax.numpy as jnp

def _softmax(x, axis=-1):
    return jax.nn.softmax(x, axis=axis)

def _gelu(x):
    return jax.nn.gelu(x, approximate=True)

def _silu(x):
    return jax.nn.silu(x)

def _sigmoid(x):
    return jax.nn.sigmoid(x)

def _layernorm(x, axis=-1, eps=1e-05):
    m = jnp.mean(x, axis=axis, keepdims=True)
    v = jnp.var(x, axis=axis, keepdims=True)
    return (x - m) / jnp.sqrt(v + eps)

def _scatter_add(tgt, idx, src, axis=0):
    return tgt.at[idx].add(src)

def _segment_sum(src, seg, n):
    return jax.ops.segment_sum(src, seg, n)
kernel_name = 'mk_sandwich_d1_jaxref_r2_2c6d74'

def setup_inputs(seed: int=0):
    np.random.seed(seed)
    _w = jnp.asarray

    def _L0_attn_setup():
        import jax, jax.numpy as jnp
        import numpy as np
        NUM_HEADS = 16
        key = jax.random.key(seed)
        ks = jax.random.split(key, 9)
        B, S, D = (2, 1024, 1024)
        scale = 1.0 / np.sqrt(D).astype(np.float32)
        x = jax.random.normal(ks[0], (B, S, D), jnp.float32)
        wq = jax.random.normal(ks[1], (D, D), jnp.float32) * scale
        wk = jax.random.normal(ks[2], (D, D), jnp.float32) * scale
        wv = jax.random.normal(ks[3], (D, D), jnp.float32) * scale
        wo = jax.random.normal(ks[4], (D, D), jnp.float32) * scale
        bq = jax.random.normal(ks[5], (D,), jnp.float32) * 0.02
        bk = jax.random.normal(ks[6], (D,), jnp.float32) * 0.02
        bv = jax.random.normal(ks[7], (D,), jnp.float32) * 0.02
        bo = jax.random.normal(ks[8], (D,), jnp.float32) * 0.02
        return {'x': x, 'wq': wq, 'bq': bq, 'wk': wk, 'bk': bk, 'wv': wv, 'bv': bv, 'wo': wo, 'bo': bo}
    _L0_attn_in = _L0_attn_setup()

    def _L0_ffn_setup():
        import jax, jax.numpy as jnp
        import numpy as np
        B, T, D = (4, 512, 1024)
        N, S, H = (8, 8, 8)
        ETA = 1.0
        key = jax.random.key(seed)
        ks = jax.random.split(key, 9)
        return {'x': jax.random.normal(ks[0], (B, T, D), jnp.float32), 'select_weight': jax.random.normal(ks[1], (N, D, S), jnp.float32) / D, 'select_mean_diff': jax.random.normal(ks[2], (N, D), jnp.float32) / D, 'imp_center': jax.random.normal(ks[3], (N,), jnp.float32), 'imp_slope': jax.random.normal(ks[4], (N,), jnp.float32) * 5.0, 'lora_update': jax.random.normal(ks[5], (N, D, H), jnp.float32) * 0.02, 'lora_degen': jax.random.normal(ks[6], (N, D, H), jnp.float32) * 0.02, 'bias_w': jax.random.normal(ks[7], (N, D), jnp.float32) * 0.02, 'debias_w': jax.random.normal(ks[8], (N, D), jnp.float32) * 0.02}
    _L0_ffn_in = _L0_ffn_setup()
    _d = {'L0_attn_x': _L0_attn_in['x'], 'L0_attn_wq': _L0_attn_in['wq'], 'L0_attn_bq': _L0_attn_in['bq'], 'L0_attn_wk': _L0_attn_in['wk'], 'L0_attn_bk': _L0_attn_in['bk'], 'L0_attn_wv': _L0_attn_in['wv'], 'L0_attn_bv': _L0_attn_in['bv'], 'L0_attn_wo': _L0_attn_in['wo'], 'L0_attn_bo': _L0_attn_in['bo'], 'L0_ffn_select_weight': _L0_ffn_in['select_weight'], 'L0_ffn_select_mean_diff': _L0_ffn_in['select_mean_diff'], 'L0_ffn_imp_center': _L0_ffn_in['imp_center'], 'L0_ffn_imp_slope': _L0_ffn_in['imp_slope'], 'L0_ffn_lora_update': _L0_ffn_in['lora_update'], 'L0_ffn_lora_degen': _L0_ffn_in['lora_degen'], 'L0_ffn_bias_w': _L0_ffn_in['bias_w'], 'L0_ffn_debias_w': _L0_ffn_in['debias_w']}
    _x0 = _d['L0_attn_x']
    _d['L0_attn_x'] = jax.random.normal(jax.random.fold_in(jax.random.key(seed), 1), (2, 2048, 1024), dtype=_x0.dtype)
    del _x0
    return _d

def reference(L0_attn_x, L0_attn_wq, L0_attn_bq, L0_attn_wk, L0_attn_bk, L0_attn_wv, L0_attn_bv, L0_attn_wo, L0_attn_bo, L0_ffn_select_weight, L0_ffn_select_mean_diff, L0_ffn_imp_center, L0_ffn_imp_slope, L0_ffn_lora_update, L0_ffn_lora_degen, L0_ffn_bias_w, L0_ffn_debias_w):

    def _L0_attn_ref(x, wq, bq, wk, bk, wv, bv, wo, bo):
        import jax, jax.numpy as jnp
        import numpy as np
        NUM_HEADS = 16
        B, S, D = x.shape
        H = NUM_HEADS
        hd = D // H
        inv_sqrt_hd = jnp.float32(1.0 / np.sqrt(hd))
        q = (x @ wq.T + bq).reshape(B, S, H, hd)
        k = (x @ wk.T + bk).reshape(B, S, H, hd)
        v = (x @ wv.T + bv).reshape(B, S, H, hd)
        scores = jnp.einsum('bqhd,bkhd->bhqk', q, k) * inv_sqrt_hd
        causal = jnp.triu(jnp.ones((S, S), dtype=bool), k=1)
        scores = jnp.where(causal[None, None, :, :], -jnp.inf, scores)
        probs = jax.nn.softmax(scores, axis=-1)
        attn = jnp.einsum('bhqk,bkhd->bqhd', probs, v).reshape(B, S, D)
        return attn @ wo.T + bo

    def _L0_ffn_ref(x, select_weight, select_mean_diff, imp_center, imp_slope, lora_update, lora_degen, bias_w, debias_w):
        import jax, jax.numpy as jnp
        import numpy as np
        B, T, D = (4, 512, 1024)
        N, S, H = (8, 8, 8)
        ETA = 1.0
        x_diff = x[:, None, :, :] - select_mean_diff[None, :, None, :]
        x_diff = x_diff / jnp.linalg.norm(x_diff, axis=3, keepdims=True)
        cont = jnp.einsum('nds,bntd->bnts', select_weight, x_diff) ** 2
        score = cont.sum(axis=-1)
        gate = jax.nn.sigmoid(imp_slope[None, :, None] * (score - imp_center[None, :, None]))
        sel_scale = gate.max(axis=1)[..., None]
        sel_idx = gate.argmax(axis=1)
        debias = jnp.take(debias_w, sel_idx, axis=0)
        bias = jnp.take(bias_w, sel_idx, axis=0)
        upd = jnp.take(lora_update, sel_idx, axis=0)
        dgn = jnp.take(lora_degen, sel_idx, axis=0)
        x_debias = x - debias
        mod_x = jnp.einsum('btdh,btd->bth', upd, x_debias)
        degen_up = jnp.einsum('btdh,bth->btd', dgn, mod_x)
        mod_x_bias = ETA * (bias + degen_up)
        return (1.0 - sel_scale) * x + sel_scale * mod_x_bias
    x = L0_attn_x
    x = x + _layernorm(_L0_attn_ref(_layernorm(x, axis=-1), L0_attn_wq, L0_attn_bq, L0_attn_wk, L0_attn_bk, L0_attn_wv, L0_attn_bv, L0_attn_wo, L0_attn_bo), axis=-1)
    x = x + _layernorm(_L0_ffn_ref(_layernorm(x, axis=-1), L0_ffn_select_weight, L0_ffn_select_mean_diff, L0_ffn_imp_center, L0_ffn_imp_slope, L0_ffn_lora_update, L0_ffn_lora_degen, L0_ffn_bias_w, L0_ffn_debias_w), axis=-1)
    return x

_drawn_inputs = setup_inputs


def setup_inputs(seed=0):
    import zlib

    import numpy as np

    out = dict(_drawn_inputs(seed))
    spreads = {}
    factors = {'L0_attn_bq': 4.513, 'L0_attn_bk': 8.0, 'L0_ffn_debias_w': 5.239}
    for name, (base, spread) in spreads.items():
        noise = np.random.default_rng([zlib.crc32(name.encode()), seed]).standard_normal(out[name].shape)
        drawn = base * np.exp(spread * noise) if base else spread * noise
        out[name] = jnp.asarray(drawn.astype(out[name].dtype))
    for name, factor in factors.items():
        out[name] = (out[name] * factor).astype(out[name].dtype)
    return out
```

```python
from contextlib import ExitStack

import concourse.bass as bass
from concourse import mybir

ALU = mybir.AluOpType
ACT = mybir.ActivationFunctionType
F32 = mybir.dt.float32
F16 = mybir.dt.float16
BF16 = mybir.dt.bfloat16
AX_X = mybir.AxisListType.X

P = 128
B, S, D, H = 2, 2048, 1024, 16
HD = D // H
BH = B * H
KT = D // P
EPS = 1e-5
TOK = 512
SUB = TOK // P
NC = S // TOK
QT = S // P
N_EXP, N_SEL, N_LOW = 8, 8, 8
FF = N_EXP * N_SEL + N_EXP * N_LOW + N_EXP
MIX = N_EXP * N_LOW + N_EXP

X_SCALE, W_SCALE, QKV_SCALE, P_SCALE = 2.0 ** 4, 2.0 ** 8, 2.0 ** 3, 2.0 ** 15
PROJ_UNSCALE = QKV_SCALE / (X_SCALE * W_SCALE)
SOFTMAX_SCALE = HD ** -0.5 / QKV_SCALE ** 2
OUT_UNSCALE = 1.0 / (QKV_SCALE * W_SCALE)


def project_phase(nc, x, w_qkv, b_cols, b_v, ident_in, q_scratch, k_scratch, v_scratch):
    with ExitStack() as ctx:
        sb = lambda name, shape, dt: ctx.enter_context(nc.sbuf_tensor(name, shape, dt))
        psum = lambda name, shape: ctx.enter_context(nc.psum_tensor(name, shape, F32))
        sem = lambda name: ctx.enter_context(nc.semaphore(name))
        NT = B * NC
        N_QK = 2 * D // P
        N_V = SUB * D // 512
        WRING = 3

        ident = sb("ident_a", [P, P], F32)
        bias_cols = sb("bias_cols", [P, N_QK], F32)
        bias_scaled = sb("bias_scaled", [P, N_QK], F32)
        bv_row = sb("bv_row", [P, D], F32)
        w_raw = sb("w_raw", [P, WRING, D], F32)
        w_hi = sb("w_hi", [P, 3, KT, D], F16)
        w_lo = sb("w_lo", [P, 3, KT, D], F16)
        x_in = sb("x_in", [P, SUB, D], F32)
        stats = sb("stats_a", [P, SUB, 2, 6], F32)
        moments = sb("moments_a", [P, SUB, 2], F32)
        var_eps = sb("var_eps_a", [P, SUB], F32)
        rstd = sb("rstd_a", [P, SUB], F32)
        eps = sb("eps_a", [P, SUB], F32)
        minus_half = sb("minus_half_a", [P, SUB], F32)
        x_norm = sb("x_norm", [P, SUB, D], F32)
        xt_hi = sb("xt_hi", [P, 2, KT, TOK], F16)
        xt_lo = sb("xt_lo", [P, 2, KT, TOK], F16)
        qk_full = sb("qk_full", [P, 4, TOK], F32)
        qk_split = sb("qk_split", [P, 4, 2, TOK], F16)
        v_full = sb("v_full", [P, 2, 512], F32)
        v_split = sb("v_split", [P, 2, H, 2, HD], F16)

        tr_ps = [psum(f"tr_ps{i}", [P, TOK]) for i in range(2)]
        qk_ps = [psum(f"qk_ps{i}", [P, TOK]) for i in range(4)]
        v_ps = [psum(f"v_ps{i}", [P, 512]) for i in range(2)]

        consts_loaded = sem("consts_loaded_a")
        set_done = sem("set_done_a")
        consts_scaled = sem("consts_scaled_a")
        w_loaded = [sem(f"w_loaded{i}") for i in range(WRING)]
        w_hi_done = sem("w_hi_done")
        w_lo_done = sem("w_lo_done")
        x_loaded = sem("x_loaded_a")
        stats_done = sem("stats_done_a")
        moments_done = sem("moments_done_a")
        var_done = sem("var_done_a")
        rstd_done = sem("rstd_done_a")
        x_norm_done = sem("x_norm_done")
        tr_done = sem("tr_done")
        xt_hi_done = sem("xt_hi_done")
        xt_lo_done = sem("xt_lo_done")
        qk_ps_done = sem("qk_ps_done")
        qk_full_done = sem("qk_full_done")
        qk_hi_done = sem("qk_hi_done")
        qk_lo_done = sem("qk_lo_done")
        qk_stored = [sem(f"qk_stored{i}") for i in range(4)]
        v_ps_done = sem("v_ps_done")
        v_full_done = sem("v_full_done")
        v_hi_done = sem("v_hi_done")
        v_lo_done = sem("v_lo_done")
        v_stored = [sem(f"v_stored{i}") for i in range(2)]

        x_view = x.rearrange("(b c s p) d -> b c p s d", b=B, c=NC, s=SUB)
        w_view = w_qkv.rearrange("m (k p) o -> m k p o", p=P)
        q_view = q_scratch.rearrange("c (b g h) f l n -> c b g (h f) l n", b=B, h=2)
        k_view = k_scratch.rearrange("c (b g h) f l n -> c b g (h f) l n", b=B, h=2)
        v_view = v_scratch.rearrange("(b h) p (c s) e -> b c s p h e", b=B, s=SUB)

        def tiles(eng, step):
            step(0, 0, 0, True, False)
            with eng.Fori(0, NC - 1) as i:
                step(2 * i + 1, i, 1, False, False)
                step(2 * i + 2, i + 1, 0, False, False)
            step(NT - 1, NC - 1, 1, False, True)

        block = ctx.enter_context(nc.Block())

        @block.sync
        def _(sp):
            sp.dma_start(x_in[:], x_view[0, 0]).then_inc(x_loaded, 16)
            sp.dma_start(ident[:], ident_in).then_inc(consts_loaded, 16)
            sp.dma_start(bias_cols[:], b_cols).then_inc(consts_loaded, 16)
            sp.dma_start(bv_row[:], b_v.partition_broadcast(P)).then_inc(consts_loaded, 16)

            def load_weight(n):
                if n >= WRING:
                    sp.wait_ge(w_lo_done, n - WRING + 1)
                sp.dma_start(w_raw[:, n % WRING, :], w_view[n // KT, n % KT]).then_inc(w_loaded[n % WRING], 16)

            def step(n, c, b, first, last):
                if first:
                    for k in range(KT):
                        load_weight(k)
                if not last:
                    sp.wait_ge(x_norm_done, SUB * n + SUB)
                    sp.dma_start(x_in[:], x_view[1, c] if b == 0 else x_view[0, c + 1]).then_inc(x_loaded, 16)
                if first:
                    for k in range(WRING):
                        load_weight(KT + k)
                for j in range(N_QK):
                    if first and KT + j + WRING < 3 * KT:
                        load_weight(KT + j + WRING)
                    sp.wait_ge(qk_lo_done, N_QK * n + j + 1)
                    view = q_view if j < KT else k_view
                    sp.dma_start(view[c, b, j % KT], qk_split[:, j % 4]).then_inc(qk_stored[j % 4], 16)
                for s in range(SUB):
                    sp.wait_ge(v_lo_done, N_V * n + 2 * s + 2)
                    sp.dma_start(v_view[b, c, s], v_split[:, s % 2].rearrange("p h l f -> p h (l f)")).then_inc(
                        v_stored[s % 2], 16)
            tiles(sp, step)
            for i in range(4):
                sp.wait_ge(qk_stored[i], 16 * (NT * N_QK // 4 + 1))
            for i in range(2):
                sp.wait_ge(v_stored[i], 16 * (NT * SUB // 2 + 1))

        @block.gpsimd
        def _(pool):
            nc.gpsimd.memset(eps[:], EPS).then_inc(set_done, 1)
            nc.gpsimd.memset(minus_half[:], -0.5).then_inc(set_done, 1)
            pool.wait_ge(set_done, 2)
            for i in range(4):
                pool.sem_inc(qk_stored[i], 16)
            for i in range(2):
                pool.sem_inc(v_stored[i], 16)

            def norm_scale(n):
                pool.wait_ge(moments_done, n + 1)
                nc.gpsimd.tensor_tensor(var_eps[:], moments[:, :, 1], eps[:], ALU.add).then_inc(var_done, 1)
                pool.wait_ge(var_done, n + 1)
                nc.gpsimd.tensor_tensor(rstd[:], var_eps[:], minus_half[:], ALU.pow).then_inc(rstd_done, 1)

            def step(n, c, b, first, last):
                if first:
                    norm_scale(0)
                if not last:
                    norm_scale(n + 1)
            tiles(pool, step)

        @block.vector
        def _(dve):
            dve.wait_ge(consts_loaded, 48)
            nc.vector.tensor_scalar(bias_scaled[:], bias_cols[:], QKV_SCALE, None, ALU.mult).then_inc(consts_scaled, 1)
            nc.vector.tensor_scalar(bv_row[:], bv_row[:], QKV_SCALE, None, ALU.mult).then_inc(consts_scaled, 1)

            def norm_stats(n):
                dve.wait_ge(x_loaded, 16 * n + 16)
                for s in range(SUB):
                    for h in range(2):
                        last = nc.vector.bn_stats(stats[:, s, h, :], x_in[:, s, h * 512:(h + 1) * 512])
                last.then_inc(stats_done, 1)
                dve.wait_ge(stats_done, 1)
                dve.sem_clear(stats_done)
                for s in range(SUB):
                    last = nc.vector.bn_aggr(moments[:, s, :], stats[:, s].rearrange("p h e -> p (h e)"))
                last.then_inc(moments_done, 1)

            def norm_apply(n):
                dve.wait_ge(rstd_done, n + 1)
                if not isinstance(n, int) or n > 0:
                    dve.wait_ge(tr_done, KT * n)
                for s in range(SUB):
                    nc.vector.tensor_scalar(x_norm[:, s, :], x_in[:, s, :], moments[:, s, 0:1], rstd[:, s:s + 1],
                                            ALU.subtract, ALU.mult).then_inc(x_norm_done, 1)

            def xt_low(n, b, k):
                dve.wait_ge(xt_hi_done, KT * n + k + 1)
                nc.vector.scalar_tensor_tensor(xt_lo[:, b, k, :], tr_ps[k % 2][:], X_SCALE, xt_hi[:, b, k, :],
                                               ALU.mult, ALU.subtract).then_inc(xt_lo_done, 1)

            def split_weight(m, k):
                n = m * KT + k
                dve.wait_ge(w_hi_done, n + 1)
                nc.vector.scalar_tensor_tensor(w_lo[:, m, k, :], w_raw[:, n % WRING, :], W_SCALE, w_hi[:, m, k, :],
                                               ALU.mult, ALU.subtract).then_inc(w_lo_done, 1)

            def step(n, c, b, first, last):
                if first:
                    norm_stats(0)
                    norm_apply(0)
                    for k in range(KT):
                        xt_low(0, 0, k)
                    for k in range(KT):
                        split_weight(0, k)
                for j in range(N_QK):
                    if first:
                        split_weight(1 + j // KT, j % KT)
                    dve.wait_ge(qk_hi_done, N_QK * n + j + 1)
                    nc.vector.tensor_tensor(qk_split[:, j % 4, 1, :], qk_full[:, j % 4, :], qk_split[:, j % 4, 0, :],
                                            ALU.subtract).then_inc(qk_lo_done, 1)
                    if not last:
                        if j == 1:
                            norm_stats(n + 1)
                        if j == 2:
                            norm_apply(n + 1)
                        if j >= KT:
                            xt_low(n + 1, 1 - b, j - KT)
                def v_low(j):
                    dve.wait_ge(v_hi_done, N_V * n + j + 1)
                    s, half = j // 2, j % 2
                    heads = slice(half * H // 2, (half + 1) * H // 2)
                    nc.vector.tensor_tensor(v_split[:, s % 2, heads, 1, :],
                                            v_full[:, j % 2, :].rearrange("p (h f) -> p h f", f=HD),
                                            v_split[:, s % 2, heads, 0, :], ALU.subtract).then_inc(v_lo_done, 1)
                for j in range(N_V):
                    half = j % 2
                    dve.wait_ge(v_ps_done, N_V * n + j + 1)
                    if not first or j >= 2:
                        dve.wait_ge(v_lo_done, N_V * n + j - 1)
                    nc.vector.scalar_tensor_tensor(v_full[:, j % 2, :], v_ps[j % 2][:], PROJ_UNSCALE,
                                                   bv_row[:, half * 512:(half + 1) * 512],
                                                   ALU.mult, ALU.add).then_inc(v_full_done, 1)
                    if j >= 1:
                        v_low(j - 1)
                v_low(N_V - 1)
            dve.wait_ge(consts_scaled, 2)
            tiles(dve, step)

        @block.scalar
        def _(act):
            act.wait_ge(consts_scaled, 2)

            def xt_high(n, b, k):
                act.wait_ge(tr_done, KT * n + k + 1)
                nc.scalar.activation(xt_hi[:, b, k, :], tr_ps[k % 2][:], ACT.Copy, scale=X_SCALE).then_inc(
                    xt_hi_done, 1)

            def split_weight(m, k):
                n = m * KT + k
                act.wait_ge(w_loaded[n % WRING], 16 * (n // WRING + 1))
                nc.scalar.activation(w_hi[:, m, k, :], w_raw[:, n % WRING, :], ACT.Copy, scale=W_SCALE).then_inc(
                    w_hi_done, 1)

            def step(n, c, b, first, last):
                if first:
                    for k in range(KT):
                        xt_high(0, 0, k)
                    for k in range(KT):
                        split_weight(0, k)
                for j in range(N_QK):
                    if first:
                        split_weight(1 + j // KT, j % KT)
                    act.wait_ge(qk_ps_done, N_QK * n + j + 1)
                    if not first or j >= 4:
                        act.wait_ge(qk_lo_done, N_QK * n + j - 3)
                    act.wait_ge(qk_stored[j % 4], 16 * (N_QK // 4 * n + j // 4 + 1))
                    nc.scalar.activation(qk_full[:, j % 4, :], qk_ps[j % 4][:], ACT.Identity,
                                         bias=bias_scaled[:, j:j + 1], scale=PROJ_UNSCALE).then_inc(qk_full_done, 1)
                    nc.scalar.activation(qk_split[:, j % 4, 0, :], qk_ps[j % 4][:], ACT.Identity,
                                         bias=bias_scaled[:, j:j + 1], scale=PROJ_UNSCALE).then_inc(qk_hi_done, 1)
                    if not last and j >= KT:
                        xt_high(n + 1, 1 - b, j - KT)
                for j in range(N_V):
                    s, half = j // 2, j % 2
                    heads = slice(half * H // 2, (half + 1) * H // 2)
                    act.wait_ge(v_full_done, N_V * n + j + 1)
                    if half == 0:
                        act.wait_ge(v_stored[s % 2], 16 * (SUB // 2 * n + s // 2 + 1))
                    nc.scalar.activation(v_split[:, s % 2, heads, 0, :],
                                         v_full[:, j % 2, :].rearrange("p (h f) -> p h f", f=HD),
                                         ACT.Copy).then_inc(v_hi_done, 1)
            tiles(act, step)

        @block.tensor
        def _(pe):
            def transposes(n, k):
                if not isinstance(n, int) or n > 0 or k >= 2:
                    pe.wait_ge(xt_lo_done, KT * n + k - 1)
                for s in range(SUB):
                    last = nc.tensor.transpose(tr_ps[k % 2][:, s * P:(s + 1) * P], x_norm[:, s, k * P:(k + 1) * P],
                                               ident[:])
                last.then_inc(tr_done, 1)

            def step(n, c, b, first, last):
                if first:
                    pe.wait_ge(consts_loaded, 48)
                    pe.wait_ge(x_norm_done, SUB)
                    for k in range(KT):
                        transposes(0, k)
                pe.wait_ge(xt_lo_done, KT * n + KT)
                for j in range(N_QK):
                    m, cols = j // KT, slice((j % KT) * P, (j % KT + 1) * P)
                    if first and j % KT == 0:
                        pe.wait_ge(w_lo_done, KT * (m + 1))
                    if not first or j >= 4:
                        pe.wait_ge(qk_hi_done, N_QK * n + j - 3)
                    for k in range(KT):
                        nc.tensor.matmul(qk_ps[j % 4][:], w_lo[:, m, k, cols], xt_hi[:, b, k, :], start=(k == 0),
                                         stop=False)
                        nc.tensor.matmul(qk_ps[j % 4][:], w_hi[:, m, k, cols], xt_lo[:, b, k, :], start=False,
                                         stop=False)
                        mm = nc.tensor.matmul(qk_ps[j % 4][:], w_hi[:, m, k, cols], xt_hi[:, b, k, :], start=False,
                                              stop=(k == KT - 1))
                    mm.then_inc(qk_ps_done, 1)
                    if not last and j >= KT:
                        if j == KT:
                            pe.wait_ge(x_norm_done, SUB * n + 2 * SUB)
                        transposes(n + 1, j - KT)
                if first:
                    pe.wait_ge(w_lo_done, 3 * KT)
                for j in range(N_V):
                    toks, cols = slice(j // 2 * P, (j // 2 + 1) * P), slice(j % 2 * 512, (j % 2 + 1) * 512)
                    if not first or j >= 2:
                        pe.wait_ge(v_full_done, N_V * n + j - 1)
                    for k in range(KT):
                        nc.tensor.matmul(v_ps[j % 2][:], xt_lo[:, b, k, toks], w_hi[:, 2, k, cols], start=(k == 0),
                                         stop=False)
                        nc.tensor.matmul(v_ps[j % 2][:], xt_hi[:, b, k, toks], w_lo[:, 2, k, cols], start=False,
                                         stop=False)
                        mm = nc.tensor.matmul(v_ps[j % 2][:], xt_hi[:, b, k, toks], w_hi[:, 2, k, cols], start=False,
                                              stop=(k == KT - 1))
                    mm.then_inc(v_ps_done, 1)
            tiles(pe, step)


UNIT_KEYS = 8
UNITS = []
for t in range(QT):
    cut = t + 1 if t < UNIT_KEYS else (t + 2) // 2
    UNITS += [(t, k, n) for k, n in ((0, cut), (cut, t + 1 - cut)) if n]
NU = len(UNITS)
N_ONE = UNIT_KEYS
N_TWO = QT - UNIT_KEYS
GROUPS = []
for u, (_, _, n) in enumerate(UNITS):
    cut = n if n <= 4 else (n + 1) // 2
    GROUPS += [(u, j, m) for j, m in ((0, cut), (cut, n - cut)) if m]
NG = len(GROUPS)
PT_SLOT = [2 * (u % 2) + (j > 0) for u, j, _ in GROUPS]
UNIT_GROUPS = [[g for g in range(NG) if GROUPS[g][0] == u] for u in range(NU)]
HEAD_LOADS = 7
MERGE = {"top": 2, "shrink": 4, "invert": 7, "scale": 9, "add": 16}


def attend_phase(nc, q_scratch, k_scratch, v_scratch, o_scratch, ident_in, mask_in):
    with ExitStack() as ctx:
        sb = lambda name, shape, dt: ctx.enter_context(nc.sbuf_tensor(name, shape, dt))
        psum = lambda name, shape: ctx.enter_context(nc.psum_tensor(name, shape, F32))
        sem = lambda name: ctx.enter_context(nc.semaphore(name))

        ident = sb("ident_b", [P, P], F32)
        ident16 = sb("ident16", [P, P], BF16)
        mask = sb("mask", [P, P], BF16)
        q_hi2 = [sb(f"q_hi2_{i}", [P, S], F16) for i in range(2)]
        q_lo2 = [sb(f"q_lo2_{i}", [P, S], F16) for i in range(2)]
        k_both = [sb(f"k_both_{i}", [P, S], F16) for i in range(2)]
        v_both = [sb(f"v_both_{i}", [P, QT, 2, HD], F16) for i in range(2)]
        probs = [sb(f"probs{i}", [P, UNIT_KEYS * P], F32) for i in range(3)]
        pt_hi = sb("pt_hi", [P, 4, 4 * P], F16)
        pt_lo = sb("pt_lo", [P, 4, 4 * P], F16)
        row_max = [sb(f"row_max{i}", [P, NU], F32) for i in range(2)]
        neg_max = [sb(f"neg_max{i}", [P, NU], F32) for i in range(2)]
        row_sum = [sb(f"row_sum{i}", [P, NU], F32) for i in range(2)]
        o_unit = [sb(f"o_unit{i}", [P, NU, HD], F32) for i in range(2)]
        o_head = [sb(f"o_head{i}", [P, QT, HD], F32) for i in range(2)]
        neg_scale = sb("neg_scale", [P, 1], F32)
        neg_top = sb("neg_top", [P, N_TWO], F32)
        gap = sb("gap", [P, N_TWO, 2], F32)
        shrink = sb("shrink", [P, N_TWO, 2], F32)
        sum_part = sb("sum_part", [P, N_TWO, 2], F32)
        sum_all = sb("sum_all", [P, QT], F32)
        inv_sum = sb("inv_sum", [P, QT], F32)
        weight = sb("weight", [P, NU], F32)

        s_ps = [psum(f"s_ps{i}", [P, UNIT_KEYS * P]) for i in range(2)]
        t_ps = [psum(f"t_ps{i}", [P, 4 * P]) for i in range(3)]
        o_ps = psum("o_ps", [P, HD])

        consts_loaded = sem("consts_loaded_b")
        head_loaded = [sem(f"head_loaded{i}") for i in range(2)]
        ident16_done = sem("ident16_done")
        set_done = sem("set_done_b")
        s_done = sem("s_done")
        max_done = sem("max_done")
        neg_done = sem("neg_done")
        exp_done = sem("exp_done")
        t_done = sem("t_done")
        pt_hi_done = sem("pt_hi_done")
        pt_lo_done = sem("pt_lo_done")
        pv_done = sem("pv_done")
        o_unit_done = sem("o_unit_done")
        top_done = sem("top_done")
        gap_done = sem("gap_done")
        shrink_done = sem("shrink_done")
        part_done = sem("part_done")
        sum_done = sem("sum_done")
        inv_done = sem("inv_done")
        weight_done = sem("weight_done")
        scaled_done = sem("scaled_done")
        merged_done = sem("merged_done")
        o_stored = [sem(f"o_stored{i}") for i in range(2)]

        def heads(eng, head):
            head(0, 0, 0, True, False)
            with eng.Fori(0, BH // 2 - 1) as i:
                head(2 * i + 1, 1, i, False, False)
                head(2 * i + 2, 0, i + 1, False, False)
            head(BH - 1, 1, BH // 2 - 1, False, True)

        def t_bank(g):
            u, j, _ = GROUPS[g]
            return t_ps[2] if j else t_ps[u % 2]

        block = ctx.enter_context(nc.Block())

        @block.sync
        def _(sp):
            sp.dma_start(ident[:], ident_in).then_inc(consts_loaded, 16)
            sp.dma_start(mask[:], mask_in).then_inc(consts_loaded, 16)

            def load(n, slot):
                halves = (slice(0, HD), slice(HD, P))
                for part, tile in ((0, q_hi2), (1, q_lo2)):
                    for rows in halves:
                        sp.dma_start(tile[slot][rows, :].rearrange("f (c n) -> f c n", c=NC),
                                     q_scratch[:, n, :, part, :].rearrange("c f n -> f c n")).then_inc(
                            head_loaded[slot], 16)
                for part, rows in enumerate(halves):
                    sp.dma_start(k_both[slot][rows, :].rearrange("f (c n) -> f c n", c=NC),
                                 k_scratch[:, n, :, part, :].rearrange("c f n -> f c n")).then_inc(
                        head_loaded[slot], 16)
                sp.dma_start(v_both[slot][:].rearrange("p t l f -> p (t l f)"),
                             v_scratch[n].rearrange("p t e -> p (t e)")).then_inc(head_loaded[slot], 16)

            def store(n, slot):
                sp.wait_ge(merged_done, 2 * n + 2)
                sp.dma_start(o_scratch[n], o_head[slot][:].rearrange("p t f -> p (t f)")).then_inc(o_stored[slot], 16)

            load(0, 0)
            load(1, 1)
            with sp.Fori(0, BH // 2 - 1) as i:
                for slot in range(2):
                    n = 2 * i + 2 + slot
                    sp.wait_ge(pv_done, NU * n - NU)
                    load(n, slot)
                    store(n - 2, slot)
            store(BH - 2, 0)
            store(BH - 1, 1)
            for slot in range(2):
                sp.wait_ge(o_stored[slot], 16 * (BH // 2 + 1))

        @block.tensor
        def _(pe):
            def scores(u, n, slot, use):
                t, k0, blocks = UNITS[u]
                if u == 0:
                    pe.wait_ge(head_loaded[slot], 16 * HEAD_LOADS * use + 16 * HEAD_LOADS)
                for j in range(0, blocks, 4):
                    w = min(4, blocks - j) * P
                    keys = slice((k0 + j) * P, (k0 + j) * P + w)
                    dst = s_ps[u % 2][:, j * P:j * P + w]
                    diagonal = k0 + j + w // P == t + 1
                    nc.tensor.matmul(dst, q_lo2[slot][:, t * P:(t + 1) * P], k_both[slot][:, keys], start=True,
                                     stop=False)
                    mm = nc.tensor.matmul(dst, q_hi2[slot][:, t * P:(t + 1) * P], k_both[slot][:, keys], start=False,
                                          stop=not diagonal)
                    if diagonal:
                        mm = nc.tensor.matmul(dst[:, w - P:w], ident16[:], mask[:], start=False, stop=True)
                mm.then_inc(s_done, 1)

            def transposes(g, n):
                u, j, blocks = GROUPS[g]
                if j == 0:
                    pe.wait_ge(exp_done, NU * n + u + 1)
                before = [x for x in range(NG) if t_bank(x) is t_bank(g)]
                back = max([x for x in before if x < g], default=before[-1] - NG)
                if not isinstance(n, int) or NG * n + back >= 0:
                    pe.wait_ge(pt_lo_done, NG * n + back + 1)
                for i in range(blocks):
                    tr = nc.tensor.transpose(t_bank(g)[:, i * P:(i + 1) * P],
                                             probs[u % 3][:, (j + i) * P:(j + i + 1) * P], ident[:])
                tr.then_inc(t_done, 1)

            def times_v(u, n, slot):
                t, k0, blocks = UNITS[u]
                if not isinstance(n, int) or NU * n + u > 0:
                    pe.wait_ge(o_unit_done, NU * n + u)
                for g in UNIT_GROUPS[u]:
                    _, j, count = GROUPS[g]
                    pe.wait_ge(pt_lo_done, NG * n + g + 1)
                    for i in range(count):
                        at = slice(i * P, (i + 1) * P)
                        kb = k0 + j + i
                        nc.tensor.matmul(o_ps[:], pt_lo[:, PT_SLOT[g], at], v_both[slot][:, kb, 0, :], start=(j + i == 0),
                                         stop=False)
                        nc.tensor.matmul(o_ps[:], pt_hi[:, PT_SLOT[g], at], v_both[slot][:, kb, 1, :], start=False,
                                         stop=False)
                        mm = nc.tensor.matmul(o_ps[:], pt_hi[:, PT_SLOT[g], at], v_both[slot][:, kb, 0, :], start=False,
                                              stop=(j + i == blocks - 1))
                mm.then_inc(pv_done, 1)

            def head(n, slot, use, first, last):
                if first:
                    scores(0, n, slot, use)
                    scores(1, n, slot, use)
                for u in range(NU):
                    transposes(UNIT_GROUPS[u][0], n)
                    if u + 2 < NU:
                        scores(u + 2, n, slot, use)
                    elif not last:
                        scores(u + 2 - NU, n + 1, 1 - slot, use + slot)
                    for g in UNIT_GROUPS[u][1:]:
                        transposes(g, n)
                    if u >= 1:
                        times_v(u - 1, n, slot)
                    elif not first:
                        times_v(NU - 1, n - 1, 1 - slot)
                if last:
                    times_v(NU - 1, n, slot)
            pe.wait_ge(consts_loaded, 32)
            pe.wait_ge(ident16_done, 1)
            heads(pe, head)

        @block.vector
        def _(dve):
            dve.wait_ge(consts_loaded, 32)
            nc.vector.tensor_copy(ident16[:], ident[:]).then_inc(ident16_done, 1)

            def maximum(u, n, slot):
                dve.wait_ge(s_done, NU * n + u + 1)
                nc.vector.tensor_reduce(row_max[slot][:, u:u + 1], s_ps[u % 2][:, 0:UNITS[u][2] * P], AX_X,
                                        ALU.max).then_inc(max_done, 1)

            def low_part(g, n):
                dve.wait_ge(pt_hi_done, NG * n + g + 1)
                w = GROUPS[g][2] * P
                nc.vector.scalar_tensor_tensor(pt_lo[:, PT_SLOT[g], 0:w], t_bank(g)[:, 0:w], P_SCALE, pt_hi[:, PT_SLOT[g], 0:w],
                                               ALU.mult, ALU.subtract).then_inc(pt_lo_done, 1)

            def merge_top(n, slot):
                dve.wait_ge(neg_done, NU * n + NU)
                nm = neg_max[slot][:, N_ONE:NU].rearrange("p (t h) -> p t h", h=2)
                nc.vector.tensor_tensor(neg_top[:], nm[:, :, 0], nm[:, :, 1], ALU.min).then_inc(top_done, 1)

            def invert(n):
                dve.wait_ge(sum_done, 2 * n + 2)
                nc.vector.reciprocal(inv_sum[:], sum_all[:]).then_inc(inv_done, 1)

            def head(n, slot, use, first, last):
                if first:
                    maximum(0, n, slot)
                    maximum(1, n, slot)
                for u in range(NU):
                    low_part(UNIT_GROUPS[u][0], n)
                    if u + 2 < NU:
                        maximum(u + 2, n, slot)
                    elif not last:
                        maximum(u + 2 - NU, n + 1, 1 - slot)
                    for g in UNIT_GROUPS[u][1:]:
                        low_part(g, n)
                    if u == MERGE["top"] and not first:
                        merge_top(n - 1, 1 - slot)
                    if u == MERGE["invert"] and not first:
                        invert(n - 1)
                if last:
                    merge_top(n, slot)
                    invert(n)
            heads(dve, head)

        @block.scalar
        def _(act):
            def exponentials(u, n, slot):
                act.wait_ge(neg_done, NU * n + u + 1)
                if u == 0 and (not isinstance(n, int) or n >= 2):
                    act.wait_ge(merged_done, 2 * n - 2)
                w = UNITS[u][2] * P
                nc.scalar.activation(probs[u % 3][:, 0:w], s_ps[u % 2][:, 0:w], ACT.Exp, bias=neg_max[slot][:, u:u + 1],
                                     scale=SOFTMAX_SCALE, accum_out=row_sum[slot][:, u:u + 1]).then_inc(exp_done, 1)

            def high_part(g, n):
                act.wait_ge(t_done, NG * n + g + 1)
                w = GROUPS[g][2] * P
                nc.scalar.activation(pt_hi[:, PT_SLOT[g], 0:w], t_bank(g)[:, 0:w], ACT.Copy, scale=P_SCALE).then_inc(
                    pt_hi_done, 1)

            def output(u, n, slot):
                act.wait_ge(pv_done, NU * n + u + 1)
                nc.scalar.activation(o_unit[slot][:, u, :], o_ps[:], ACT.Copy, scale=1.0 / P_SCALE).then_inc(
                    o_unit_done, 1)

            def shrink_factors(n):
                act.wait_ge(gap_done, n + 1)
                nc.scalar.activation(shrink[:], gap[:], ACT.Exp).then_inc(shrink_done, 1)

            def head(n, slot, use, first, last):
                if first:
                    exponentials(0, n, slot)
                for u in range(NU):
                    if u >= 2:
                        output(u - 2, n, slot)
                    elif not first:
                        output(NU - 2 + u, n - 1, 1 - slot)
                    high_part(UNIT_GROUPS[u][0], n)
                    if u + 1 < NU:
                        exponentials(u + 1, n, slot)
                    elif not last:
                        exponentials(0, n + 1, 1 - slot)
                    for g in UNIT_GROUPS[u][1:]:
                        high_part(g, n)
                    if u == MERGE["shrink"] and not first:
                        shrink_factors(n - 1)
                if last:
                    output(NU - 2, n, slot)
                    output(NU - 1, n, slot)
                    shrink_factors(n)
            heads(act, head)

        @block.gpsimd
        def _(pool):
            nc.gpsimd.memset(neg_scale[:], -SOFTMAX_SCALE).then_inc(set_done, 1)
            pool.wait_ge(set_done, 1)
            for slot in range(2):
                pool.sem_inc(o_stored[slot], 16)

            def negate(u, n, slot):
                pool.wait_ge(max_done, NU * n + u + 1)
                nc.gpsimd.tensor_tensor(neg_max[slot][:, u:u + 1], row_max[slot][:, u:u + 1], neg_scale[:],
                                        ALU.mult).then_inc(neg_done, 1)

            pairs = lambda x: x[:, N_ONE:NU].rearrange("p (t h) -> p t h", h=2)

            def merge_gap(n, slot):
                pool.wait_ge(top_done, n + 1)
                nc.gpsimd.tensor_tensor(gap[:], neg_top[:].unsqueeze(2).broadcast_to([P, N_TWO, 2]),
                                        pairs(neg_max[slot]), ALU.subtract).then_inc(gap_done, 1)

            def merge_part(n, slot):
                pool.wait_ge(shrink_done, n + 1)
                nc.gpsimd.tensor_tensor(sum_part[:], shrink[:], pairs(row_sum[slot]), ALU.mult).then_inc(part_done, 1)

            def merge_sum(n, slot):
                pool.wait_ge(part_done, n + 1)
                nc.gpsimd.tensor_tensor(sum_all[:, N_ONE:QT], sum_part[:, :, 0], sum_part[:, :, 1],
                                        ALU.add).then_inc(sum_done, 1)
                nc.gpsimd.tensor_copy(sum_all[:, 0:N_ONE], row_sum[slot][:, 0:N_ONE]).then_inc(sum_done, 1)

            def merge_weight(n, slot):
                pool.wait_ge(inv_done, n + 1)
                nc.gpsimd.tensor_tensor(pairs(weight), shrink[:],
                                        inv_sum[:, N_ONE:QT].unsqueeze(2).broadcast_to([P, N_TWO, 2]),
                                        ALU.mult).then_inc(weight_done, 1)
                nc.gpsimd.tensor_copy(weight[:, 0:N_ONE], inv_sum[:, 0:N_ONE]).then_inc(weight_done, 1)

            def merge_scale(n, slot, use, piece):
                at = slice(4 * piece, 4 * piece + 4)
                if piece == 0:
                    pool.wait_ge(weight_done, 2 * n + 2)
                    pool.wait_ge(o_unit_done, NU * n + NU)
                    pool.wait_ge(o_stored[slot], 16 * use + 16)
                out = o_head[slot][:, at, :] if 4 * piece < N_ONE else o_unit[slot][:, at, :]
                nc.gpsimd.tensor_tensor(out, o_unit[slot][:, at, :], weight[:, at].unsqueeze(2).broadcast_to([P, 4, HD]),
                                        ALU.mult).then_inc(scaled_done, 1)

            def merge_add(n, slot, piece):
                if piece == 0:
                    pool.wait_ge(scaled_done, NU // 4 * n + NU // 4)
                both = o_unit[slot][:, N_ONE + 8 * piece:N_ONE + 8 * piece + 8, :].rearrange(
                    "p (t h) f -> p t h f", h=2)
                nc.gpsimd.tensor_tensor(o_head[slot][:, N_ONE + 4 * piece:N_ONE + 4 * piece + 4, :], both[:, :, 0],
                                        both[:, :, 1], ALU.add).then_inc(merged_done, 1)

            def merge_step(u, n, slot, use):
                if u == MERGE["top"] + 1:
                    merge_gap(n, slot)
                if u == MERGE["shrink"] + 1:
                    merge_part(n, slot)
                if u == MERGE["shrink"] + 2:
                    merge_sum(n, slot)
                if u == MERGE["invert"] + 1:
                    merge_weight(n, slot)
                if 0 <= u - MERGE["scale"] < NU // 4:
                    merge_scale(n, slot, use, u - MERGE["scale"])
                if 0 <= u - MERGE["add"] < 2:
                    merge_add(n, slot, u - MERGE["add"])

            def head(n, slot, use, first, last):
                if first:
                    negate(0, n, slot)
                    negate(1, n, slot)
                for u in range(NU):
                    if u + 2 < NU:
                        negate(u + 2, n, slot)
                    elif not last:
                        negate(u + 2 - NU, n + 1, 1 - slot)
                    if not first:
                        merge_step(u, n - 1, 1 - slot, use - 1 + slot)
                if last:
                    for u in range(NU):
                        merge_step(u, n, slot, use)
            heads(pool, head)


def finish_phase(nc, x, o_scratch, wo, b_o, ident_in, ffn_in, ffn_probe, ffn_mix, own_in, rank_in, center, slope, out):
    with ExitStack() as ctx:
        sb = lambda name, shape, dt: ctx.enter_context(nc.sbuf_tensor(name, shape, dt))
        psum = lambda name, shape: ctx.enter_context(nc.psum_tensor(name, shape, F32))
        sem = lambda name: ctx.enter_context(nc.semaphore(name))
        NT = B * QT
        HALF = 512
        halves = [slice(0, HALF), slice(HALF, D)]
        SEL, LOW, DIF = slice(0, 64), slice(64, 128), slice(128, 136)

        ident = sb("ident_c", [P, P], F32)
        w_raw = sb("wo_raw", [P, 2, D], F32)
        w_hi = sb("wo_hi", [P, KT, D], F16)
        w_lo = sb("wo_lo", [P, KT, D], F16)
        bo_row = sb("bo_row", [P, D], F32)
        ffn_w = sb("ffn_w", [P, KT, FF], F32)
        probe = sb("probe", [P, KT, 2 * N_EXP], F32)
        mix_w = sb("mix_w", [MIX, D], F32)
        own = sb("own", [2 * N_EXP, FF], F32)
        ones = sb("ones", [2 * N_EXP, P], F32)
        own_dots = sb("own_dots", [2 * N_EXP, FF], F32)
        offsets = sb("offsets", [P, FF], F32)
        rank = sb("rank", [P, N_EXP], F32)
        center_row = sb("center_row", [P, N_EXP], F32)
        slope_row = sb("slope_row", [P, N_EXP], F32)
        eps = sb("eps_c", [P, 1], F32)
        minus_half = sb("minus_half_c", [P, 1], F32)
        o_in = [sb(f"o_in{i}", [P, D], F32) for i in range(4)]
        x_in = [sb(f"x_in_c{i}", [P, D], F32) for i in range(4)]
        ot_hi = [sb(f"ot_hi{i}", [P, KT, P], F16) for i in range(2)]
        ot_lo = [sb(f"ot_lo{i}", [P, KT, P], F16) for i in range(2)]
        attn = [sb(f"attn{i}", [P, D], F32) for i in range(2)]
        x1 = [sb(f"x1_{i}", [P, D], F32) for i in range(4)]
        x2 = [sb(f"x2_{i}", [P, D], F32) for i in range(4)]
        square = sb("square", [P, D], F32)
        x2_norm2 = [sb(f"x2_norm2_{i}", [P, 1], F32) for i in range(4)]
        x2t = sb("x2t", [P, KT, P], F32)
        mixed = [sb(f"mixed{i}", [P, D], F32) for i in range(2)]
        y = [sb(f"y{i}", [P, D], F32) for i in range(2)]
        result = [sb(f"result{i}", [P, D], F32) for i in range(2)]
        stats = sb("stats_c", [P, 3, 2, 6], F32)
        moments = sb("moments_c", [P, 3, 2], F32)
        var_eps = sb("var_eps_c", [P, 3], F32)
        rstd = sb("rstd_c", [P, 3], F32)
        neg_mean = sb("neg_mean", [P, 3], F32)
        shift = sb("shift", [P, 3], F32)
        dots = sb("dots", [P, 2 * 64], F32)
        dots2 = sb("dots2", [P, 64], F32)
        select = sb("select", [P, 10, N_EXP], F32)
        sel_scale = [sb(f"sel_scale{i}", [P, 1], F32) for i in range(2)]
        sel_rest = [sb(f"sel_rest{i}", [P, 1], F32) for i in range(2)]
        top_rank = sb("top_rank", [P, 1], F32)
        mix = sb("mix", [P, MIX], F32)
        mix_t = sb("mix_t", [MIX, P], F32)

        ot_ps = [psum(f"ot_ps{i}", [P, HALF]) for i in range(2)]
        proj_ps = [psum(f"proj_ps{i}", [P, HALF]) for i in range(2)]
        ffn_ps = [psum(f"ffn_ps{i}", [P, HALF]) for i in range(2)]
        dots_ps = psum("dots_ps", [P, FF])
        mix_ps = psum("mix_ps", [MIX, P])

        consts_loaded = sem("consts_loaded_c")
        set_done = sem("set_done_c")
        w_loaded = [sem(f"wo_loaded{i}") for i in range(2)]
        w_hi_done = sem("wo_hi_done")
        w_lo_done = sem("wo_lo_done")
        own_ps_done = sem("own_ps_done")
        own_done = sem("own_done")
        offsets_ps_done = sem("offsets_ps_done")
        offsets_done = sem("offsets_done")
        tile_loaded = [sem(f"tile_loaded{i}") for i in range(4)]
        ot_ps_done = sem("ot_ps_done")
        ot_hi_done = sem("ot_hi_done")
        ot_lo_done = sem("ot_lo_done")
        proj_done = sem("proj_done")
        attn_done = sem("attn_done")
        stats_done = sem("stats_done_c")
        moments_done = [sem(f"moments_done_c{i}") for i in range(3)]
        var_done = [sem(f"var_done_c{i}") for i in range(3)]
        rstd_done = [sem(f"rstd_done_c{i}") for i in range(3)]
        shift_done = [sem(f"shift_done{i}") for i in range(3)]
        attn_norm_done = sem("attn_norm_done")
        x1_done = sem("x1_done")
        x2_done = sem("x2_done")
        norm2_done = sem("norm2_done")
        x2t_ps_done = sem("x2t_ps_done")
        x2t_done = sem("x2t_done")
        dots_ps_done = sem("dots_ps_done")
        gate_step = sem("gate_step")
        logit_done = sem("logit_done")
        gate_exp_done = sem("gate_exp_done")
        mix_done = sem("mix_done")
        mix_ps_done = sem("mix_ps_done")
        mix_t_done = sem("mix_t_done")
        ffn_done = sem("ffn_done")
        mixed_done = sem("mixed_done")
        y_done = sem("y_done")
        y_norm_done = sem("y_norm_done")
        result_done = sem("result_done")
        stored = [sem(f"stored{i}") for i in range(2)]

        x_view = x.rearrange("(b t p) d -> b t p d", b=B, t=QT)
        out_view = out.rearrange("(b t p) d -> b t p d", b=B, t=QT)
        o_view = o_scratch.rearrange("(b h) p (t f) -> b t p h f", b=B, f=HD)
        wo_view = wo.rearrange("(k p) o -> k p o", p=P)
        CONSTS = 9

        def tiles(eng, step):
            def fixed(m):
                step(m, m // 2, m % 4, lambda d: 0 <= m + d < NT)
            for m in range(4):
                fixed(m)
            with eng.Fori(1, NT // 4 - 1) as i:
                for v in range(4):
                    step(4 * i + v, 2 * i + v // 2, v, lambda d: True)
            for m in range(NT - 4, NT + 4):
                fixed(m)

        block = ctx.enter_context(nc.Block())

        @block.sync
        def _(sp):
            def load(m, t, r):
                sp.dma_start(o_in[r][:].rearrange("p (h f) -> p h f", f=HD), o_view[r % 2, t]).then_inc(
                    tile_loaded[r], 16)
                sp.dma_start(x_in[r][:], x_view[r % 2, t]).then_inc(tile_loaded[r], 16)

            sp.dma_start(ident[:], ident_in).then_inc(consts_loaded, 16)
            load(0, 0, 0)
            for k in range(KT):
                if k >= 2:
                    sp.wait_ge(w_lo_done, k - 1)
                sp.dma_start(w_raw[:, k % 2, :], wo_view[k]).then_inc(w_loaded[k % 2], 16)
            sp.dma_start(bo_row[:], b_o.partition_broadcast(P)).then_inc(consts_loaded, 16)
            sp.dma_start(ffn_w[:], ffn_in.rearrange("(k p) o -> p k o", p=P)).then_inc(consts_loaded, 16)
            sp.dma_start(probe[:], ffn_probe.rearrange("(k p) o -> p k o", p=P)).then_inc(consts_loaded, 16)
            sp.dma_start(mix_w[:], ffn_mix).then_inc(consts_loaded, 16)
            sp.dma_start(own[:], own_in).then_inc(consts_loaded, 16)
            sp.dma_start(rank[:], rank_in).then_inc(consts_loaded, 16)
            sp.dma_start(center_row[:], center.partition_broadcast(P)).then_inc(consts_loaded, 16)
            sp.dma_start(slope_row[:], slope.partition_broadcast(P)).then_inc(consts_loaded, 16)
            load(1, 0, 1)
            load(2, 1, 2)

            def step(m, t, r, has):
                if has(3):
                    if has(-1):
                        sp.wait_ge(ot_ps_done, 2 * m)
                        sp.wait_ge(x1_done, m)
                    load(m + 3, t + 1 + r % 2, (r + 3) % 4)
                if has(-4):
                    sp.wait_ge(result_done, m - 3)
                    sp.dma_start(out_view[r % 2, t - 2], result[r % 2][:]).then_inc(stored[r % 2], 16)

            tiles(sp, step)
            for i in range(2):
                sp.wait_ge(stored[i], 16 * (NT // 2 + 1))

        @block.tensor
        def _(pe):
            def transpose_attention(m, r):
                for h in range(2):
                    pe.wait_ge(tile_loaded[r], 8 * (m - r) + 32)
                    if not isinstance(m, int) or m > 0:
                        pe.wait_ge(ot_lo_done, 2 * m - 1 + h)
                    for k in range(4):
                        at = slice((4 * h + k) * P, (4 * h + k + 1) * P)
                        tr = nc.tensor.transpose(ot_ps[h][:, k * P:(k + 1) * P], o_in[r][:, at], ident[:])
                    tr.then_inc(ot_ps_done, 1)

            def project(m, r, h):
                if h == 0:
                    pe.wait_ge(ot_lo_done, 2 * m + 2)
                if not isinstance(m, int) or m > 0:
                    pe.wait_ge(attn_done, 2 * m - 1 + h)
                for k in range(KT):
                    nc.tensor.matmul(proj_ps[h][:], ot_lo[r % 2][:, k, :], w_hi[:, k, halves[h]], start=(k == 0),
                                     stop=False)
                    nc.tensor.matmul(proj_ps[h][:], ot_hi[r % 2][:, k, :], w_lo[:, k, halves[h]], start=False,
                                     stop=False)
                    mm = nc.tensor.matmul(proj_ps[h][:], ot_hi[r % 2][:, k, :], w_hi[:, k, halves[h]], start=False,
                                          stop=(k == KT - 1))
                mm.then_inc(proj_done, 1)

            def transpose_x2(m, r):
                pe.wait_ge(x2_done, m + 1)
                for h in range(2):
                    if h == 0 and (not isinstance(m, int) or m > 1):
                        pe.wait_ge(mixed_done, 2 * m - 2)
                    for k in range(4):
                        at = slice((4 * h + k) * P, (4 * h + k + 1) * P)
                        tr = nc.tensor.transpose(ffn_ps[h][:, k * P:(k + 1) * P], x2[r][:, at], ident[:])
                    tr.then_inc(x2t_ps_done, 1)

            def ffn_dots(m):
                pe.wait_ge(x2t_done, 2 * m + 2)
                if not isinstance(m, int) or m > 0:
                    pe.wait_ge(mix_done, m)
                for k in range(KT):
                    mm = nc.tensor.matmul(dots_ps[:], x2t[:, k, :], ffn_w[:, k, :], start=(k == 0),
                                          stop=(k == KT - 1))
                mm.then_inc(dots_ps_done, 1)

            def mix_transpose(m):
                pe.wait_ge(mix_done, m + 1)
                nc.tensor.transpose(mix_ps[:], mix[:], ident[:]).then_inc(mix_ps_done, 1)

            def ffn_mix_out(m):
                pe.wait_ge(mix_t_done, m + 1)
                for h in range(2):
                    nc.tensor.matmul(ffn_ps[h][:], mix_t[:], mix_w[:, halves[h]], start=True, stop=True).then_inc(
                        ffn_done, 1)

            def step(m, t, r, has):
                if has(-2):
                    transpose_x2(m - 2, (r + 2) % 4)
                if has(-3):
                    mix_transpose(m - 3)
                if has(1):
                    transpose_attention(m + 1, (r + 1) % 4)
                if has(0):
                    project(m, r, 0)
                if has(-2):
                    ffn_dots(m - 2)
                if has(-3):
                    ffn_mix_out(m - 3)
                if has(0):
                    project(m, r, 1)

            pe.wait_ge(consts_loaded, 16 * CONSTS)
            for k in range(KT):
                mm = nc.tensor.matmul(dots_ps[0:2 * N_EXP, :], probe[:, k, :], ffn_w[:, k, :], start=(k == 0),
                                      stop=(k == KT - 1))
            mm.then_inc(own_ps_done, 1)
            pe.wait_ge(own_done, 1)
            nc.tensor.matmul(dots_ps[:], ones[:], own_dots[:], start=True, stop=True).then_inc(offsets_ps_done, 1)
            transpose_attention(0, 0)
            pe.wait_ge(w_lo_done, KT)
            pe.wait_ge(offsets_done, 1)
            tiles(pe, step)

        @block.vector
        def _(dve):
            nc.vector.memset(ones[:], 1.0)

            def attention_low(m, r):
                for h in range(2):
                    dve.wait_ge(ot_hi_done, 2 * m + 1 + h)
                    nc.vector.tensor_tensor(ot_lo[r % 2][:, 4 * h:4 * h + 4, :].rearrange("p k n -> p (k n)"), ot_ps[h][:],
                                            ot_hi[r % 2][:, 4 * h:4 * h + 4, :].rearrange("p k n -> p (k n)"),
                                            ALU.subtract).then_inc(ot_lo_done, 1)

            def norm_stats(which, m, tile):
                for h in range(2):
                    bn = nc.vector.bn_stats(stats[:, which, h, :], tile[:, halves[h]])
                bn.then_inc(stats_done, 1)
                dve.wait_ge(stats_done, 1)
                dve.sem_clear(stats_done)
                nc.vector.bn_aggr(moments[:, which, :], stats[:, which].rearrange("p h e -> p (h e)")).then_inc(
                    moments_done[which], 1)

            def attention_out(m, r, h):
                dve.wait_ge(proj_done, 2 * m + 1 + h)
                nc.vector.scalar_tensor_tensor(attn[r % 2][:, halves[h]], proj_ps[h][:], OUT_UNSCALE,
                                               bo_row[:, halves[h]], ALU.mult, ALU.add).then_inc(attn_done, 1)

            def attention_stats(m, r):
                dve.wait_ge(attn_done, 2 * m + 2)
                norm_stats(0, m, attn[r % 2])

            def x1_stats(m, r):
                dve.wait_ge(x1_done, m + 1)
                norm_stats(1, m, x1[r])

            GATE_STEPS = 16

            def gates(m, r):
                count = [0]

                def step(op):
                    count[0] += 1
                    op.then_inc(gate_step, 1)

                def settled():
                    dve.wait_ge(gate_step, GATE_STEPS * m + count[0])
                num, dist, inv, score, off, logit, gate1, gate, first, chosen = (select[:, i, :] for i in range(10))
                dve.wait_ge(dots_ps_done, m + 1)
                dve.wait_ge(norm2_done, m + 1)
                step(nc.vector.tensor_tensor(dots[:], dots_ps[:, 0:128], offsets[:, 0:128], ALU.subtract))
                step(nc.vector.scalar_tensor_tensor(dist, dots_ps[:, DIF], -2.0, offsets[:, DIF], ALU.mult, ALU.add))
                settled()
                step(nc.vector.tensor_tensor(dots2[:], dots[:, SEL], dots[:, SEL], ALU.mult))
                step(nc.vector.tensor_scalar(dist, dist, x2_norm2[r][:], None, ALU.add))
                settled()
                step(nc.vector.tensor_reduce(num, dots2[:].rearrange("p (n s) -> p n s", n=N_EXP), AX_X, ALU.add))
                step(nc.vector.reciprocal(inv, dist))
                settled()
                step(nc.vector.tensor_tensor(score, num, inv, ALU.mult))
                settled()
                step(nc.vector.tensor_tensor(off, score, center_row[:], ALU.subtract))
                settled()
                nc.vector.tensor_tensor(logit, off, slope_row[:], ALU.mult).then_inc(logit_done, 1)
                dve.wait_ge(gate_exp_done, m + 1)
                step(nc.vector.tensor_scalar(gate1, gate1, 1.0, None, ALU.add))
                settled()
                step(nc.vector.reciprocal(gate, gate1))
                settled()
                if not isinstance(m, int) or m >= 2:
                    dve.wait_ge(y_done, m - 1)
                    dve.wait_ge(mixed_done, 2 * m - 2)
                step(nc.vector.tensor_reduce(sel_scale[r % 2][:], gate, AX_X, ALU.max))
                settled()
                step(nc.vector.tensor_scalar(sel_rest[r % 2][:], sel_scale[r % 2][:], -1.0, 1.0, ALU.mult, ALU.add))
                step(nc.vector.scalar_tensor_tensor(first, gate, sel_scale[r % 2][:], rank[:], ALU.is_equal, ALU.mult))
                settled()
                step(nc.vector.tensor_reduce(top_rank[:], first, AX_X, ALU.max))
                settled()
                if not isinstance(m, int) or m >= 1:
                    dve.wait_ge(mix_ps_done, m)
                step(nc.vector.tensor_scalar(mix[:, 64:MIX], rank[:], top_rank[:], None, ALU.is_equal))
                step(nc.vector.tensor_scalar(chosen, rank[:], top_rank[:], None, ALU.is_equal))
                settled()
                assert count[0] == GATE_STEPS, count
                nc.vector.tensor_tensor(mix[:, 0:64].rearrange("p (n h) -> p n h", n=N_EXP),
                                        dots[:, LOW].rearrange("p (n h) -> p n h", n=N_EXP),
                                        chosen.unsqueeze(2).broadcast_to([P, N_EXP, N_LOW]), ALU.mult).then_inc(
                    mix_done, 1)

            def ffn_out(m, r):
                dve.wait_ge(mixed_done, 2 * m + 2)
                nc.vector.scalar_tensor_tensor(y[r % 2][:], x2[r][:], sel_rest[r % 2][:], mixed[r % 2][:], ALU.mult,
                                               ALU.add).then_inc(y_done, 1)
                dve.wait_ge(y_done, m + 1)
                norm_stats(2, m, y[r % 2])

            def step(m, t, r, has):
                if has(-1):
                    attention_out(m - 1, (r + 3) % 4, 1)
                    attention_stats(m - 1, (r + 3) % 4)
                if has(-4):
                    ffn_out(m - 4, r)
                if has(1):
                    attention_low(m + 1, (r + 1) % 4)
                if has(-1):
                    x1_stats(m - 1, (r + 3) % 4)
                if has(0):
                    attention_out(m, r, 0)
                if has(-2):
                    gates(m - 2, (r + 2) % 4)

            for k in range(KT):
                dve.wait_ge(w_hi_done, k + 1)
                nc.vector.scalar_tensor_tensor(w_lo[:, k, :], w_raw[:, k % 2, :], W_SCALE, w_hi[:, k, :], ALU.mult,
                                               ALU.subtract).then_inc(w_lo_done, 1)
            dve.wait_ge(consts_loaded, 16 * CONSTS)
            dve.wait_ge(own_ps_done, 1)
            nc.vector.tensor_tensor(own_dots[:], dots_ps[0:2 * N_EXP, :], own[:], ALU.mult).then_inc(own_done, 1)
            dve.wait_ge(offsets_ps_done, 1)
            nc.vector.tensor_copy(offsets[:], dots_ps[:]).then_inc(offsets_done, 1)
            dve.wait_ge(offsets_done, 1)
            attention_low(0, 0)
            tiles(dve, step)

        @block.scalar
        def _(act):
            def attention_high(m, r):
                for h in range(2):
                    act.wait_ge(ot_ps_done, 2 * m + 1 + h)
                    if h == 0 and (not isinstance(m, int) or m >= 2):
                        act.wait_ge(proj_done, 2 * m - 2)
                    nc.scalar.activation(ot_hi[r % 2][:, 4 * h:4 * h + 4, :].rearrange("p k n -> p (k n)"), ot_ps[h][:],
                                         ACT.Copy).then_inc(ot_hi_done, 1)

            def attention_norm(m, r):
                act.wait_ge(shift_done[0], m + 1)
                nc.scalar.activation(attn[r % 2][:], attn[r % 2][:], ACT.Identity, bias=shift[:, 0:1],
                                     scale=rstd[:, 0:1]).then_inc(attn_norm_done, 1)

            def x2_norm(m, r):
                act.wait_ge(shift_done[1], m + 1)
                nc.scalar.activation(x2[r][:], x1[r][:], ACT.Identity, bias=shift[:, 1:2],
                                     scale=rstd[:, 1:2]).then_inc(x2_done, 1)

            def x2_square(m, r):
                act.wait_ge(x2_done, m + 1)
                nc.scalar.activation(square[:], x2[r][:], ACT.Square, accum_out=x2_norm2[r][:]).then_inc(norm2_done, 1)

            def x2_transposed(m):
                for h in range(2):
                    act.wait_ge(x2t_ps_done, 2 * m + 1 + h)
                    if h == 0 and (not isinstance(m, int) or m >= 1):
                        act.wait_ge(dots_ps_done, m)
                    nc.scalar.activation(x2t[:, 4 * h:4 * h + 4, :].rearrange("p k n -> p (k n)"), ffn_ps[h][:],
                                         ACT.Copy).then_inc(x2t_done, 1)

            def gate_exp(m):
                act.wait_ge(logit_done, m + 1)
                nc.scalar.activation(select[:, 6, :], select[:, 5, :], ACT.Exp, scale=-1.0).then_inc(gate_exp_done, 1)

            def mix_transposed(m):
                act.wait_ge(mix_ps_done, m + 1)
                if not isinstance(m, int) or m >= 1:
                    act.wait_ge(ffn_done, 2 * m)
                nc.scalar.activation(mix_t[:], mix_ps[:], ACT.Copy).then_inc(mix_t_done, 1)

            def ffn_gated(m, r):
                for h in range(2):
                    act.wait_ge(ffn_done, 2 * m + 1 + h)
                    if h == 0 and (not isinstance(m, int) or m >= 2):
                        act.wait_ge(y_done, m - 1)
                    nc.scalar.activation(mixed[r % 2][:, halves[h]], ffn_ps[h][:], ACT.Copy,
                                         scale=sel_scale[r % 2][:]).then_inc(mixed_done, 1)

            def ffn_norm(m, r):
                act.wait_ge(shift_done[2], m + 1)
                nc.scalar.activation(y[r % 2][:], y[r % 2][:], ACT.Identity, bias=shift[:, 2:3],
                                     scale=rstd[:, 2:3]).then_inc(y_norm_done, 1)

            def step(m, t, r, has):
                if has(-2):
                    x2_transposed(m - 2)
                if has(-3):
                    mix_transposed(m - 3)
                if has(1):
                    attention_high(m + 1, (r + 1) % 4)
                if has(-1):
                    attention_norm(m - 1, (r + 3) % 4)
                if has(-4):
                    ffn_norm(m - 4, r)
                if has(-1):
                    x2_norm(m - 1, (r + 3) % 4)
                if has(-2):
                    gate_exp(m - 2)
                if has(-3):
                    ffn_gated(m - 3, (r + 1) % 4)
                if has(-1):
                    x2_square(m - 1, (r + 3) % 4)

            for k in range(KT):
                act.wait_ge(w_loaded[k % 2], 16 * (k // 2 + 1))
                nc.scalar.activation(w_hi[:, k, :], w_raw[:, k % 2, :], ACT.Copy, scale=W_SCALE).then_inc(w_hi_done, 1)
            attention_high(0, 0)
            tiles(act, step)

        @block.gpsimd
        def _(pool):
            nc.gpsimd.memset(eps[:], EPS).then_inc(set_done, 1)
            nc.gpsimd.memset(minus_half[:], -0.5).then_inc(set_done, 1)
            pool.wait_ge(set_done, 2)
            for i in range(2):
                pool.sem_inc(stored[i], 16)

            def norm_scale(which, m):
                pool.wait_ge(moments_done[which], m + 1)
                w = slice(which, which + 1)
                nc.gpsimd.tensor_tensor(var_eps[:, w], moments[:, which, 1:2], eps[:], ALU.add).then_inc(
                    var_done[which], 1)
                nc.gpsimd.tensor_scalar(neg_mean[:, w], moments[:, which, 0:1], -1.0, None, ALU.mult).then_inc(
                    var_done[which], 1)
                pool.wait_ge(var_done[which], 2 * m + 2)
                nc.gpsimd.tensor_tensor(rstd[:, w], var_eps[:, w], minus_half[:], ALU.pow).then_inc(
                    rstd_done[which], 1)
                pool.wait_ge(rstd_done[which], m + 1)
                nc.gpsimd.tensor_tensor(shift[:, w], neg_mean[:, w], rstd[:, w], ALU.mult).then_inc(
                    shift_done[which], 1)

            def residual(m, r):
                pool.wait_ge(attn_norm_done, m + 1)
                nc.gpsimd.tensor_tensor(x1[r][:], x_in[r][:], attn[r % 2][:], ALU.add).then_inc(x1_done, 1)

            def final(m, r):
                pool.wait_ge(y_norm_done, m + 1)
                pool.wait_ge(stored[r % 2], stores(m, r))
                nc.gpsimd.tensor_tensor(result[r % 2][:], x1[r][:], y[r % 2][:], ALU.add).then_inc(result_done, 1)

            def stores(m, r):
                return 16 * (m // 2 + 1) if isinstance(m, int) else 8 * (m - r % 2) + 16

            def step(m, t, r, has):
                if has(-1):
                    norm_scale(0, m - 1)
                    residual(m - 1, (r + 3) % 4)
                if has(-4):
                    norm_scale(2, m - 4)
                if has(-1):
                    norm_scale(1, m - 1)
                if has(-4):
                    final(m - 4, r)
            tiles(pool, step)


def attention_ffn(nc, x, w_qkv, b_cols, b_v, w_o, b_o, ffn_in, ffn_probe, ffn_mix, center, slope, ident, mask, own, rank,
                  out):
    q_scratch = nc.dram_tensor("q_scratch", (NC, BH, HD, 2, TOK), F16, kind="Internal").ap()
    k_scratch = nc.dram_tensor("k_scratch", (NC, BH, HD, 2, TOK), F16, kind="Internal").ap()
    v_scratch = nc.dram_tensor("v_scratch", (BH, P, QT, 2 * HD), F16, kind="Internal").ap()
    o_scratch = nc.dram_tensor("o_scratch", (BH, P, QT * HD), F32, kind="Internal").ap()
    project_phase(nc, x, w_qkv, b_cols, b_v, ident, q_scratch, k_scratch, v_scratch)
    attend_phase(nc, q_scratch, k_scratch, v_scratch, o_scratch, ident, mask)
    finish_phase(nc, x, o_scratch, w_o, b_o, ident, ffn_in, ffn_probe, ffn_mix, own, rank, center, slope, out)


def kernel(L0_attn_x, L0_attn_wq, L0_attn_bq, L0_attn_wk, L0_attn_bk, L0_attn_wv, L0_attn_bv, L0_attn_wo, L0_attn_bo,
           L0_ffn_select_weight, L0_ffn_select_mean_diff, L0_ffn_imp_center, L0_ffn_imp_slope, L0_ffn_lora_update,
           L0_ffn_lora_degen, L0_ffn_bias_w, L0_ffn_debias_w):
    import ml_dtypes
    import numpy as np
    import concourse.bacc as bacc
    from concourse.bass_utils import run_bass_kernel_spmd

    a = np.asarray
    by_column = lambda w: a(w).transpose(1, 0, 2).reshape(D, -1)
    expert = np.concatenate([np.repeat(np.arange(N_EXP), N_SEL), N_EXP + np.repeat(np.arange(N_EXP), N_LOW),
                             np.arange(N_EXP)])
    arrays = {
        "x": a(L0_attn_x).reshape(B * S, D),
        "w_qkv": np.stack([a(w).T for w in (L0_attn_wq, L0_attn_wk, L0_attn_wv)]),
        "b_cols": np.concatenate([a(L0_attn_bq).reshape(KT, P), a(L0_attn_bk).reshape(KT, P)]).T,
        "b_v": a(L0_attn_bv),
        "w_o": a(L0_attn_wo).T,
        "b_o": a(L0_attn_bo),
        "ffn_in": np.concatenate([by_column(L0_ffn_select_weight), by_column(L0_ffn_lora_update),
                                  a(L0_ffn_select_mean_diff).T], axis=1),
        "ffn_probe": np.concatenate([a(L0_ffn_select_mean_diff).T, a(L0_ffn_debias_w).T], axis=1),
        "ffn_mix": np.concatenate([a(L0_ffn_lora_degen).transpose(0, 2, 1).reshape(-1, D), a(L0_ffn_bias_w)]),
        "center": a(L0_ffn_imp_center),
        "slope": a(L0_ffn_imp_slope),
        "ident": np.eye(P, dtype=np.float32),
        "mask": np.where(np.arange(P)[None, :] > np.arange(P)[:, None], -1e30, 0.0).astype(ml_dtypes.bfloat16),
        "own": (np.arange(2 * N_EXP)[:, None] == expert[None, :]).astype(np.float32),
        "rank": np.broadcast_to(np.arange(N_EXP, 0, -1, dtype=np.float32), (P, N_EXP)),
    }
    nc = bacc.Bacc("TRN2", target_bir_lowering=False, num_devices=1)
    given, aps = {}, []
    for name, array in arrays.items():
        array = np.ascontiguousarray(array)
        given[f"in_{name}"] = array
        aps.append(nc.dram_tensor(f"in_{name}", array.shape, mybir.dt.from_np(array.dtype), kind="ExternalInput").ap())
    aps.append(nc.dram_tensor("out", (B * S, D), F32, kind="ExternalOutput").ap())
    attention_ffn(nc, *aps)
    result = run_bass_kernel_spmd(nc, [given], core_ids=[0])
    return result.results[0]["out"].reshape(B, S, D)
```

```python
import math
from contextlib import ExitStack

import concourse.bass as bass
from concourse import mybir

ALU = mybir.AluOpType
ACT = mybir.ActivationFunctionType
F32 = mybir.dt.float32
F16 = mybir.dt.float16
BF16 = mybir.dt.bfloat16
AX_X = mybir.AxisListType.X

P = 128
B, S, D, H = 2, 2048, 1024, 16
HD = D // H
BH = B * H
KT = D // P
EPS = 1e-5
TOK = 512
SUB = TOK // P
NC = S // TOK
QT = S // P
N_EXP, N_SEL, N_LOW = 8, 8, 8
FF = N_EXP * N_SEL + N_EXP * N_LOW + N_EXP
MIX = N_EXP * N_LOW + N_EXP

X_SCALE, W_SCALE, QKV_SCALE, P_SCALE = 2.0 ** 4, 2.0 ** 8, 2.0 ** 3, 2.0 ** 8
LOG_P_SCALE = math.log(P_SCALE)
MAX_SCALE = 2.0 ** 5
PROJ_UNSCALE = QKV_SCALE / (X_SCALE * W_SCALE)
SOFTMAX_SCALE = HD ** -0.5 / QKV_SCALE ** 2
OUT_UNSCALE = 1.0 / (QKV_SCALE * W_SCALE)


def project_phase(nc, x, w_qkv, b_cols, b_v, ident_in, q_scratch, k_scratch, v_scratch):
    with ExitStack() as ctx:
        sb = lambda name, shape, dt: ctx.enter_context(nc.sbuf_tensor(name, shape, dt))
        psum = lambda name, shape: ctx.enter_context(nc.psum_tensor(name, shape, F32))
        sem = lambda name: ctx.enter_context(nc.semaphore(name))
        NT = B * NC
        N_QK = 2 * D // P
        N_V = SUB * D // 512
        WRING = 3

        ident = sb("ident_a", [P, P], F32)
        bias_cols = sb("bias_cols", [P, N_QK], F32)
        bias_scaled = sb("bias_scaled", [P, N_QK], F32)
        bv_row = sb("bv_row", [P, D], F32)
        w_raw = sb("w_raw", [P, WRING, D], F32)
        w_hi = sb("w_hi", [P, 3, KT, D], F16)
        w_lo = sb("w_lo", [P, 3, KT, D], F16)
        x_in = sb("x_in", [P, SUB, D], F32)
        stats = sb("stats_a", [P, SUB, 2, 6], F32)
        moments = sb("moments_a", [P, SUB, 2], F32)
        var_eps = sb("var_eps_a", [P, SUB], F32)
        rstd = sb("rstd_a", [P, SUB], F32)
        eps = sb("eps_a", [P, SUB], F32)
        minus_half = sb("minus_half_a", [P, SUB], F32)
        x_norm = sb("x_norm", [P, SUB, D], F32)
        xt_hi = sb("xt_hi", [P, 2, KT, TOK], F16)
        xt_lo = sb("xt_lo", [P, 2, KT, TOK], F16)
        qk_full = sb("qk_full", [P, 4, TOK], F32)
        qk_split = sb("qk_split", [P, 4, 2, TOK], F16)
        v_full = sb("v_full", [P, 2, 512], F32)
        v_split = sb("v_split", [P, 2, H, 2, HD], F16)

        tr_ps = [psum(f"tr_ps{i}", [P, TOK]) for i in range(2)]
        qk_ps = [psum(f"qk_ps{i}", [P, TOK]) for i in range(4)]
        v_ps = [psum(f"v_ps{i}", [P, 512]) for i in range(2)]

        consts_loaded = sem("consts_loaded_a")
        set_done = sem("set_done_a")
        consts_scaled = sem("consts_scaled_a")
        w_loaded = [sem(f"w_loaded{i}") for i in range(WRING)]
        w_hi_done = sem("w_hi_done")
        w_lo_done = sem("w_lo_done")
        x_loaded = sem("x_loaded_a")
        stats_done = sem("stats_done_a")
        moments_done = sem("moments_done_a")
        var_done = sem("var_done_a")
        rstd_done = sem("rstd_done_a")
        x_norm_done = sem("x_norm_done")
        tr_done = sem("tr_done")
        xt_hi_done = sem("xt_hi_done")
        xt_lo_done = sem("xt_lo_done")
        qk_ps_done = sem("qk_ps_done")
        qk_full_done = sem("qk_full_done")
        qk_hi_done = sem("qk_hi_done")
        qk_lo_done = sem("qk_lo_done")
        qk_stored = [sem(f"qk_stored{i}") for i in range(4)]
        v_ps_done = sem("v_ps_done")
        v_full_done = sem("v_full_done")
        v_hi_done = sem("v_hi_done")
        v_lo_done = sem("v_lo_done")
        v_stored = [sem(f"v_stored{i}") for i in range(2)]

        x_view = x.rearrange("(b c s p) d -> b c p s d", b=B, c=NC, s=SUB)
        w_view = w_qkv.rearrange("m (k p) o -> m k p o", p=P)
        q_view = q_scratch.rearrange("c (b g h) f l n -> c b g (h f) l n", b=B, h=2)
        k_view = k_scratch.rearrange("c (b g h) f l n -> c b g (h f) l n", b=B, h=2)
        v_view = v_scratch.rearrange("(b h) p (c s) e -> b c s p h e", b=B, s=SUB)

        def tiles(eng, step):
            step(0, 0, 0, True, False)
            with eng.Fori(0, NC - 1) as i:
                step(2 * i + 1, i, 1, False, False)
                step(2 * i + 2, i + 1, 0, False, False)
            step(NT - 1, NC - 1, 1, False, True)

        block = ctx.enter_context(nc.Block())

        @block.sync
        def _(sp):
            sp.dma_start(x_in[:], x_view[0, 0]).then_inc(x_loaded, 16)
            sp.dma_start(ident[:], ident_in).then_inc(consts_loaded, 16)
            sp.dma_start(bias_cols[:], b_cols).then_inc(consts_loaded, 16)
            sp.dma_start(bv_row[:], b_v.partition_broadcast(P)).then_inc(consts_loaded, 16)

            def load_weight(n):
                if n >= WRING:
                    sp.wait_ge(w_lo_done, n - WRING + 1)
                sp.dma_start(w_raw[:, n % WRING, :], w_view[n // KT, n % KT]).then_inc(w_loaded[n % WRING], 16)

            def step(n, c, b, first, last):
                if first:
                    for k in range(KT):
                        load_weight(k)
                if not last:
                    sp.wait_ge(x_norm_done, SUB * n + SUB)
                    sp.dma_start(x_in[:], x_view[1, c] if b == 0 else x_view[0, c + 1]).then_inc(x_loaded, 16)
                if first:
                    for k in range(WRING):
                        load_weight(KT + k)
                for j in range(N_QK):
                    if first and KT + j + WRING < 3 * KT:
                        load_weight(KT + j + WRING)
                    sp.wait_ge(qk_lo_done, N_QK * n + j + 1)
                    view = q_view if j < KT else k_view
                    sp.dma_start(view[c, b, j % KT], qk_split[:, j % 4]).then_inc(qk_stored[j % 4], 16)
                for s in range(SUB):
                    sp.wait_ge(v_lo_done, N_V * n + 2 * s + 2)
                    sp.dma_start(v_view[b, c, s], v_split[:, s % 2].rearrange("p h l f -> p h (l f)")).then_inc(
                        v_stored[s % 2], 16)
            tiles(sp, step)
            for i in range(4):
                sp.wait_ge(qk_stored[i], 16 * (NT * N_QK // 4 + 1))
            for i in range(2):
                sp.wait_ge(v_stored[i], 16 * (NT * SUB // 2 + 1))

        @block.gpsimd
        def _(pool):
            nc.gpsimd.memset(eps[:], EPS).then_inc(set_done, 1)
            nc.gpsimd.memset(minus_half[:], -0.5).then_inc(set_done, 1)
            pool.wait_ge(set_done, 2)
            for i in range(4):
                pool.sem_inc(qk_stored[i], 16)
            for i in range(2):
                pool.sem_inc(v_stored[i], 16)

            def norm_scale(n):
                pool.wait_ge(moments_done, n + 1)
                nc.gpsimd.tensor_tensor(var_eps[:], moments[:, :, 1], eps[:], ALU.add).then_inc(var_done, 1)
                pool.wait_ge(var_done, n + 1)
                nc.gpsimd.tensor_tensor(rstd[:], var_eps[:], minus_half[:], ALU.pow).then_inc(rstd_done, 1)

            def step(n, c, b, first, last):
                if first:
                    norm_scale(0)
                if not last:
                    norm_scale(n + 1)
            tiles(pool, step)

        @block.vector
        def _(dve):
            dve.wait_ge(consts_loaded, 48)
            nc.vector.tensor_scalar(bias_scaled[:], bias_cols[:], QKV_SCALE, None, ALU.mult).then_inc(consts_scaled, 1)
            nc.vector.tensor_scalar(bv_row[:], bv_row[:], QKV_SCALE, None, ALU.mult).then_inc(consts_scaled, 1)

            def norm_stats(n):
                dve.wait_ge(x_loaded, 16 * n + 16)
                for s in range(SUB):
                    for h in range(2):
                        last = nc.vector.bn_stats(stats[:, s, h, :], x_in[:, s, h * 512:(h + 1) * 512])
                last.then_inc(stats_done, 1)
                dve.wait_ge(stats_done, 1)
                dve.sem_clear(stats_done)
                for s in range(SUB):
                    last = nc.vector.bn_aggr(moments[:, s, :], stats[:, s].rearrange("p h e -> p (h e)"))
                last.then_inc(moments_done, 1)

            def norm_apply(n):
                dve.wait_ge(rstd_done, n + 1)
                if not isinstance(n, int) or n > 0:
                    dve.wait_ge(tr_done, KT * n)
                for s in range(SUB):
                    nc.vector.tensor_scalar(x_norm[:, s, :], x_in[:, s, :], moments[:, s, 0:1], rstd[:, s:s + 1],
                                            ALU.subtract, ALU.mult).then_inc(x_norm_done, 1)

            def xt_low(n, b, k):
                dve.wait_ge(xt_hi_done, KT * n + k + 1)
                nc.vector.scalar_tensor_tensor(xt_lo[:, b, k, :], tr_ps[k % 2][:], X_SCALE, xt_hi[:, b, k, :],
                                               ALU.mult, ALU.subtract).then_inc(xt_lo_done, 1)

            def split_weight(m, k):
                n = m * KT + k
                dve.wait_ge(w_hi_done, n + 1)
                nc.vector.scalar_tensor_tensor(w_lo[:, m, k, :], w_raw[:, n % WRING, :], W_SCALE, w_hi[:, m, k, :],
                                               ALU.mult, ALU.subtract).then_inc(w_lo_done, 1)

            def step(n, c, b, first, last):
                if first:
                    norm_stats(0)
                    norm_apply(0)
                    for k in range(KT):
                        xt_low(0, 0, k)
                    for k in range(KT):
                        split_weight(0, k)
                for j in range(N_QK):
                    if first:
                        split_weight(1 + j // KT, j % KT)
                    dve.wait_ge(qk_hi_done, N_QK * n + j + 1)
                    nc.vector.tensor_tensor(qk_split[:, j % 4, 1, :], qk_full[:, j % 4, :], qk_split[:, j % 4, 0, :],
                                            ALU.subtract).then_inc(qk_lo_done, 1)
                    if not last:
                        if j == 1:
                            norm_stats(n + 1)
                        if j == 2:
                            norm_apply(n + 1)
                        if j >= KT:
                            xt_low(n + 1, 1 - b, j - KT)
                def v_low(j):
                    dve.wait_ge(v_hi_done, N_V * n + j + 1)
                    s, half = j // 2, j % 2
                    heads = slice(half * H // 2, (half + 1) * H // 2)
                    nc.vector.tensor_tensor(v_split[:, s % 2, heads, 1, :],
                                            v_full[:, j % 2, :].rearrange("p (h f) -> p h f", f=HD),
                                            v_split[:, s % 2, heads, 0, :], ALU.subtract).then_inc(v_lo_done, 1)
                for j in range(N_V):
                    half = j % 2
                    dve.wait_ge(v_ps_done, N_V * n + j + 1)
                    if not first or j >= 2:
                        dve.wait_ge(v_lo_done, N_V * n + j - 1)
                    nc.vector.scalar_tensor_tensor(v_full[:, j % 2, :], v_ps[j % 2][:], PROJ_UNSCALE,
                                                   bv_row[:, half * 512:(half + 1) * 512],
                                                   ALU.mult, ALU.add).then_inc(v_full_done, 1)
                    if j >= 1:
                        v_low(j - 1)
                v_low(N_V - 1)
            dve.wait_ge(consts_scaled, 2)
            tiles(dve, step)

        @block.scalar
        def _(act):
            act.wait_ge(consts_scaled, 2)

            def xt_high(n, b, k):
                act.wait_ge(tr_done, KT * n + k + 1)
                nc.scalar.activation(xt_hi[:, b, k, :], tr_ps[k % 2][:], ACT.Copy, scale=X_SCALE).then_inc(
                    xt_hi_done, 1)

            def split_weight(m, k):
                n = m * KT + k
                act.wait_ge(w_loaded[n % WRING], 16 * (n // WRING + 1))
                nc.scalar.activation(w_hi[:, m, k, :], w_raw[:, n % WRING, :], ACT.Copy, scale=W_SCALE).then_inc(
                    w_hi_done, 1)

            def step(n, c, b, first, last):
                if first:
                    for k in range(KT):
                        xt_high(0, 0, k)
                    for k in range(KT):
                        split_weight(0, k)
                for j in range(N_QK):
                    if first:
                        split_weight(1 + j // KT, j % KT)
                    act.wait_ge(qk_ps_done, N_QK * n + j + 1)
                    if not first or j >= 4:
                        act.wait_ge(qk_lo_done, N_QK * n + j - 3)
                    act.wait_ge(qk_stored[j % 4], 16 * (N_QK // 4 * n + j // 4 + 1))
                    nc.scalar.activation(qk_full[:, j % 4, :], qk_ps[j % 4][:], ACT.Identity,
                                         bias=bias_scaled[:, j:j + 1], scale=PROJ_UNSCALE).then_inc(qk_full_done, 1)
                    nc.scalar.activation(qk_split[:, j % 4, 0, :], qk_ps[j % 4][:], ACT.Identity,
                                         bias=bias_scaled[:, j:j + 1], scale=PROJ_UNSCALE).then_inc(qk_hi_done, 1)
                    if not last and j >= KT:
                        xt_high(n + 1, 1 - b, j - KT)
                for j in range(N_V):
                    s, half = j // 2, j % 2
                    heads = slice(half * H // 2, (half + 1) * H // 2)
                    act.wait_ge(v_full_done, N_V * n + j + 1)
                    if half == 0:
                        act.wait_ge(v_stored[s % 2], 16 * (SUB // 2 * n + s // 2 + 1))
                    nc.scalar.activation(v_split[:, s % 2, heads, 0, :],
                                         v_full[:, j % 2, :].rearrange("p (h f) -> p h f", f=HD),
                                         ACT.Copy).then_inc(v_hi_done, 1)
            tiles(act, step)

        @block.tensor
        def _(pe):
            def transposes(n, k):
                if not isinstance(n, int) or n > 0 or k >= 2:
                    pe.wait_ge(xt_lo_done, KT * n + k - 1)
                for s in range(SUB):
                    last = nc.tensor.transpose(tr_ps[k % 2][:, s * P:(s + 1) * P], x_norm[:, s, k * P:(k + 1) * P],
                                               ident[:])
                last.then_inc(tr_done, 1)

            def step(n, c, b, first, last):
                if first:
                    pe.wait_ge(consts_loaded, 48)
                    pe.wait_ge(x_norm_done, SUB)
                    for k in range(KT):
                        transposes(0, k)
                pe.wait_ge(xt_lo_done, KT * n + KT)
                for j in range(N_QK):
                    m, cols = j // KT, slice((j % KT) * P, (j % KT + 1) * P)
                    if first and j % KT == 0:
                        pe.wait_ge(w_lo_done, KT * (m + 1))
                    if not first or j >= 4:
                        pe.wait_ge(qk_hi_done, N_QK * n + j - 3)
                    for k in range(KT):
                        nc.tensor.matmul(qk_ps[j % 4][:], w_lo[:, m, k, cols], xt_hi[:, b, k, :], start=(k == 0),
                                         stop=False)
                        nc.tensor.matmul(qk_ps[j % 4][:], w_hi[:, m, k, cols], xt_lo[:, b, k, :], start=False,
                                         stop=False)
                        mm = nc.tensor.matmul(qk_ps[j % 4][:], w_hi[:, m, k, cols], xt_hi[:, b, k, :], start=False,
                                              stop=(k == KT - 1))
                    mm.then_inc(qk_ps_done, 1)
                    if not last and j >= KT:
                        if j == KT:
                            pe.wait_ge(x_norm_done, SUB * n + 2 * SUB)
                        transposes(n + 1, j - KT)
                if first:
                    pe.wait_ge(w_lo_done, 3 * KT)
                for j in range(N_V):
                    toks, cols = slice(j // 2 * P, (j // 2 + 1) * P), slice(j % 2 * 512, (j % 2 + 1) * 512)
                    if not first or j >= 2:
                        pe.wait_ge(v_full_done, N_V * n + j - 1)
                    for k in range(KT):
                        nc.tensor.matmul(v_ps[j % 2][:], xt_lo[:, b, k, toks], w_hi[:, 2, k, cols], start=(k == 0),
                                         stop=False)
                        nc.tensor.matmul(v_ps[j % 2][:], xt_hi[:, b, k, toks], w_lo[:, 2, k, cols], start=False,
                                         stop=False)
                        mm = nc.tensor.matmul(v_ps[j % 2][:], xt_hi[:, b, k, toks], w_hi[:, 2, k, cols], start=False,
                                              stop=(k == KT - 1))
                    mm.then_inc(v_ps_done, 1)
            tiles(pe, step)


GQ = 4
N_GROUPS = QT // GQ
BANK = 512
BANKS = []
for g in range(N_GROUPS):
    for kb in range(GQ * g + 1):
        BANKS.append([(g, kb, GQ * g, 0)])
    BANKS.append([(g, GQ * g + 1, GQ * g + 1, 0), (g, GQ * g + 3, GQ * g + 3, 3 * P)])
    BANKS.append([(g, GQ * g + 2, GQ * g + 2, (1 - len(BANKS) % 2) * 2 * P)])
NB = len(BANKS)
NU = NB // 2
FIRST_BANK = [min(b for b in range(NB) if BANKS[b][0][0] == g) for g in range(N_GROUPS)]
LAST_BANK = [max(b for b in range(NB) if BANKS[b][0][0] == g) for g in range(N_GROUPS)]
UNIT_COLS = [(BANKS[2 * u][0][3] if len(BANKS[2 * u]) == 1 else 0,
              BANK + sum((GQ * g + GQ - t) * P for g, _, t, _ in BANKS[2 * u + 1])) for u in range(NU)]
CHUNKS = [(t, k, min(GQ, t + 1 - k)) for t in range(QT) for k in range(0, t + 1, GQ)]
N_CHUNKS = len(CHUNKS)
CHUNK_SUM = [sum(c[2] for c in CHUNKS[:i + 1]) for i in range(N_CHUNKS)]
CHUNK_UNIT = [(s - 1) * NU // CHUNK_SUM[-1] for s in CHUNK_SUM]
LAST_CHUNK = [max(i for i in range(N_CHUNKS) if CHUNKS[i][0] // GQ == g) for g in range(N_GROUPS)]
ROW_UNIT = [CHUNK_UNIT[i] + 1 for i in LAST_CHUNK]
assert ROW_UNIT[-1] == NU and max(ROW_UNIT[:-1]) < NU
ITEMS = []
for u in range(NU + 1):
    ITEMS += [("chunk", i) for i in range(N_CHUNKS) if CHUNK_UNIT[i] == u]
    ITEMS += [("row", g) for g in range(N_GROUPS) if ROW_UNIT[g] == u]
MAX_BANKS = 3
CUT = [lo + (hi - lo) * 6 // 8 // P * P for lo, hi in UNIT_COLS]
HEAD_LOADS = 7
SLOTS = 3
P_SLOTS = 6
LAG = 4
LOW_LAG = 3
OUTPUT_UNIT = [(b + 1) // 2 + LAG for b in LAST_BANK]


def attend_phase(nc, q_scratch, k_scratch, v_scratch, o_scratch, ident_in, mask_in):
    with ExitStack() as ctx:
        sb = lambda name, shape, dt: ctx.enter_context(nc.sbuf_tensor(name, shape, dt))
        psum = lambda name, shape: ctx.enter_context(nc.psum_tensor(name, shape, F32))
        sem = lambda name: ctx.enter_context(nc.semaphore(name))
        slots = range(SLOTS)

        ident = sb("ident_b", [P, P], F32)
        ident_bf = sb("ident_bf", [P, P], BF16)
        ident_f16 = sb("ident_f16", [P, P], F16)
        mask = sb("mask", [P, P], BF16)
        exp_bias = sb("exp_bias", [P, 1], F32)
        q_hi2 = [sb(f"q_hi2_{i}", [P, S], F16) for i in slots]
        k_both = [sb(f"k_both_{i}", [P, S], F16) for i in slots]
        q_lo_max = [sb(f"q_lo_max_{i}", [P, S], F16) for i in slots]
        k_hi_one = [sb(f"k_hi_one_{i}", [P, S], F16) for i in slots]
        v_one = [sb(f"v_one_{i}", [P, QT, 2, HD + 2], F16) for i in slots]
        probs = [sb(f"probs{i}", [P, 2 * BANK], F32) for i in range(P_SLOTS)]
        p_hi = [sb(f"p_hi{i}", [P, 2 * BANK], F16) for i in range(P_SLOTS)]
        p_lo = [sb(f"p_lo{i}", [P, 2 * BANK], F16) for i in range(P_SLOTS)]
        chunk_max = sb("chunk_max", [P, N_GROUPS, GQ, N_GROUPS], F32)
        group_max = sb("group_max", [P, N_GROUPS, GQ], F32)
        max_cols = sb("max_cols", [P, GQ, HD + 1], F16)
        zeros = sb("zeros", [P, BANK], F16)
        inv_sum = sb("inv_sum", [P, GQ], F32)
        o_head = [sb(f"o_head{i}", [P, QT, HD], F32) for i in slots]

        st_ps = [psum(f"st_ps{i}", [P, 2 * BANK]) for i in range(2)]
        max_ps = [psum(f"max_ps{i}", [P, BANK]) for i in range(MAX_BANKS)]
        o_ps = psum("o_ps", [P, GQ, P])

        consts_loaded = sem("consts_loaded_b")
        head_loaded = [sem(f"head_loaded{i}") for i in slots]
        zero_done = sem("zero_done")
        set_done = sem("set_done_b")
        chunk_ps_done = sem("chunk_ps_done")
        chunk_done = sem("chunk_done")
        group_max_done = sem("group_max_done")
        max_cols_done = sem("max_cols_done")
        row_ps_done = sem("row_ps_done")
        row_done = sem("row_done")
        st_done = sem("st_done")
        exp_done = sem("exp_done")
        hi_done = sem("hi_done")
        lo0_done = sem("lo0_done")
        lo1_done = sem("lo1_done")
        pv_done = sem("pv_done")
        inv_done = sem("inv_done")
        o_done = sem("o_done")
        o_stored = [sem(f"o_stored{i}") for i in slots]

        def heads(eng, head):
            head(0, 0, 0, True, False)
            with eng.Fori(0, (BH - 2) // SLOTS) as i:
                head(3 * i + 1, 1, i, False, False)
                head(3 * i + 2, 2, i, False, False)
                head(3 * i + 3, 0, i + 1, False, False)
            head(BH - 1, 1, BH // SLOTS, False, True)

        def chunks(u):
            return [i for i in range(N_CHUNKS) if CHUNK_UNIT[i] == u]

        def max_bank(kind, i, slot):
            return max_ps[(len(ITEMS) * slot + ITEMS.index((kind, i))) % MAX_BANKS]

        SETS = 4 * SLOTS + 5
        block = ctx.enter_context(nc.Block())

        @block.sync
        def _(sp):
            sp.dma_start(ident[:], ident_in).then_inc(consts_loaded, 16)
            sp.dma_start(mask[:], mask_in).then_inc(consts_loaded, 16)

            def load(n, slot):
                halves = (slice(0, HD), slice(HD, P))
                by_feature = lambda tile, rows: tile[slot][rows, :].rearrange("f (c n) -> f c n", c=NC)
                q_part = lambda part: q_scratch[:, n, :, part, :].rearrange("c f n -> f c n")
                k_part = lambda part: k_scratch[:, n, :, part, :].rearrange("c f n -> f c n")
                for part, rows in enumerate(halves):
                    sp.dma_start(by_feature(q_hi2, rows), q_part(0)).then_inc(head_loaded[slot], 16)
                    sp.dma_start(by_feature(k_both, rows), k_part(part)).then_inc(head_loaded[slot], 16)
                sp.dma_start(by_feature(q_lo_max, halves[0]), q_part(1)).then_inc(head_loaded[slot], 16)
                sp.dma_start(by_feature(k_hi_one, halves[0]), k_part(0)).then_inc(head_loaded[slot], 16)
                sp.dma_start(v_one[slot][:, :, :, 0:HD], v_scratch[n].rearrange("p t (l f) -> p t l f", l=2)).then_inc(
                    head_loaded[slot], 16)

            def store(n, slot):
                sp.wait_ge(o_done, N_GROUPS * n + N_GROUPS)
                sp.dma_start(o_scratch[n], o_head[slot][:].rearrange("p t f -> p (t f)")).then_inc(o_stored[slot], 16)

            for n in range(SLOTS):
                load(n, n)
            store(0, 0)
            load(SLOTS, 0)
            with sp.Fori(0, (BH - 2) // SLOTS - 1) as i:
                for r in range(SLOTS):
                    store(3 * i + 1 + r, (1 + r) % SLOTS)
                    load(3 * i + 1 + r + SLOTS, (1 + r) % SLOTS)
            for n in range(BH - 4, BH):
                store(n, n % SLOTS)
                if n + SLOTS < BH:
                    load(n + SLOTS, n % SLOTS)
            for slot in slots:
                sp.wait_ge(o_stored[slot], 16 * (len(range(slot, BH, SLOTS)) + 1))

        @block.tensor
        def _(pe):
            def bank_free(kind, i, n):
                at = ITEMS.index((kind, i)) - MAX_BANKS
                old, j = ITEMS[at]
                m = n if at >= 0 else n - 1
                if isinstance(m, int) and m < 0:
                    return
                if old == "chunk":
                    pe.wait_ge(chunk_done, N_CHUNKS * m + j + 1)
                else:
                    pe.wait_ge(row_done, N_GROUPS * m + j + 1)

            def chunk_scores(i, n, slot, use):
                t, k0, blocks = CHUNKS[i]
                if i == 0:
                    pe.wait_ge(head_loaded[slot], 16 * HEAD_LOADS * use + 16 * HEAD_LOADS)
                bank = max_bank("chunk", i, slot)
                bank_free("chunk", i, n)
                w = blocks * P
                diagonal = k0 + blocks == t + 1
                mm = nc.tensor.matmul(bank[:, 0:w], q_hi2[slot][:, t * P:(t + 1) * P],
                                      k_both[slot][:, k0 * P:k0 * P + w], start=True, stop=not diagonal)
                if diagonal:
                    mm = nc.tensor.matmul(bank[:, w - P:w], ident_bf[:], mask[:], start=False, stop=True)
                mm.then_inc(chunk_ps_done, 1)

            def max_row(g, n, slot):
                pe.wait_ge(max_cols_done, N_GROUPS * n + g + 1)
                bank_free("row", g, n)
                for b in range(GQ):
                    mm = nc.tensor.matmul(max_bank("row", g, slot)[0:HD + 1, b * P:(b + 1) * P], max_cols[:, b, :], ident_f16[:],
                                          start=True, stop=True)
                mm.then_inc(row_ps_done, 1)

            def scores(u, n, slot):
                if not isinstance(n, int) or NU * n + u >= 2:
                    pe.wait_ge(exp_done, NU * n + u - 1)
                for b in (2 * u, 2 * u + 1):
                    if b in FIRST_BANK:
                        pe.wait_ge(row_done, N_GROUPS * n + BANKS[b][0][0] + 1)
                    for g, kb, t, at in BANKS[b]:
                        w = (GQ * g + GQ - t) * P
                        at += b % 2 * BANK
                        keys, queries = slice(kb * P, (kb + 1) * P), slice(t * P, t * P + w)
                        dst = st_ps[u % 2][:, at:at + w]
                        nc.tensor.matmul(dst, k_hi_one[slot][:, keys], q_lo_max[slot][:, queries], start=True, stop=False)
                        mm = nc.tensor.matmul(dst, k_both[slot][:, keys], q_hi2[slot][:, queries], start=False,
                                              stop=(kb != t))
                        if kb == t:
                            mm = nc.tensor.matmul(dst[:, 0:P], mask[:], ident_bf[:], start=False, stop=True)
                mm.then_inc(st_done, 1)

            def times_v(b, n, slot):
                u = b // 2
                pe.wait_ge(lo0_done, NU * n + u + 1)
                if b % 2 == 1 or CUT[u] < BANK:
                    pe.wait_ge(lo1_done, NU * n + u + 1)
                first = b in FIRST_BANK
                if first and (not isinstance(n, int) or N_GROUPS * n + BANKS[b][0][0] > 0):
                    pe.wait_ge(o_done, N_GROUPS * n + BANKS[b][0][0])
                if first:
                    nc.tensor.matmul(o_ps[:], zeros[:, 0:P], zeros[:], start=True, stop=False)
                for g, kb, t0, at in BANKS[b]:
                    at += b % 2 * BANK
                    for t in range(t0, GQ * g + GQ):
                        rows = slice(at + (t - t0) * P, at + (t - t0 + 1) * P)
                        dst = o_ps[:, t % GQ, 0:HD + 1]
                        nc.tensor.matmul(dst, p_lo[u % P_SLOTS][:, rows], v_one[slot][:, kb, 0, 0:HD + 1], start=False, stop=False)
                        nc.tensor.matmul(dst, p_hi[u % P_SLOTS][:, rows], v_one[slot][:, kb, 1, 0:HD + 1], start=False, stop=False)
                        mm = nc.tensor.matmul(dst, p_hi[u % P_SLOTS][:, rows], v_one[slot][:, kb, 0, 0:HD + 1], start=False,
                                              stop=(b == LAST_BANK[g] and t == GQ * g + GQ - 1))
                mm.then_inc(pv_done, 1)

            def head(n, slot, use, first, last):
                after, before = (slot + 1) % SLOTS, (slot + 2) % SLOTS
                for u in range(NU):
                    ends = 2 * (u - LAG) in LAST_BANK
                    if not ends:
                        scores(u, n, slot)
                    if u >= LAG:
                        times_v(2 * (u - LAG), n, slot)
                    elif not first:
                        times_v(2 * (u - LAG) + NB, n - 1, before)
                    if ends:
                        scores(u, n, slot)
                    if u == 0:
                        max_row(N_GROUPS - 1, n, slot)
                    if not last:
                        for i in chunks(u):
                            chunk_scores(i, n + 1, after, use + (slot == SLOTS - 1))
                    if u >= LAG:
                        times_v(2 * (u - LAG) + 1, n, slot)
                    elif not first:
                        times_v(2 * (u - LAG) + 1 + NB, n - 1, before)
                    if not last:
                        for g in range(N_GROUPS - 1):
                            if ROW_UNIT[g] == u:
                                max_row(g, n + 1, after)
                if last:
                    for b in range(NB - 2 * LAG, NB):
                        times_v(b, n, slot)

            pe.wait_ge(consts_loaded, 32)
            pe.wait_ge(set_done, SETS)
            for kind, i in ITEMS[:-1]:
                if kind == "chunk":
                    chunk_scores(i, 0, 0, 0)
                else:
                    max_row(i, 0, 0)
            heads(pe, head)

        @block.vector
        def _(dve):
            for i in slots:
                nc.vector.memset(q_lo_max[i][HD:P, :], 0.0).then_inc(set_done, 1)
                nc.vector.memset(k_hi_one[i][HD:P, :], 0.0).then_inc(zero_done, 1)
                nc.vector.memset(v_one[i][:, :, 0, HD:HD + 1], 1.0).then_inc(set_done, 1)
                nc.vector.memset(v_one[i][:, :, 1, HD:HD + 1], 0.0).then_inc(set_done, 1)
            dve.wait_ge(zero_done, SLOTS)
            for i in slots:
                nc.vector.memset(k_hi_one[i][HD:HD + 1, :], MAX_SCALE).then_inc(set_done, 1)
            nc.vector.memset(max_cols[:], 0.0).then_inc(set_done, 1)
            nc.vector.memset(zeros[:], 0.0).then_inc(set_done, 1)
            nc.vector.memset(exp_bias[:], LOG_P_SCALE).then_inc(set_done, 1)
            dve.wait_ge(consts_loaded, 32)
            nc.vector.tensor_copy(ident_bf[:], ident[:]).then_inc(set_done, 1)
            nc.vector.tensor_copy(ident_f16[:], ident[:]).then_inc(set_done, 1)
            dve.wait_ge(set_done, SETS)

            def maxima(i, n, slot):
                t, k0, blocks = CHUNKS[i]
                dve.wait_ge(chunk_ps_done, N_CHUNKS * n + i + 1)
                nc.vector.tensor_reduce(chunk_max[:, t // GQ, t % GQ, k0 // GQ:k0 // GQ + 1], max_bank("chunk", i, slot)[:, 0:blocks * P],
                                        AX_X, ALU.max).then_inc(chunk_done, 1)
                g = t // GQ
                if i == LAST_CHUNK[g]:
                    dve.wait_ge(chunk_done, N_CHUNKS * n + i + 1)
                    nc.vector.tensor_reduce(group_max[:, g, :], chunk_max[:, g, :, 0:g + 1], AX_X, ALU.max).then_inc(
                        group_max_done, 1)
                    dve.wait_ge(group_max_done, N_GROUPS * n + g + 1)
                    if not isinstance(n, int) or N_GROUPS * n + g > 0:
                        dve.wait_ge(row_ps_done, N_GROUPS * n + g)
                    nc.vector.tensor_scalar(max_cols[:, :, HD], group_max[:, g, :], -1.0 / MAX_SCALE, None,
                                            ALU.mult).then_inc(max_cols_done, 1)

            def low_last(u, n):
                cols = slice(CUT[u], UNIT_COLS[u][1])
                dve.wait_ge(hi_done, NU * n + u + 1)
                nc.vector.tensor_tensor(p_lo[u % P_SLOTS][:, cols], probs[u % P_SLOTS][:, cols], p_hi[u % P_SLOTS][:, cols],
                                        ALU.subtract).then_inc(lo1_done, 1)

            def output(g, n, slot, use):
                dve.wait_ge(pv_done, NB * n + LAST_BANK[g] + 1)
                nc.vector.reciprocal(inv_sum[:], o_ps[:, :, HD]).then_inc(inv_done, 1)
                dve.wait_ge(inv_done, N_GROUPS * n + g + 1)
                if g == 0:
                    dve.wait_ge(o_stored[slot], 16 * use + 16)
                nc.vector.tensor_tensor(o_head[slot][:, GQ * g:GQ * g + GQ, :], o_ps[:, :, 0:HD],
                                        inv_sum[:].unsqueeze(2).broadcast_to([P, GQ, HD]), ALU.mult).then_inc(o_done, 1)

            def head(n, slot, use, first, last):
                for u in range(NU):
                    for g in range(N_GROUPS):
                        if OUTPUT_UNIT[g] == u:
                            output(g, n, slot, use)
                        if OUTPUT_UNIT[g] == u + NU and not first:
                            output(g, n - 1, (slot + 2) % SLOTS, use - (slot == 0))
                    if u >= LOW_LAG:
                        low_last(u - LOW_LAG, n)
                    elif not first:
                        low_last(u - LOW_LAG + NU, n - 1)
                    if not last:
                        for i in chunks(u):
                            maxima(i, n + 1, (slot + 1) % SLOTS)
                if last:
                    for u in range(NU - LOW_LAG, NU):
                        low_last(u, n)
                    output(N_GROUPS - 1, n, slot, use)

            for i in range(N_CHUNKS):
                maxima(i, 0, 0)
            heads(dve, head)

        @block.scalar
        def _(act):
            act.wait_ge(set_done, SETS)

            def max_row(g, n, slot):
                act.wait_ge(row_ps_done, N_GROUPS * n + g + 1)
                nc.scalar.activation(q_lo_max[slot][HD:HD + 1, g * BANK:(g + 1) * BANK], max_bank("row", g, slot)[HD:HD + 1, :],
                                     ACT.Copy).then_inc(row_done, 1)

            def exponentials(u, n):
                act.wait_ge(st_done, NU * n + u + 1)
                if not isinstance(n, int) or NU * n + u >= P_SLOTS:
                    act.wait_ge(lo0_done, NU * n + u - P_SLOTS + 1)
                    act.wait_ge(lo1_done, NU * n + u - P_SLOTS + 1)
                cols = slice(*UNIT_COLS[u])
                nc.scalar.activation(probs[u % P_SLOTS][:, cols], st_ps[u % 2][:, cols], ACT.Exp, bias=exp_bias[:],
                                     scale=SOFTMAX_SCALE).then_inc(exp_done, 1)

            def high(u, n):
                act.wait_ge(exp_done, NU * n + u + 1)
                if not isinstance(n, int) or NU * n + u >= P_SLOTS:
                    act.wait_ge(pv_done, NB * n + 2 * (u - P_SLOTS) + 2)
                cols = slice(*UNIT_COLS[u])
                nc.scalar.activation(p_hi[u % P_SLOTS][:, cols], probs[u % P_SLOTS][:, cols], ACT.Copy).then_inc(hi_done, 1)

            def head(n, slot, use, first, last):
                for u in range(NU):
                    exponentials(u, n)
                    if u == 0:
                        max_row(N_GROUPS - 1, n, slot)
                    if not last:
                        for g in range(N_GROUPS - 1):
                            if ROW_UNIT[g] == u:
                                max_row(g, n + 1, (slot + 1) % SLOTS)
                    if u >= 1:
                        high(u - 1, n)
                    elif not first:
                        high(NU - 1, n - 1)
                if last:
                    high(NU - 1, n)

            for g in range(N_GROUPS - 1):
                max_row(g, 0, 0)
            heads(act, head)

        @block.gpsimd
        def _(pool):
            for slot in slots:
                pool.sem_inc(o_stored[slot], 16)

            def low_first(u, n):
                pool.wait_ge(hi_done, NU * n + u + 1)
                cols = slice(UNIT_COLS[u][0], CUT[u])
                nc.gpsimd.tensor_tensor(p_lo[u % P_SLOTS][:, cols], probs[u % P_SLOTS][:, cols], p_hi[u % P_SLOTS][:, cols],
                                        ALU.subtract).then_inc(lo0_done, 1)

            def head(n, slot, use, first, last):
                for u in range(NU):
                    low_first(u, n)
            heads(pool, head)


def finish_phase(nc, x, o_scratch, wo, b_o, ident_in, ffn_in, ffn_probe, ffn_mix, own_in, rank_in, center, slope, out):
    with ExitStack() as ctx:
        sb = lambda name, shape, dt: ctx.enter_context(nc.sbuf_tensor(name, shape, dt))
        psum = lambda name, shape: ctx.enter_context(nc.psum_tensor(name, shape, F32))
        sem = lambda name: ctx.enter_context(nc.semaphore(name))
        NT = B * QT
        HALF = 512
        halves = [slice(0, HALF), slice(HALF, D)]
        SEL, LOW, DIF = slice(0, 64), slice(64, 128), slice(128, 136)

        ident = sb("ident_c", [P, P], F32)
        w_raw = sb("wo_raw", [P, 2, D], F32)
        w_hi = sb("wo_hi", [P, KT, D], F16)
        w_lo = sb("wo_lo", [P, KT, D], F16)
        bo_row = sb("bo_row", [P, D], F32)
        ffn_w = sb("ffn_w", [P, KT, FF], F32)
        probe = sb("probe", [P, KT, 2 * N_EXP], F32)
        mix_w = sb("mix_w", [MIX, D], F32)
        own = sb("own", [2 * N_EXP, FF], F32)
        ones = sb("ones", [2 * N_EXP, P], F32)
        own_dots = sb("own_dots", [2 * N_EXP, FF], F32)
        offsets = sb("offsets", [P, FF], F32)
        rank = sb("rank", [P, N_EXP], F32)
        center_row = sb("center_row", [P, N_EXP], F32)
        slope_row = sb("slope_row", [P, N_EXP], F32)
        eps = sb("eps_c", [P, 1], F32)
        minus_half = sb("minus_half_c", [P, 1], F32)
        o_in = [sb(f"o_in{i}", [P, D], F32) for i in range(4)]
        x_in = [sb(f"x_in_c{i}", [P, D], F32) for i in range(4)]
        ot_hi = [sb(f"ot_hi{i}", [P, KT, P], F16) for i in range(2)]
        ot_lo = [sb(f"ot_lo{i}", [P, KT, P], F16) for i in range(2)]
        attn = [sb(f"attn{i}", [P, D], F32) for i in range(2)]
        x1 = [sb(f"x1_{i}", [P, D], F32) for i in range(4)]
        x2 = [sb(f"x2_{i}", [P, D], F32) for i in range(4)]
        square = sb("square", [P, D], F32)
        x2_norm2 = [sb(f"x2_norm2_{i}", [P, 1], F32) for i in range(4)]
        x2t = sb("x2t", [P, KT, P], F32)
        mixed = [sb(f"mixed{i}", [P, D], F32) for i in range(2)]
        y = [sb(f"y{i}", [P, D], F32) for i in range(2)]
        result = [sb(f"result{i}", [P, D], F32) for i in range(2)]
        stats = sb("stats_c", [P, 3, 2, 6], F32)
        moments = sb("moments_c", [P, 3, 2], F32)
        var_eps = sb("var_eps_c", [P, 3], F32)
        rstd = sb("rstd_c", [P, 3], F32)
        neg_mean = sb("neg_mean", [P, 3], F32)
        shift = sb("shift", [P, 3], F32)
        dots = sb("dots", [P, 2 * 64], F32)
        dots2 = sb("dots2", [P, 64], F32)
        select = sb("select", [P, 10, N_EXP], F32)
        sel_scale = [sb(f"sel_scale{i}", [P, 1], F32) for i in range(2)]
        sel_rest = [sb(f"sel_rest{i}", [P, 1], F32) for i in range(2)]
        top_rank = sb("top_rank", [P, 1], F32)
        mix = sb("mix", [P, MIX], F32)
        mix_t = sb("mix_t", [MIX, P], F32)

        ot_ps = [psum(f"ot_ps{i}", [P, HALF]) for i in range(2)]
        proj_ps = [psum(f"proj_ps{i}", [P, HALF]) for i in range(2)]
        ffn_ps = [psum(f"ffn_ps{i}", [P, HALF]) for i in range(2)]
        dots_ps = psum("dots_ps", [P, FF])
        mix_ps = psum("mix_ps", [MIX, P])

        consts_loaded = sem("consts_loaded_c")
        set_done = sem("set_done_c")
        w_loaded = [sem(f"wo_loaded{i}") for i in range(2)]
        w_hi_done = sem("wo_hi_done")
        w_lo_done = sem("wo_lo_done")
        own_ps_done = sem("own_ps_done")
        own_done = sem("own_done")
        offsets_ps_done = sem("offsets_ps_done")
        offsets_done = sem("offsets_done")
        tile_loaded = [sem(f"tile_loaded{i}") for i in range(4)]
        ot_ps_done = sem("ot_ps_done")
        ot_hi_done = sem("ot_hi_done")
        ot_lo_done = sem("ot_lo_done")
        proj_done = sem("proj_done")
        attn_done = sem("attn_done")
        stats_done = sem("stats_done_c")
        moments_done = [sem(f"moments_done_c{i}") for i in range(3)]
        var_done = [sem(f"var_done_c{i}") for i in range(3)]
        rstd_done = [sem(f"rstd_done_c{i}") for i in range(3)]
        shift_done = [sem(f"shift_done{i}") for i in range(3)]
        attn_norm_done = sem("attn_norm_done")
        x1_done = sem("x1_done")
        x2_done = sem("x2_done")
        norm2_done = sem("norm2_done")
        x2t_ps_done = sem("x2t_ps_done")
        x2t_done = sem("x2t_done")
        dots_ps_done = sem("dots_ps_done")
        gate_step = sem("gate_step")
        logit_done = sem("logit_done")
        gate_exp_done = sem("gate_exp_done")
        mix_done = sem("mix_done")
        mix_ps_done = sem("mix_ps_done")
        mix_t_done = sem("mix_t_done")
        ffn_done = sem("ffn_done")
        mixed_done = sem("mixed_done")
        y_done = sem("y_done")
        y_norm_done = sem("y_norm_done")
        result_done = sem("result_done")
        stored = [sem(f"stored{i}") for i in range(2)]

        x_view = x.rearrange("(b t p) d -> b t p d", b=B, t=QT)
        out_view = out.rearrange("(b t p) d -> b t p d", b=B, t=QT)
        o_view = o_scratch.rearrange("(b h) p (t f) -> b t p h f", b=B, f=HD)
        wo_view = wo.rearrange("(k p) o -> k p o", p=P)
        CONSTS = 9

        def tiles(eng, step):
            def fixed(m):
                step(m, m // 2, m % 4, lambda d: 0 <= m + d < NT)
            for m in range(4):
                fixed(m)
            with eng.Fori(1, NT // 4 - 1) as i:
                for v in range(4):
                    step(4 * i + v, 2 * i + v // 2, v, lambda d: True)
            for m in range(NT - 4, NT + 4):
                fixed(m)

        block = ctx.enter_context(nc.Block())

        @block.sync
        def _(sp):
            def load(m, t, r):
                sp.dma_start(o_in[r][:].rearrange("p (h f) -> p h f", f=HD), o_view[r % 2, t]).then_inc(
                    tile_loaded[r], 16)
                sp.dma_start(x_in[r][:], x_view[r % 2, t]).then_inc(tile_loaded[r], 16)

            sp.dma_start(ident[:], ident_in).then_inc(consts_loaded, 16)
            load(0, 0, 0)
            for k in range(KT):
                if k >= 2:
                    sp.wait_ge(w_lo_done, k - 1)
                sp.dma_start(w_raw[:, k % 2, :], wo_view[k]).then_inc(w_loaded[k % 2], 16)
            sp.dma_start(bo_row[:], b_o.partition_broadcast(P)).then_inc(consts_loaded, 16)
            sp.dma_start(ffn_w[:], ffn_in.rearrange("(k p) o -> p k o", p=P)).then_inc(consts_loaded, 16)
            sp.dma_start(probe[:], ffn_probe.rearrange("(k p) o -> p k o", p=P)).then_inc(consts_loaded, 16)
            sp.dma_start(mix_w[:], ffn_mix).then_inc(consts_loaded, 16)
            sp.dma_start(own[:], own_in).then_inc(consts_loaded, 16)
            sp.dma_start(rank[:], rank_in).then_inc(consts_loaded, 16)
            sp.dma_start(center_row[:], center.partition_broadcast(P)).then_inc(consts_loaded, 16)
            sp.dma_start(slope_row[:], slope.partition_broadcast(P)).then_inc(consts_loaded, 16)
            load(1, 0, 1)
            load(2, 1, 2)

            def step(m, t, r, has):
                if has(3):
                    if has(-1):
                        sp.wait_ge(ot_ps_done, 2 * m)
                        sp.wait_ge(x1_done, m)
                    load(m + 3, t + 1 + r % 2, (r + 3) % 4)
                if has(-4):
                    sp.wait_ge(result_done, m - 3)
                    sp.dma_start(out_view[r % 2, t - 2], result[r % 2][:]).then_inc(stored[r % 2], 16)

            tiles(sp, step)
            for i in range(2):
                sp.wait_ge(stored[i], 16 * (NT // 2 + 1))

        @block.tensor
        def _(pe):
            def transpose_attention(m, r):
                for h in range(2):
                    pe.wait_ge(tile_loaded[r], 8 * (m - r) + 32)
                    if not isinstance(m, int) or m > 0:
                        pe.wait_ge(ot_lo_done, 2 * m - 1 + h)
                    for k in range(4):
                        at = slice((4 * h + k) * P, (4 * h + k + 1) * P)
                        tr = nc.tensor.transpose(ot_ps[h][:, k * P:(k + 1) * P], o_in[r][:, at], ident[:])
                    tr.then_inc(ot_ps_done, 1)

            def project(m, r, h):
                if h == 0:
                    pe.wait_ge(ot_lo_done, 2 * m + 2)
                if not isinstance(m, int) or m > 0:
                    pe.wait_ge(attn_done, 2 * m - 1 + h)
                for k in range(KT):
                    nc.tensor.matmul(proj_ps[h][:], ot_lo[r % 2][:, k, :], w_hi[:, k, halves[h]], start=(k == 0),
                                     stop=False)
                    nc.tensor.matmul(proj_ps[h][:], ot_hi[r % 2][:, k, :], w_lo[:, k, halves[h]], start=False,
                                     stop=False)
                    mm = nc.tensor.matmul(proj_ps[h][:], ot_hi[r % 2][:, k, :], w_hi[:, k, halves[h]], start=False,
                                          stop=(k == KT - 1))
                mm.then_inc(proj_done, 1)

            def transpose_x2(m, r):
                pe.wait_ge(x2_done, m + 1)
                for h in range(2):
                    if h == 0 and (not isinstance(m, int) or m > 1):
                        pe.wait_ge(mixed_done, 2 * m - 2)
                    for k in range(4):
                        at = slice((4 * h + k) * P, (4 * h + k + 1) * P)
                        tr = nc.tensor.transpose(ffn_ps[h][:, k * P:(k + 1) * P], x2[r][:, at], ident[:])
                    tr.then_inc(x2t_ps_done, 1)

            def ffn_dots(m):
                pe.wait_ge(x2t_done, 2 * m + 2)
                if not isinstance(m, int) or m > 0:
                    pe.wait_ge(mix_done, m)
                for k in range(KT):
                    mm = nc.tensor.matmul(dots_ps[:], x2t[:, k, :], ffn_w[:, k, :], start=(k == 0),
                                          stop=(k == KT - 1))
                mm.then_inc(dots_ps_done, 1)

            def mix_transpose(m):
                pe.wait_ge(mix_done, m + 1)
                nc.tensor.transpose(mix_ps[:], mix[:], ident[:]).then_inc(mix_ps_done, 1)

            def ffn_mix_out(m):
                pe.wait_ge(mix_t_done, m + 1)
                for h in range(2):
                    nc.tensor.matmul(ffn_ps[h][:], mix_t[:], mix_w[:, halves[h]], start=True, stop=True).then_inc(
                        ffn_done, 1)

            def step(m, t, r, has):
                if has(-2):
                    transpose_x2(m - 2, (r + 2) % 4)
                if has(-3):
                    mix_transpose(m - 3)
                if has(1):
                    transpose_attention(m + 1, (r + 1) % 4)
                if has(0):
                    project(m, r, 0)
                if has(-2):
                    ffn_dots(m - 2)
                if has(-3):
                    ffn_mix_out(m - 3)
                if has(0):
                    project(m, r, 1)

            pe.wait_ge(consts_loaded, 16 * CONSTS)
            for k in range(KT):
                mm = nc.tensor.matmul(dots_ps[0:2 * N_EXP, :], probe[:, k, :], ffn_w[:, k, :], start=(k == 0),
                                      stop=(k == KT - 1))
            mm.then_inc(own_ps_done, 1)
            pe.wait_ge(own_done, 1)
            nc.tensor.matmul(dots_ps[:], ones[:], own_dots[:], start=True, stop=True).then_inc(offsets_ps_done, 1)
            transpose_attention(0, 0)
            pe.wait_ge(w_lo_done, KT)
            pe.wait_ge(offsets_done, 1)
            tiles(pe, step)

        @block.vector
        def _(dve):
            nc.vector.memset(ones[:], 1.0)

            def attention_low(m, r):
                for h in range(2):
                    dve.wait_ge(ot_hi_done, 2 * m + 1 + h)
                    nc.vector.tensor_tensor(ot_lo[r % 2][:, 4 * h:4 * h + 4, :].rearrange("p k n -> p (k n)"), ot_ps[h][:],
                                            ot_hi[r % 2][:, 4 * h:4 * h + 4, :].rearrange("p k n -> p (k n)"),
                                            ALU.subtract).then_inc(ot_lo_done, 1)

            def norm_stats(which, m, tile):
                for h in range(2):
                    bn = nc.vector.bn_stats(stats[:, which, h, :], tile[:, halves[h]])
                bn.then_inc(stats_done, 1)
                dve.wait_ge(stats_done, 1)
                dve.sem_clear(stats_done)
                nc.vector.bn_aggr(moments[:, which, :], stats[:, which].rearrange("p h e -> p (h e)")).then_inc(
                    moments_done[which], 1)

            def attention_out(m, r, h):
                dve.wait_ge(proj_done, 2 * m + 1 + h)
                nc.vector.scalar_tensor_tensor(attn[r % 2][:, halves[h]], proj_ps[h][:], OUT_UNSCALE,
                                               bo_row[:, halves[h]], ALU.mult, ALU.add).then_inc(attn_done, 1)

            def attention_stats(m, r):
                dve.wait_ge(attn_done, 2 * m + 2)
                norm_stats(0, m, attn[r % 2])

            def x1_stats(m, r):
                dve.wait_ge(x1_done, m + 1)
                norm_stats(1, m, x1[r])

            GATE_STEPS = 16

            def gates(m, r):
                count = [0]

                def step(op):
                    count[0] += 1
                    op.then_inc(gate_step, 1)

                def settled():
                    dve.wait_ge(gate_step, GATE_STEPS * m + count[0])
                num, dist, inv, score, off, logit, gate1, gate, first, chosen = (select[:, i, :] for i in range(10))
                dve.wait_ge(dots_ps_done, m + 1)
                dve.wait_ge(norm2_done, m + 1)
                step(nc.vector.tensor_tensor(dots[:], dots_ps[:, 0:128], offsets[:, 0:128], ALU.subtract))
                step(nc.vector.scalar_tensor_tensor(dist, dots_ps[:, DIF], -2.0, offsets[:, DIF], ALU.mult, ALU.add))
                settled()
                step(nc.vector.tensor_tensor(dots2[:], dots[:, SEL], dots[:, SEL], ALU.mult))
                step(nc.vector.tensor_scalar(dist, dist, x2_norm2[r][:], None, ALU.add))
                settled()
                step(nc.vector.tensor_reduce(num, dots2[:].rearrange("p (n s) -> p n s", n=N_EXP), AX_X, ALU.add))
                step(nc.vector.reciprocal(inv, dist))
                settled()
                step(nc.vector.tensor_tensor(score, num, inv, ALU.mult))
                settled()
                step(nc.vector.tensor_tensor(off, score, center_row[:], ALU.subtract))
                settled()
                nc.vector.tensor_tensor(logit, off, slope_row[:], ALU.mult).then_inc(logit_done, 1)
                dve.wait_ge(gate_exp_done, m + 1)
                step(nc.vector.tensor_scalar(gate1, gate1, 1.0, None, ALU.add))
                settled()
                step(nc.vector.reciprocal(gate, gate1))
                settled()
                if not isinstance(m, int) or m >= 2:
                    dve.wait_ge(y_done, m - 1)
                    dve.wait_ge(mixed_done, 2 * m - 2)
                step(nc.vector.tensor_reduce(sel_scale[r % 2][:], gate, AX_X, ALU.max))
                settled()
                step(nc.vector.tensor_scalar(sel_rest[r % 2][:], sel_scale[r % 2][:], -1.0, 1.0, ALU.mult, ALU.add))
                step(nc.vector.scalar_tensor_tensor(first, gate, sel_scale[r % 2][:], rank[:], ALU.is_equal, ALU.mult))
                settled()
                step(nc.vector.tensor_reduce(top_rank[:], first, AX_X, ALU.max))
                settled()
                if not isinstance(m, int) or m >= 1:
                    dve.wait_ge(mix_ps_done, m)
                step(nc.vector.tensor_scalar(mix[:, 64:MIX], rank[:], top_rank[:], None, ALU.is_equal))
                step(nc.vector.tensor_scalar(chosen, rank[:], top_rank[:], None, ALU.is_equal))
                settled()
                assert count[0] == GATE_STEPS, count
                nc.vector.tensor_tensor(mix[:, 0:64].rearrange("p (n h) -> p n h", n=N_EXP),
                                        dots[:, LOW].rearrange("p (n h) -> p n h", n=N_EXP),
                                        chosen.unsqueeze(2).broadcast_to([P, N_EXP, N_LOW]), ALU.mult).then_inc(
                    mix_done, 1)

            def ffn_out(m, r):
                dve.wait_ge(mixed_done, 2 * m + 2)
                nc.vector.scalar_tensor_tensor(y[r % 2][:], x2[r][:], sel_rest[r % 2][:], mixed[r % 2][:], ALU.mult,
                                               ALU.add).then_inc(y_done, 1)
                dve.wait_ge(y_done, m + 1)
                norm_stats(2, m, y[r % 2])

            def step(m, t, r, has):
                if has(-1):
                    attention_out(m - 1, (r + 3) % 4, 1)
                    attention_stats(m - 1, (r + 3) % 4)
                if has(-4):
                    ffn_out(m - 4, r)
                if has(1):
                    attention_low(m + 1, (r + 1) % 4)
                if has(-1):
                    x1_stats(m - 1, (r + 3) % 4)
                if has(0):
                    attention_out(m, r, 0)
                if has(-2):
                    gates(m - 2, (r + 2) % 4)

            for k in range(KT):
                dve.wait_ge(w_hi_done, k + 1)
                nc.vector.scalar_tensor_tensor(w_lo[:, k, :], w_raw[:, k % 2, :], W_SCALE, w_hi[:, k, :], ALU.mult,
                                               ALU.subtract).then_inc(w_lo_done, 1)
            dve.wait_ge(consts_loaded, 16 * CONSTS)
            dve.wait_ge(own_ps_done, 1)
            nc.vector.tensor_tensor(own_dots[:], dots_ps[0:2 * N_EXP, :], own[:], ALU.mult).then_inc(own_done, 1)
            dve.wait_ge(offsets_ps_done, 1)
            nc.vector.tensor_copy(offsets[:], dots_ps[:]).then_inc(offsets_done, 1)
            dve.wait_ge(offsets_done, 1)
            attention_low(0, 0)
            tiles(dve, step)

        @block.scalar
        def _(act):
            def attention_high(m, r):
                for h in range(2):
                    act.wait_ge(ot_ps_done, 2 * m + 1 + h)
                    if h == 0 and (not isinstance(m, int) or m >= 2):
                        act.wait_ge(proj_done, 2 * m - 2)
                    nc.scalar.activation(ot_hi[r % 2][:, 4 * h:4 * h + 4, :].rearrange("p k n -> p (k n)"), ot_ps[h][:],
                                         ACT.Copy).then_inc(ot_hi_done, 1)

            def attention_norm(m, r):
                act.wait_ge(shift_done[0], m + 1)
                nc.scalar.activation(attn[r % 2][:], attn[r % 2][:], ACT.Identity, bias=shift[:, 0:1],
                                     scale=rstd[:, 0:1]).then_inc(attn_norm_done, 1)

            def x2_norm(m, r):
                act.wait_ge(shift_done[1], m + 1)
                nc.scalar.activation(x2[r][:], x1[r][:], ACT.Identity, bias=shift[:, 1:2],
                                     scale=rstd[:, 1:2]).then_inc(x2_done, 1)

            def x2_square(m, r):
                act.wait_ge(x2_done, m + 1)
                nc.scalar.activation(square[:], x2[r][:], ACT.Square, accum_out=x2_norm2[r][:]).then_inc(norm2_done, 1)

            def x2_transposed(m):
                for h in range(2):
                    act.wait_ge(x2t_ps_done, 2 * m + 1 + h)
                    if h == 0 and (not isinstance(m, int) or m >= 1):
                        act.wait_ge(dots_ps_done, m)
                    nc.scalar.activation(x2t[:, 4 * h:4 * h + 4, :].rearrange("p k n -> p (k n)"), ffn_ps[h][:],
                                         ACT.Copy).then_inc(x2t_done, 1)

            def gate_exp(m):
                act.wait_ge(logit_done, m + 1)
                nc.scalar.activation(select[:, 6, :], select[:, 5, :], ACT.Exp, scale=-1.0).then_inc(gate_exp_done, 1)

            def mix_transposed(m):
                act.wait_ge(mix_ps_done, m + 1)
                if not isinstance(m, int) or m >= 1:
                    act.wait_ge(ffn_done, 2 * m)
                nc.scalar.activation(mix_t[:], mix_ps[:], ACT.Copy).then_inc(mix_t_done, 1)

            def ffn_gated(m, r):
                for h in range(2):
                    act.wait_ge(ffn_done, 2 * m + 1 + h)
                    if h == 0 and (not isinstance(m, int) or m >= 2):
                        act.wait_ge(y_done, m - 1)
                    nc.scalar.activation(mixed[r % 2][:, halves[h]], ffn_ps[h][:], ACT.Copy,
                                         scale=sel_scale[r % 2][:]).then_inc(mixed_done, 1)

            def ffn_norm(m, r):
                act.wait_ge(shift_done[2], m + 1)
                nc.scalar.activation(y[r % 2][:], y[r % 2][:], ACT.Identity, bias=shift[:, 2:3],
                                     scale=rstd[:, 2:3]).then_inc(y_norm_done, 1)

            def step(m, t, r, has):
                if has(-2):
                    x2_transposed(m - 2)
                if has(-3):
                    mix_transposed(m - 3)
                if has(1):
                    attention_high(m + 1, (r + 1) % 4)
                if has(-1):
                    attention_norm(m - 1, (r + 3) % 4)
                if has(-4):
                    ffn_norm(m - 4, r)
                if has(-1):
                    x2_norm(m - 1, (r + 3) % 4)
                if has(-2):
                    gate_exp(m - 2)
                if has(-3):
                    ffn_gated(m - 3, (r + 1) % 4)
                if has(-1):
                    x2_square(m - 1, (r + 3) % 4)

            for k in range(KT):
                act.wait_ge(w_loaded[k % 2], 16 * (k // 2 + 1))
                nc.scalar.activation(w_hi[:, k, :], w_raw[:, k % 2, :], ACT.Copy, scale=W_SCALE).then_inc(w_hi_done, 1)
            attention_high(0, 0)
            tiles(act, step)

        @block.gpsimd
        def _(pool):
            nc.gpsimd.memset(eps[:], EPS).then_inc(set_done, 1)
            nc.gpsimd.memset(minus_half[:], -0.5).then_inc(set_done, 1)
            pool.wait_ge(set_done, 2)
            for i in range(2):
                pool.sem_inc(stored[i], 16)

            def norm_scale(which, m):
                pool.wait_ge(moments_done[which], m + 1)
                w = slice(which, which + 1)
                nc.gpsimd.tensor_tensor(var_eps[:, w], moments[:, which, 1:2], eps[:], ALU.add).then_inc(
                    var_done[which], 1)
                nc.gpsimd.tensor_scalar(neg_mean[:, w], moments[:, which, 0:1], -1.0, None, ALU.mult).then_inc(
                    var_done[which], 1)
                pool.wait_ge(var_done[which], 2 * m + 2)
                nc.gpsimd.tensor_tensor(rstd[:, w], var_eps[:, w], minus_half[:], ALU.pow).then_inc(
                    rstd_done[which], 1)
                pool.wait_ge(rstd_done[which], m + 1)
                nc.gpsimd.tensor_tensor(shift[:, w], neg_mean[:, w], rstd[:, w], ALU.mult).then_inc(
                    shift_done[which], 1)

            def residual(m, r):
                pool.wait_ge(attn_norm_done, m + 1)
                nc.gpsimd.tensor_tensor(x1[r][:], x_in[r][:], attn[r % 2][:], ALU.add).then_inc(x1_done, 1)

            def final(m, r):
                pool.wait_ge(y_norm_done, m + 1)
                pool.wait_ge(stored[r % 2], stores(m, r))
                nc.gpsimd.tensor_tensor(result[r % 2][:], x1[r][:], y[r % 2][:], ALU.add).then_inc(result_done, 1)

            def stores(m, r):
                return 16 * (m // 2 + 1) if isinstance(m, int) else 8 * (m - r % 2) + 16

            def step(m, t, r, has):
                if has(-1):
                    norm_scale(0, m - 1)
                    residual(m - 1, (r + 3) % 4)
                if has(-4):
                    norm_scale(2, m - 4)
                if has(-1):
                    norm_scale(1, m - 1)
                if has(-4):
                    final(m - 4, r)
            tiles(pool, step)


def attention_ffn(nc, x, w_qkv, b_cols, b_v, w_o, b_o, ffn_in, ffn_probe, ffn_mix, center, slope, ident, mask, own, rank,
                  out):
    q_scratch = nc.dram_tensor("q_scratch", (NC, BH, HD, 2, TOK), F16, kind="Internal").ap()
    k_scratch = nc.dram_tensor("k_scratch", (NC, BH, HD, 2, TOK), F16, kind="Internal").ap()
    v_scratch = nc.dram_tensor("v_scratch", (BH, P, QT, 2 * HD), F16, kind="Internal").ap()
    o_scratch = nc.dram_tensor("o_scratch", (BH, P, QT * HD), F32, kind="Internal").ap()
    project_phase(nc, x, w_qkv, b_cols, b_v, ident, q_scratch, k_scratch, v_scratch)
    attend_phase(nc, q_scratch, k_scratch, v_scratch, o_scratch, ident, mask)
    finish_phase(nc, x, o_scratch, w_o, b_o, ident, ffn_in, ffn_probe, ffn_mix, own, rank, center, slope, out)


def kernel(L0_attn_x, L0_attn_wq, L0_attn_bq, L0_attn_wk, L0_attn_bk, L0_attn_wv, L0_attn_bv, L0_attn_wo, L0_attn_bo,
           L0_ffn_select_weight, L0_ffn_select_mean_diff, L0_ffn_imp_center, L0_ffn_imp_slope, L0_ffn_lora_update,
           L0_ffn_lora_degen, L0_ffn_bias_w, L0_ffn_debias_w):
    import ml_dtypes
    import numpy as np
    import concourse.bacc as bacc
    from concourse.bass_utils import run_bass_kernel_spmd

    a = np.asarray
    by_column = lambda w: a(w).transpose(1, 0, 2).reshape(D, -1)
    expert = np.concatenate([np.repeat(np.arange(N_EXP), N_SEL), N_EXP + np.repeat(np.arange(N_EXP), N_LOW),
                             np.arange(N_EXP)])
    arrays = {
        "x": a(L0_attn_x).reshape(B * S, D),
        "w_qkv": np.stack([a(w).T for w in (L0_attn_wq, L0_attn_wk, L0_attn_wv)]),
        "b_cols": np.concatenate([a(L0_attn_bq).reshape(KT, P), a(L0_attn_bk).reshape(KT, P)]).T,
        "b_v": a(L0_attn_bv),
        "w_o": a(L0_attn_wo).T,
        "b_o": a(L0_attn_bo),
        "ffn_in": np.concatenate([by_column(L0_ffn_select_weight), by_column(L0_ffn_lora_update),
                                  a(L0_ffn_select_mean_diff).T], axis=1),
        "ffn_probe": np.concatenate([a(L0_ffn_select_mean_diff).T, a(L0_ffn_debias_w).T], axis=1),
        "ffn_mix": np.concatenate([a(L0_ffn_lora_degen).transpose(0, 2, 1).reshape(-1, D), a(L0_ffn_bias_w)]),
        "center": a(L0_ffn_imp_center),
        "slope": a(L0_ffn_imp_slope),
        "ident": np.eye(P, dtype=np.float32),
        "mask": np.where(np.arange(P)[None, :] > np.arange(P)[:, None], -1e30, 0.0).astype(ml_dtypes.bfloat16),
        "own": (np.arange(2 * N_EXP)[:, None] == expert[None, :]).astype(np.float32),
        "rank": np.broadcast_to(np.arange(N_EXP, 0, -1, dtype=np.float32), (P, N_EXP)),
    }
    nc = bacc.Bacc("TRN2", target_bir_lowering=False, num_devices=1)
    given, aps = {}, []
    for name, array in arrays.items():
        array = np.ascontiguousarray(array)
        given[f"in_{name}"] = array
        aps.append(nc.dram_tensor(f"in_{name}", array.shape, mybir.dt.from_np(array.dtype), kind="ExternalInput").ap())
    aps.append(nc.dram_tensor("out", (B * S, D), F32, kind="ExternalOutput").ap())
    attention_ffn(nc, *aps)
    result = run_bass_kernel_spmd(nc, [given], core_ids=[0])
    return result.results[0]["out"].reshape(B, S, D)
```

```python
import math
from contextlib import ExitStack

import concourse.bass as bass
from concourse import mybir

ALU = mybir.AluOpType
ACT = mybir.ActivationFunctionType
F32 = mybir.dt.float32
F16 = mybir.dt.float16
BF16 = mybir.dt.bfloat16
AX_X = mybir.AxisListType.X

P = 128
B, S, D, H = 2, 2048, 1024, 16
HD = D // H
BH = B * H
KT = D // P
EPS = 1e-5
TOK = 512
SUB = TOK // P
NC = S // TOK
QT = S // P
N_EXP, N_SEL, N_LOW = 8, 8, 8
FF = N_EXP * N_SEL + N_EXP * N_LOW + N_EXP
LOWS = N_EXP * N_LOW
BIAS_HI, BIAS_LO = LOWS, LOWS + 32

X_SCALE, W_SCALE, QKV_SCALE, P_SCALE = 2.0 ** 4, 2.0 ** 8, 2.0 ** 3, 2.0 ** 8
LOG_P_SCALE = math.log(P_SCALE)
MAX_SCALE = 2.0 ** 5
PROJ_UNSCALE = QKV_SCALE / (X_SCALE * W_SCALE)
SOFTMAX_SCALE = HD ** -0.5 / QKV_SCALE ** 2
OUT_UNSCALE = 1.0 / (QKV_SCALE * W_SCALE)
FFN_SCALE = 2.0 ** 12
DOTS_UNSCALE = 1.0 / (X_SCALE * FFN_SCALE)


def project_phase(nc, x, w_qkv, b_cols, b_v, ident_in, q_scratch, k_scratch, v_scratch):
    with ExitStack() as ctx:
        sb = lambda name, shape, dt: ctx.enter_context(nc.sbuf_tensor(name, shape, dt))
        psum = lambda name, shape: ctx.enter_context(nc.psum_tensor(name, shape, F32))
        sem = lambda name: ctx.enter_context(nc.semaphore(name))
        NT = B * NC
        N_QK = 2 * D // P
        N_V = SUB * D // 512
        WRING = 3
        QK_BANKS = 4

        ident = sb("ident_a", [P, P], F32)
        bias_cols = sb("bias_cols", [P, N_QK], F32)
        bias_scaled = sb("bias_scaled", [P, N_QK], F32)
        bv_row = sb("bv_row", [P, D], F32)
        w_raw = sb("w_raw", [P, WRING, D], F32)
        w_hi = sb("w_hi", [P, 3, KT, D], F16)
        w_lo = sb("w_lo", [P, 3, KT, D], F16)
        x_in = sb("x_in", [P, SUB, D], F32)
        stats = sb("stats_a", [P, SUB, 2, 6], F32)
        moments = sb("moments_a", [P, SUB, 2], F32)
        var_eps = sb("var_eps_a", [P, SUB], F32)
        rstd = sb("rstd_a", [P, SUB], F32)
        eps = sb("eps_a", [P, SUB], F32)
        minus_half = sb("minus_half_a", [P, SUB], F32)
        x_norm = sb("x_norm", [P, SUB, D], F32)
        xt_hi = sb("xt_hi", [P, 2, KT, TOK], F16)
        xt_lo = sb("xt_lo", [P, 2, KT, TOK], F16)
        qk_full = sb("qk_full", [P, 4, TOK], F32)
        qk_split = sb("qk_split", [P, 4, 2, TOK], F16)
        v_full = sb("v_full", [P, 2, 512], F32)
        v_split = sb("v_split", [P, 2, H, 2, HD], F16)

        tr_ps = [psum(f"tr_ps{i}", [P, TOK]) for i in range(2)]
        qk_ps = [psum(f"qk_ps{i}", [P, TOK]) for i in range(QK_BANKS)]
        v_ps = [psum(f"v_ps{i}", [P, 512]) for i in range(2)]

        consts_loaded = sem("consts_loaded_a")
        set_done = sem("set_done_a")
        consts_scaled = sem("consts_scaled_a")
        w_loaded = [sem(f"w_loaded{i}") for i in range(WRING)]
        w_hi_done = sem("w_hi_done")
        w_lo_done = sem("w_lo_done")
        x_loaded = [sem(f"x_loaded_a{i}") for i in range(SUB)]
        stats_done = sem("stats_done_a")
        moments_done = sem("moments_done_a")
        var_done = sem("var_done_a")
        rstd_done = sem("rstd_done_a")
        x_norm_done = sem("x_norm_done")
        tr_done = sem("tr_done")
        xt_hi_done = sem("xt_hi_done")
        xt_lo_done = sem("xt_lo_done")
        qk_ps_done = sem("qk_ps_done")
        qk_full_done = sem("qk_full_done")
        qk_hi_done = sem("qk_hi_done")
        qk_lo_done = sem("qk_lo_done")
        qk_stored = [sem(f"qk_stored{i}") for i in range(4)]
        v_ps_done = sem("v_ps_done")
        v_full_done = sem("v_full_done")
        v_hi_done = sem("v_hi_done")
        v_lo_done = sem("v_lo_done")
        v_stored = [sem(f"v_stored{i}") for i in range(2)]

        x_view = x.rearrange("(b c s p) d -> b c p s d", b=B, c=NC, s=SUB)
        w_view = w_qkv.rearrange("m (k p) o -> m k p o", p=P)
        q_view = q_scratch.rearrange("c (b g h) f l n -> c b g (h f) l n", b=B, h=2)
        k_view = k_scratch.rearrange("c (b g h) f l n -> c b g (h f) l n", b=B, h=2)
        v_view = v_scratch.rearrange("(b h) p (c s) e -> b c s p h e", b=B, s=SUB)

        def tiles(eng, step):
            step(0, 0, 0, True, False)
            with eng.Fori(0, NC - 1) as i:
                step(2 * i + 1, i, 1, False, False)
                step(2 * i + 2, i + 1, 0, False, False)
            step(NT - 1, NC - 1, 1, False, True)

        block = ctx.enter_context(nc.Block())

        @block.sync
        def _(sp):
            def load_tokens(view):
                for s in range(SUB):
                    sp.dma_start(x_in[:, s, :], view[:, s, :]).then_inc(x_loaded[s], 16)

            load_tokens(x_view[0, 0])
            sp.dma_start(ident[:], ident_in).then_inc(consts_loaded, 16)
            sp.dma_start(bias_cols[:], b_cols).then_inc(consts_loaded, 16)
            sp.dma_start(bv_row[:], b_v.partition_broadcast(P)).then_inc(consts_loaded, 16)

            def load_weight(n):
                if n >= WRING:
                    sp.wait_ge(w_lo_done, n - WRING + 1)
                sp.dma_start(w_raw[:, n % WRING, :], w_view[n // KT, n % KT]).then_inc(w_loaded[n % WRING], 16)

            def step(n, c, b, first, last):
                if first:
                    for k in range(KT):
                        load_weight(k)
                if not last:
                    sp.wait_ge(x_norm_done, SUB * n + SUB)
                    load_tokens(x_view[1, c] if b == 0 else x_view[0, c + 1])
                if first:
                    for k in range(WRING):
                        load_weight(KT + k)
                for j in range(N_QK):
                    if first and KT + j + WRING < 3 * KT:
                        load_weight(KT + j + WRING)
                    sp.wait_ge(qk_lo_done, N_QK * n + j + 1)
                    view = q_view if j < KT else k_view
                    sp.dma_start(view[c, b, j % KT], qk_split[:, j % 4]).then_inc(qk_stored[j % 4], 16)
                for s in range(SUB):
                    sp.wait_ge(v_lo_done, N_V * n + 2 * s + 2)
                    sp.dma_start(v_view[b, c, s], v_split[:, s % 2].rearrange("p h l f -> p h (l f)")).then_inc(
                        v_stored[s % 2], 16)
            tiles(sp, step)
            for i in range(4):
                sp.wait_ge(qk_stored[i], 16 * (NT * N_QK // 4 + 1))
            for i in range(2):
                sp.wait_ge(v_stored[i], 16 * (NT * SUB // 2 + 1))

        @block.gpsimd
        def _(pool):
            nc.gpsimd.memset(eps[:], EPS).then_inc(set_done, 1)
            nc.gpsimd.memset(minus_half[:], -0.5).then_inc(set_done, 1)
            pool.wait_ge(set_done, 2)
            for i in range(4):
                pool.sem_inc(qk_stored[i], 16)
            for i in range(2):
                pool.sem_inc(v_stored[i], 16)

            def norm_scale(n):
                pool.wait_ge(moments_done, n + 1)
                nc.gpsimd.tensor_tensor(var_eps[:], moments[:, :, 1], eps[:], ALU.add).then_inc(var_done, 1)
                pool.wait_ge(var_done, n + 1)
                nc.gpsimd.tensor_tensor(rstd[:], var_eps[:], minus_half[:], ALU.pow).then_inc(rstd_done, 1)

            def step(n, c, b, first, last):
                if first:
                    norm_scale(0)
                if not last:
                    norm_scale(n + 1)
            tiles(pool, step)

        @block.vector
        def _(dve):
            def norm_stats(n):
                for s in range(SUB):
                    dve.wait_ge(x_loaded[s], 16 * n + 16)
                    for h in range(2):
                        last = nc.vector.bn_stats(stats[:, s, h, :], x_in[:, s, h * 512:(h + 1) * 512])
                last.then_inc(stats_done, 1)
                dve.wait_ge(stats_done, 1)
                dve.sem_clear(stats_done)
                for s in range(SUB):
                    last = nc.vector.bn_aggr(moments[:, s, :], stats[:, s].rearrange("p h e -> p (h e)"))
                last.then_inc(moments_done, 1)

            def norm_apply(n):
                dve.wait_ge(rstd_done, n + 1)
                if not isinstance(n, int) or n > 0:
                    dve.wait_ge(tr_done, KT * n)
                for s in range(SUB):
                    nc.vector.tensor_scalar(x_norm[:, s, :], x_in[:, s, :], moments[:, s, 0:1], rstd[:, s:s + 1],
                                            ALU.subtract, ALU.mult).then_inc(x_norm_done, 1)

            def xt_low(n, b, k):
                dve.wait_ge(xt_hi_done, KT * n + k + 1)
                nc.vector.scalar_tensor_tensor(xt_lo[:, b, k, :], tr_ps[k % 2][:], X_SCALE, xt_hi[:, b, k, :],
                                               ALU.mult, ALU.subtract).then_inc(xt_lo_done, 1)

            def split_weight(m, k):
                n = m * KT + k
                dve.wait_ge(w_hi_done, n + 1)
                nc.vector.scalar_tensor_tensor(w_lo[:, m, k, :], w_raw[:, n % WRING, :], W_SCALE, w_hi[:, m, k, :],
                                               ALU.mult, ALU.subtract).then_inc(w_lo_done, 1)

            def step(n, c, b, first, last):
                if first:
                    norm_stats(0)
                    norm_apply(0)
                    for k in range(KT):
                        xt_low(0, 0, k)
                        split_weight(0, k)
                    dve.wait_ge(consts_loaded, 48)
                    nc.vector.tensor_scalar(bias_scaled[:], bias_cols[:], QKV_SCALE, None, ALU.mult).then_inc(
                        consts_scaled, 1)
                    nc.vector.tensor_scalar(bv_row[:], bv_row[:], QKV_SCALE, None, ALU.mult).then_inc(consts_scaled, 1)
                    dve.wait_ge(consts_scaled, 2)
                for j in range(N_QK):
                    if first:
                        split_weight(1 + j // KT, j % KT)
                    dve.wait_ge(qk_hi_done, N_QK * n + j + 1)
                    nc.vector.tensor_tensor(qk_split[:, j % 4, 1, :], qk_full[:, j % 4, :], qk_split[:, j % 4, 0, :],
                                            ALU.subtract).then_inc(qk_lo_done, 1)
                    if not last:
                        if j == 1:
                            norm_stats(n + 1)
                        if j == 2:
                            norm_apply(n + 1)
                        if j >= KT:
                            xt_low(n + 1, 1 - b, j - KT)
                def v_low(j):
                    dve.wait_ge(v_hi_done, N_V * n + j + 1)
                    s, half = j // 2, j % 2
                    heads = slice(half * H // 2, (half + 1) * H // 2)
                    nc.vector.tensor_tensor(v_split[:, s % 2, heads, 1, :],
                                            v_full[:, j % 2, :].rearrange("p (h f) -> p h f", f=HD),
                                            v_split[:, s % 2, heads, 0, :], ALU.subtract).then_inc(v_lo_done, 1)
                for j in range(N_V):
                    half = j % 2
                    dve.wait_ge(v_ps_done, N_V * n + j + 1)
                    if not first or j >= 2:
                        dve.wait_ge(v_lo_done, N_V * n + j - 1)
                    nc.vector.scalar_tensor_tensor(v_full[:, j % 2, :], v_ps[j % 2][:], PROJ_UNSCALE,
                                                   bv_row[:, half * 512:(half + 1) * 512],
                                                   ALU.mult, ALU.add).then_inc(v_full_done, 1)
                    if j >= 1:
                        v_low(j - 1)
                v_low(N_V - 1)
            tiles(dve, step)

        @block.scalar
        def _(act):
            def xt_high(n, b, k):
                act.wait_ge(tr_done, KT * n + k + 1)
                nc.scalar.activation(xt_hi[:, b, k, :], tr_ps[k % 2][:], ACT.Copy, scale=X_SCALE).then_inc(
                    xt_hi_done, 1)

            def split_weight(m, k):
                n = m * KT + k
                act.wait_ge(w_loaded[n % WRING], 16 * (n // WRING + 1))
                nc.scalar.activation(w_hi[:, m, k, :], w_raw[:, n % WRING, :], ACT.Copy, scale=W_SCALE).then_inc(
                    w_hi_done, 1)

            def step(n, c, b, first, last):
                if first:
                    for k in range(KT):
                        xt_high(0, 0, k)
                        split_weight(0, k)
                    act.wait_ge(consts_scaled, 2)
                for j in range(N_QK):
                    if first:
                        split_weight(1 + j // KT, j % KT)
                    act.wait_ge(qk_ps_done, N_QK * n + j + 1)
                    if not first or j >= 4:
                        act.wait_ge(qk_lo_done, N_QK * n + j - 3)
                    act.wait_ge(qk_stored[j % 4], 16 * (N_QK // 4 * n + j // 4 + 1))
                    nc.scalar.activation(qk_full[:, j % 4, :], qk_ps[j % 4][:], ACT.Identity,
                                         bias=bias_scaled[:, j:j + 1], scale=PROJ_UNSCALE).then_inc(qk_full_done, 1)
                    nc.scalar.activation(qk_split[:, j % 4, 0, :], qk_ps[j % 4][:], ACT.Identity,
                                         bias=bias_scaled[:, j:j + 1], scale=PROJ_UNSCALE).then_inc(qk_hi_done, 1)
                    if not last and j >= KT:
                        xt_high(n + 1, 1 - b, j - KT)
                for j in range(N_V):
                    s, half = j // 2, j % 2
                    heads = slice(half * H // 2, (half + 1) * H // 2)
                    act.wait_ge(v_full_done, N_V * n + j + 1)
                    if half == 0:
                        act.wait_ge(v_stored[s % 2], 16 * (SUB // 2 * n + s // 2 + 1))
                    nc.scalar.activation(v_split[:, s % 2, heads, 0, :],
                                         v_full[:, j % 2, :].rearrange("p (h f) -> p h f", f=HD),
                                         ACT.Copy).then_inc(v_hi_done, 1)
            tiles(act, step)

        @block.tensor
        def _(pe):
            def transposes(n, k):
                if not isinstance(n, int) or n > 0 or k >= 2:
                    pe.wait_ge(xt_lo_done, KT * n + k - 1)
                for s in range(SUB):
                    last = nc.tensor.transpose(tr_ps[k % 2][:, s * P:(s + 1) * P], x_norm[:, s, k * P:(k + 1) * P],
                                               ident[:])
                last.then_inc(tr_done, 1)

            def qk_products(j, b, k):
                m, cols, bank = j // KT, slice((j % KT) * P, (j % KT + 1) * P), qk_ps[j % QK_BANKS]
                nc.tensor.matmul(bank[:], w_lo[:, m, k, cols], xt_hi[:, b, k, :], start=(k == 0), stop=False)
                nc.tensor.matmul(bank[:], w_hi[:, m, k, cols], xt_lo[:, b, k, :], start=False, stop=False)
                return nc.tensor.matmul(bank[:], w_hi[:, m, k, cols], xt_hi[:, b, k, :], start=False,
                                        stop=(k == KT - 1))

            def step(n, c, b, first, last):
                if first:
                    pe.wait_ge(consts_loaded, 48)
                    pe.wait_ge(x_norm_done, SUB)
                    transposes(0, 0)
                    transposes(0, 1)
                    for k in range(KT):
                        pe.wait_ge(xt_lo_done, k + 1)
                        pe.wait_ge(w_lo_done, k + 1)
                        for j in range(QK_BANKS):
                            mm = qk_products(j, b, k)
                            if k == KT - 1:
                                mm.then_inc(qk_ps_done, 1)
                        if k + 2 < KT:
                            transposes(0, k + 2)
                else:
                    pe.wait_ge(xt_lo_done, KT * n + KT)
                for j in range(QK_BANKS if first else 0, N_QK):
                    if first and j % KT == 0:
                        pe.wait_ge(w_lo_done, KT * (j // KT + 1))
                    pe.wait_ge(qk_hi_done, N_QK * n + j - QK_BANKS + 1)
                    for k in range(KT):
                        mm = qk_products(j, b, k)
                    mm.then_inc(qk_ps_done, 1)
                    if not last and j >= KT:
                        if j == KT:
                            pe.wait_ge(x_norm_done, SUB * n + 2 * SUB)
                        transposes(n + 1, j - KT)
                if first:
                    pe.wait_ge(w_lo_done, 3 * KT)
                for j in range(N_V):
                    toks, cols = slice(j // 2 * P, (j // 2 + 1) * P), slice(j % 2 * 512, (j % 2 + 1) * 512)
                    if not first or j >= 2:
                        pe.wait_ge(v_full_done, N_V * n + j - 1)
                    for k in range(KT):
                        nc.tensor.matmul(v_ps[j % 2][:], xt_lo[:, b, k, toks], w_hi[:, 2, k, cols], start=(k == 0),
                                         stop=False)
                        nc.tensor.matmul(v_ps[j % 2][:], xt_hi[:, b, k, toks], w_lo[:, 2, k, cols], start=False,
                                         stop=False)
                        mm = nc.tensor.matmul(v_ps[j % 2][:], xt_hi[:, b, k, toks], w_hi[:, 2, k, cols], start=False,
                                              stop=(k == KT - 1))
                    mm.then_inc(v_ps_done, 1)
            tiles(pe, step)


GQ = 4
N_GROUPS = QT // GQ
BANK = 512
BANKS = []
for g in range(N_GROUPS):
    for kb in range(GQ * g + 1):
        BANKS.append([(g, kb, GQ * g, 0)])
    BANKS.append([(g, GQ * g + 1, GQ * g + 1, 0), (g, GQ * g + 3, GQ * g + 3, 3 * P)])
    BANKS.append([(g, GQ * g + 2, GQ * g + 2, (1 - len(BANKS) % 2) * 2 * P)])
NB = len(BANKS)
NU = NB // 2
FIRST_BANK = [min(b for b in range(NB) if BANKS[b][0][0] == g) for g in range(N_GROUPS)]
LAST_BANK = [max(b for b in range(NB) if BANKS[b][0][0] == g) for g in range(N_GROUPS)]
UNIT_COLS = [(BANKS[2 * u][0][3] if len(BANKS[2 * u]) == 1 else 0,
              BANK + sum((GQ * g + GQ - t) * P for g, _, t, _ in BANKS[2 * u + 1])) for u in range(NU)]
CHUNKS = [(t, k, min(GQ, t + 1 - k)) for t in range(QT) for k in range(0, t + 1, GQ)]
N_CHUNKS = len(CHUNKS)
LAST_CHUNK = [max(i for i in range(N_CHUNKS) if CHUNKS[i][0] // GQ == g) for g in range(N_GROUPS)]
ROW_LAG = 4
ITEMS = []
for i in range(N_CHUNKS + ROW_LAG):
    ITEMS += [("chunk", i)] if i < N_CHUNKS else []
    ITEMS += [("row", g) for g in range(N_GROUPS) if LAST_CHUNK[g] + ROW_LAG == i]


def beside_units(items):
    weight = [4 if kind == "row" else CHUNKS[i][2] + 0.5 for kind, i, _ in items[:-1]]
    done = [sum(weight[:i + 1]) / sum(weight) for i in range(len(weight))]
    return [(math.ceil(d * (NU - 1)) - 1, *item) for d, item in zip(done, items)] + [(NU - 1, *items[-1])]


ITEMS_BEFORE = ITEMS[:ITEMS.index(("row", 1)) + 1]
BESIDE_FIRST = beside_units([(*item, 0) for item in ITEMS[len(ITEMS_BEFORE):]] + [(*item, 1) for item in ITEMS])
BESIDE = beside_units([(*item, 1) for item in ITEMS])
MAX_BANKS = 3
CUT = [lo + (hi - lo) * 6 // 8 // P * P for lo, hi in UNIT_COLS]
MAX_LOADS, REST_LOADS = 4, 3
SLOTS = 3
assert all(FIRST_BANK[i] // 2 > u for u, kind, i, n in BESIDE_FIRST if kind == "row" and n == 0)
WO_RING = 4
P_SLOTS = 6
LAG = 4
LOW_LAG = 3
OUTPUT_UNIT = [(b + 1) // 2 + LAG - 1 for b in LAST_BANK]


def attend_phase(nc, q_scratch, k_scratch, v_scratch, o_scratch, mask_in, fin):
    with ExitStack() as ctx:
        sb = lambda name, shape, dt: ctx.enter_context(nc.sbuf_tensor(name, shape, dt))
        psum = lambda name, shape: ctx.enter_context(nc.psum_tensor(name, shape, F32))
        sem = lambda name: ctx.enter_context(nc.semaphore(name))
        slots = range(SLOTS)

        ident_bf = sb("ident_bf", [P, P], BF16)
        ident_f16 = sb("ident_f16", [P, P], F16)
        mask = sb("mask", [P, P], BF16)
        exp_bias = sb("exp_bias", [P, 1], F32)
        q_hi2 = [sb(f"q_hi2_{i}", [P, S], F16) for i in slots]
        k_both = [sb(f"k_both_{i}", [P, S], F16) for i in slots]
        q_lo_max = [sb(f"q_lo_max_{i}", [P, S], F16) for i in slots]
        k_hi_one = [sb(f"k_hi_one_{i}", [P, S], F16) for i in slots]
        v_one = [sb(f"v_one_{i}", [P, QT, 2, HD + 2], F16) for i in slots]
        probs = [sb(f"probs{i}", [P, 2 * BANK], F32) for i in range(P_SLOTS)]
        p_hi = [sb(f"p_hi{i}", [P, 2 * BANK], F16) for i in range(P_SLOTS)]
        p_lo = [sb(f"p_lo{i}", [P, 2 * BANK], F16) for i in range(P_SLOTS)]
        chunk_max = sb("chunk_max", [P, N_GROUPS, GQ, N_GROUPS], F32)
        group_max = sb("group_max", [P, N_GROUPS, GQ], F32)
        max_cols = sb("max_cols", [P, HD + GQ], F16)
        inv_sum = sb("inv_sum", [P, GQ], F32)
        o_head = [sb(f"o_head{i}", [P, QT, HD], F32) for i in slots]

        st_ps = [psum(f"st_ps{i}", [P, 2 * BANK]) for i in range(2)]
        max_ps = [psum(f"max_ps{i}", [P, BANK]) for i in range(MAX_BANKS)]
        o_ps = psum("o_ps", [P, GQ, P])

        consts_loaded = sem("consts_loaded_b")
        max_loaded = [sem(f"max_loaded{i}") for i in slots]
        rest_loaded = [sem(f"rest_loaded{i}") for i in slots]
        set_done = sem("set_done_b")
        rows_set = [sem(f"rows_set{i}") for i in slots]
        fin_loaded = sem("fin_loaded")
        tile0_loaded = sem("tile0_loaded")
        w_loaded = [sem(f"wo_loaded{i}") for i in range(WO_RING)]
        ffn_hi_done = sem("ffn_hi_done")
        w_hi_done = sem("wo_hi_done")
        w_lo_done = sem("wo_lo_done")
        chunk_ps_done = sem("chunk_ps_done")
        chunk_done = sem("chunk_done")
        group_max_done = sem("group_max_done")
        max_cols_done = sem("max_cols_done")
        row_ps_done = sem("row_ps_done")
        row_done = sem("row_done")
        st_done = sem("st_done")
        exp_done = sem("exp_done")
        hi_done = sem("hi_done")
        lo0_done = sem("lo0_done")
        lo1_done = sem("lo1_done")
        pv_done = sem("pv_done")
        inv_done = sem("inv_done")
        o_done = sem("o_done")
        o_stored = [sem(f"o_stored{i}") for i in slots]

        def heads(eng, head):
            head(0, 0, 0, True, False)
            with eng.Fori(0, (BH - 2) // SLOTS) as i:
                head(3 * i + 1, 1, i, False, False)
                head(3 * i + 2, 2, i, False, False)
                head(3 * i + 3, 0, i + 1, False, False)
            head(BH - 1, 1, BH // SLOTS, False, True)

        def items(u, first, last):
            return [] if last else [item for unit, *item in (BESIDE_FIRST if first else BESIDE) if unit == u]

        def max_bank(kind, i, slot):
            return max_ps[(len(ITEMS) * slot + ITEMS.index((kind, i))) % MAX_BANKS]

        SETS, ROWS = 5, 4
        block = ctx.enter_context(nc.Block())

        @block.sync
        def _(sp):
            sp.dma_start(fin["ident"][:], fin["ident_in"]).then_inc(consts_loaded, 16)
            sp.dma_start(mask[:], mask_in).then_inc(consts_loaded, 16)

            def load(n, slot):
                halves = (slice(0, HD), slice(HD, P))
                by_feature = lambda tile, rows: tile[slot][rows, :].rearrange("f (c n) -> f c n", c=NC)
                q_part = lambda part: q_scratch[:, n, :, part, :].rearrange("c f n -> f c n")
                k_part = lambda part: k_scratch[:, n, :, part, :].rearrange("c f n -> f c n")
                for part, rows in enumerate(halves):
                    sp.dma_start(by_feature(q_hi2, rows), q_part(0)).then_inc(max_loaded[slot], 16)
                    sp.dma_start(by_feature(k_both, rows), k_part(part)).then_inc(max_loaded[slot], 16)
                sp.dma_start(by_feature(q_lo_max, halves[0]), q_part(1)).then_inc(rest_loaded[slot], 16)
                sp.dma_start(by_feature(k_hi_one, halves[0]), k_part(0)).then_inc(rest_loaded[slot], 16)
                sp.dma_start(v_one[slot][:, :, :, 0:HD], v_scratch[n].rearrange("p t (l f) -> p t l f", l=2)).then_inc(
                    rest_loaded[slot], 16)

            def store(n, slot):
                sp.wait_ge(o_done, N_GROUPS * n + N_GROUPS)
                sp.dma_start(o_scratch[n], o_head[slot][:].rearrange("p t f -> p (t f)")).then_inc(o_stored[slot], 16)

            for n in range(SLOTS):
                load(n, n)
            for tile, source in fin["loads"]:
                sp.dma_start(tile, source).then_inc(fin_loaded, 16)
            for k in range(WO_RING):
                sp.dma_start(fin["w_raw"][:, k, :], fin["w_view"][k]).then_inc(w_loaded[k], 16)
            store(0, 0)
            load(SLOTS, 0)
            with sp.Fori(0, (BH - 2) // SLOTS - 1) as i:
                for r in range(SLOTS):
                    store(3 * i + 1 + r, (1 + r) % SLOTS)
                    load(3 * i + 1 + r + SLOTS, (1 + r) % SLOTS)
            for n in range(BH - 4, BH - 1):
                store(n, n % SLOTS)
                if n + SLOTS < BH:
                    load(n + SLOTS, n % SLOTS)
            for slot in slots:
                sp.wait_ge(o_stored[slot], 16 * (len(range(slot, H, SLOTS)) + 1))
            sp.dma_start(fin["o_in0"][:].rearrange("p (h f) -> p h f", f=HD), fin["o_view"][0, 0]).then_inc(
                tile0_loaded, 16)
            for k in range(WO_RING, KT):
                sp.wait_ge(w_lo_done, k - WO_RING + 1)
                sp.dma_start(fin["w_raw"][:, k % WO_RING, :], fin["w_view"][k]).then_inc(w_loaded[k % WO_RING], 16)
            store(BH - 1, (BH - 1) % SLOTS)
            sp.wait_ge(tile0_loaded, 16)
            for slot in slots:
                sp.wait_ge(o_stored[slot], 16 * (len(range(slot, BH, SLOTS)) + 1))

        @block.tensor
        def _(pe):
            def bank_free(kind, i, n):
                at = ITEMS.index((kind, i)) - MAX_BANKS
                old, j = ITEMS[at]
                m = n if at >= 0 else n - 1
                if isinstance(m, int) and m < 0:
                    return
                if old == "chunk":
                    pe.wait_ge(chunk_done, N_CHUNKS * m + j + 1)
                else:
                    pe.wait_ge(row_done, N_GROUPS * m + j + 1)

            def chunk_scores(i, n, slot, use):
                t, k0, blocks = CHUNKS[i]
                if i == 0:
                    pe.wait_ge(max_loaded[slot], 16 * MAX_LOADS * use + 16 * MAX_LOADS)
                bank = max_bank("chunk", i, slot)
                bank_free("chunk", i, n)
                w = blocks * P
                diagonal = k0 + blocks == t + 1
                mm = nc.tensor.matmul(bank[:, 0:w], q_hi2[slot][:, t * P:(t + 1) * P],
                                      k_both[slot][:, k0 * P:k0 * P + w], start=True, stop=not diagonal)
                if diagonal:
                    mm = nc.tensor.matmul(bank[:, w - P:w], ident_bf[:], mask[:], start=False, stop=True)
                mm.then_inc(chunk_ps_done, 1)

            def max_row(g, n, slot):
                pe.wait_ge(max_cols_done, N_GROUPS * n + g + 1)
                bank_free("row", g, n)
                nc.tensor.matmul(max_bank("row", g, slot)[0:HD + GQ, 0:P], max_cols[:], ident_f16[:], start=True,
                                 stop=True).then_inc(row_ps_done, 1)

            def scores(u, n, slot, use):
                if u == 0:
                    pe.wait_ge(rows_set[slot], ROWS)
                    pe.wait_ge(rest_loaded[slot], 16 * REST_LOADS * use + 16 * REST_LOADS)
                if not isinstance(n, int) or NU * n + u >= 2:
                    pe.wait_ge(exp_done, NU * n + u - 1)
                for b in (2 * u, 2 * u + 1):
                    if b in FIRST_BANK:
                        pe.wait_ge(row_done, N_GROUPS * n + BANKS[b][0][0] + 1)
                    for g, kb, t, at in BANKS[b]:
                        w = (GQ * g + GQ - t) * P
                        at += b % 2 * BANK
                        keys, queries = slice(kb * P, (kb + 1) * P), slice(t * P, t * P + w)
                        dst = st_ps[u % 2][:, at:at + w]
                        nc.tensor.matmul(dst, k_hi_one[slot][:, keys], q_lo_max[slot][:, queries], start=True,
                                         stop=False)
                        mm = nc.tensor.matmul(dst, k_both[slot][:, keys], q_hi2[slot][:, queries], start=False,
                                              stop=(kb != t))
                        if kb == t:
                            mm = nc.tensor.matmul(dst[:, 0:P], mask[:], ident_bf[:], start=False, stop=True)
                mm.then_inc(st_done, 1)

            def times_v(b, n, slot):
                u = b // 2
                pe.wait_ge(lo0_done, NU * n + u + 1)
                if b % 2 == 1 or CUT[u] < BANK:
                    pe.wait_ge(lo1_done, NU * n + u + 1)
                first = b in FIRST_BANK
                if first and (not isinstance(n, int) or N_GROUPS * n + BANKS[b][0][0] > 0):
                    pe.wait_ge(o_done, N_GROUPS * n + BANKS[b][0][0])
                for g, kb, t0, at in BANKS[b]:
                    at += b % 2 * BANK
                    for t in range(t0, GQ * g + GQ):
                        rows = slice(at + (t - t0) * P, at + (t - t0 + 1) * P)
                        hi, lo = p_hi[u % P_SLOTS][:, rows], p_lo[u % P_SLOTS][:, rows]
                        v_hi, v_lo = (v_one[slot][:, kb, part, 0:HD + 1] for part in range(2))
                        dst = o_ps[:, t % GQ, 0:HD + 1]
                        nc.tensor.matmul(dst, lo, v_hi, start=first, stop=False)
                        first = False
                        nc.tensor.matmul(dst, hi, v_lo, start=False, stop=False)
                        mm = nc.tensor.matmul(dst, hi, v_hi, start=False,
                                              stop=(b == LAST_BANK[g] and t == GQ * g + GQ - 1))
                mm.then_inc(pv_done, 1)

            def maxima(kind, i, n, slot, use):
                if kind == "chunk":
                    chunk_scores(i, n, slot, use)
                else:
                    max_row(i, n, slot)

            def head(n, slot, use, first, last):
                after, before = (slot + 1) % SLOTS, (slot + 2) % SLOTS
                for u in range(NU):
                    ends = 2 * (u - LAG) in LAST_BANK
                    if not ends:
                        scores(u, n, slot, use)
                    if u >= LAG:
                        times_v(2 * (u - LAG), n, slot)
                    elif not first:
                        times_v(2 * (u - LAG) + NB, n - 1, before)
                    if ends:
                        scores(u, n, slot, use)
                    some = [] if u == NU - 1 else items(u, first, last)
                    for kind, i, ahead in some:
                        if ahead:
                            maxima(kind, i, n + 1, after, use + (slot == SLOTS - 1))
                        else:
                            maxima(kind, i, n, slot, use)
                    if u >= LAG:
                        times_v(2 * (u - LAG) + 1, n, slot)
                    elif not first:
                        times_v(2 * (u - LAG) + 1 + NB, n - 1, before)
                    if u == NU - 1 and not last:
                        max_row(N_GROUPS - 1, n + 1, after)
                if last:
                    for b in range(NB - 2 * LAG, NB):
                        times_v(b, n, slot)

            pe.wait_ge(consts_loaded, 32)
            pe.wait_ge(set_done, SETS)
            for kind, i in ITEMS_BEFORE:
                maxima(kind, i, 0, 0, 0)
            heads(pe, head)

        @block.vector
        def _(dve):
            nc.vector.memset(fin["mix_w2"][:], 0.0).then_inc(set_done, 1)
            nc.vector.memset(max_cols[:], 0.0).then_inc(set_done, 1)
            nc.vector.memset(exp_bias[:], LOG_P_SCALE).then_inc(set_done, 1)
            for i in slots:
                nc.vector.memset(v_one[i][:, :, 0, HD:HD + 1], 1.0).then_inc(rows_set[i], 1)
                nc.vector.memset(v_one[i][:, :, 1, HD:HD + 1], 0.0).then_inc(rows_set[i], 1)
            dve.wait_ge(consts_loaded, 32)
            nc.vector.tensor_copy(ident_bf[:], fin["ident"][:]).then_inc(set_done, 1)
            nc.vector.tensor_copy(ident_f16[:], fin["ident"][:]).then_inc(set_done, 1)
            dve.wait_ge(set_done, SETS)

            def maxima(i, n, slot):
                t, k0, blocks = CHUNKS[i]
                dve.wait_ge(chunk_ps_done, N_CHUNKS * n + i + 1)
                nc.vector.tensor_reduce(chunk_max[:, t // GQ, t % GQ, k0 // GQ:k0 // GQ + 1],
                                        max_bank("chunk", i, slot)[:, 0:blocks * P], AX_X, ALU.max).then_inc(
                    chunk_done, 1)
                g = t // GQ
                if i == LAST_CHUNK[g]:
                    dve.wait_ge(chunk_done, N_CHUNKS * n + i + 1)
                    nc.vector.tensor_reduce(group_max[:, g, :], chunk_max[:, g, :, 0:g + 1], AX_X, ALU.max).then_inc(
                        group_max_done, 1)
                    dve.wait_ge(group_max_done, N_GROUPS * n + g + 1)
                    if not isinstance(n, int) or N_GROUPS * n + g > 0:
                        dve.wait_ge(row_ps_done, N_GROUPS * n + g)
                    nc.vector.tensor_scalar(max_cols[:, HD:HD + GQ], group_max[:, g, :], -1.0 / MAX_SCALE, None,
                                            ALU.mult).then_inc(max_cols_done, 1)

            def max_row(g, n, slot):
                dve.wait_ge(row_ps_done, N_GROUPS * n + g + 1)
                rows = slice(HD, HD + GQ)
                nc.vector.tensor_tensor(
                    q_lo_max[slot][rows, g * BANK:(g + 1) * BANK].rearrange("p (b n) -> p b n", b=GQ),
                    max_bank("row", g, slot)[rows, 0:P].unsqueeze(1).broadcast_to([GQ, GQ, P]),
                    fin["ident"][rows, rows].unsqueeze(2).broadcast_to([GQ, GQ, P]), ALU.mult).then_inc(row_done, 1)

            def low_last(u, n):
                cols = slice(CUT[u], UNIT_COLS[u][1])
                dve.wait_ge(hi_done, NU * n + u + 1)
                p = u % P_SLOTS
                nc.vector.tensor_tensor(p_lo[p][:, cols], probs[p][:, cols], p_hi[p][:, cols],
                                        ALU.subtract).then_inc(lo1_done, 1)

            def output(g, n, slot, use):
                dve.wait_ge(pv_done, NB * n + LAST_BANK[g] + 1)
                nc.vector.reciprocal(inv_sum[:], o_ps[:, :, HD]).then_inc(inv_done, 1)
                dve.wait_ge(inv_done, N_GROUPS * n + g + 1)
                if g == 0:
                    dve.wait_ge(o_stored[slot], 16 * use + 16)
                nc.vector.tensor_tensor(o_head[slot][:, GQ * g:GQ * g + GQ, :], o_ps[:, :, 0:HD],
                                        inv_sum[:].unsqueeze(2).broadcast_to([P, GQ, HD]), ALU.mult).then_inc(o_done, 1)

            def split_weight(k, part):
                hi, lo, raw = fin["w_hi"][:, k, :], fin["w_lo"][:, k, :], fin["w_raw"][:, k % WO_RING, :]
                if part == 0:
                    dve.wait_ge(w_loaded[k % WO_RING], 16 * (k // WO_RING + 1))
                    nc.vector.tensor_scalar(hi, raw, W_SCALE, None, ALU.mult).then_inc(w_hi_done, 1)
                else:
                    dve.wait_ge(w_hi_done, k + 1)
                    nc.vector.scalar_tensor_tensor(lo, raw, W_SCALE, hi, ALU.mult, ALU.subtract).then_inc(w_lo_done, 1)

            def split_ffn_weights():
                low, bias_hi, bias_lo = slice(0, LOWS), slice(BIAS_HI, BIAS_HI + N_EXP), slice(BIAS_LO, BIAS_LO + N_EXP)
                dve.wait_ge(fin_loaded, 16 * len(fin["loads"]))
                for to, raw, rows, scale in (("ffn_hi", "ffn_w", slice(0, P), FFN_SCALE),
                                             ("mix_w1", "degen", slice(0, P), W_SCALE),
                                             ("mix_w2", "bias", bias_hi, W_SCALE), ("bias_hi", "bias", bias_lo, W_SCALE)):
                    nc.vector.tensor_scalar(fin[to][rows], fin[raw][rows], scale, None, ALU.mult).then_inc(
                        ffn_hi_done, 1)
                dve.wait_ge(ffn_hi_done, 4)
                for to, raw, hi, rows, scale in (("ffn_lo", "ffn_w", "ffn_hi", slice(0, P), FFN_SCALE),
                                                 ("mix_w2", "degen", "mix_w1", low, W_SCALE),
                                                 ("mix_w2", "bias", "bias_hi", bias_lo, W_SCALE)):
                    nc.vector.scalar_tensor_tensor(fin[to][rows], fin[raw][rows], scale, fin[hi][rows], ALU.mult,
                                                   ALU.subtract)

            def head(n, slot, use, first, last):
                for u in range(NU):
                    for kind, g, ahead in items(u - 1, first, last) if u >= 1 else []:
                        if kind == "row":
                            max_row(g, n + ahead, (slot + ahead) % SLOTS)
                    if u == 0 and not first:
                        max_row(N_GROUPS - 1, n, slot)
                    if u >= LOW_LAG:
                        low_last(u - LOW_LAG, n)
                    elif not first:
                        low_last(u - LOW_LAG + NU, n - 1)
                    some = [(i, ahead) for kind, i, ahead in items(u, first, last) if kind == "chunk"]
                    for i, ahead in some[:-1]:
                        maxima(i, n + ahead, (slot + ahead) % SLOTS)
                    for g in range(N_GROUPS):
                        if OUTPUT_UNIT[g] == u:
                            output(g, n, slot, use)
                        if OUTPUT_UNIT[g] == u + NU and not first:
                            output(g, n - 1, (slot + 2) % SLOTS, use - (slot == 0))
                    for i, ahead in some[-1:]:
                        maxima(i, n + ahead, (slot + ahead) % SLOTS)
                    if last and u < 2 * KT:
                        split_weight(u // 2, u % 2)
                if last:
                    split_ffn_weights()
                    for u in range(NU - LOW_LAG, NU):
                        low_last(u, n)
                    output(N_GROUPS - 1, n, slot, use)

            for slot in slots:
                dve.wait_ge(rows_set[slot], ROWS)
            for kind, i in ITEMS_BEFORE:
                if kind == "chunk":
                    maxima(i, 0, 0)
                else:
                    max_row(i, 0, 0)
            heads(dve, head)

        @block.scalar
        def _(act):
            act.wait_ge(set_done, SETS)

            def exponentials(u, n):
                act.wait_ge(st_done, NU * n + u + 1)
                if not isinstance(n, int) or NU * n + u >= P_SLOTS:
                    act.wait_ge(lo0_done, NU * n + u - P_SLOTS + 1)
                    act.wait_ge(lo1_done, NU * n + u - P_SLOTS + 1)
                cols = slice(*UNIT_COLS[u])
                nc.scalar.activation(probs[u % P_SLOTS][:, cols], st_ps[u % 2][:, cols], ACT.Exp, bias=exp_bias[:],
                                     scale=SOFTMAX_SCALE).then_inc(exp_done, 1)

            def high(u, n):
                act.wait_ge(exp_done, NU * n + u + 1)
                if not isinstance(n, int) or NU * n + u >= P_SLOTS:
                    act.wait_ge(pv_done, NB * n + 2 * (u - P_SLOTS) + 2)
                cols = slice(*UNIT_COLS[u])
                nc.scalar.activation(p_hi[u % P_SLOTS][:, cols], probs[u % P_SLOTS][:, cols], ACT.Copy).then_inc(
                    hi_done, 1)

            def head(n, slot, use, first, last):
                for u in range(NU):
                    exponentials(u, n)
                    if u >= 1:
                        high(u - 1, n)
                    elif not first:
                        high(NU - 1, n - 1)
                if last:
                    high(NU - 1, n)

            heads(act, head)

        @block.gpsimd
        def _(pool):
            for slot in slots:
                pool.sem_inc(o_stored[slot], 16)

            for i in slots:
                nc.gpsimd.memset(q_lo_max[i][HD:P, :], 0.0).then_inc(rows_set[i], 1)
                nc.gpsimd.memset(k_hi_one[i][HD:P, :], MAX_SCALE).then_inc(rows_set[i], 1)

            def low_first(u, n):
                pool.wait_ge(hi_done, NU * n + u + 1)
                cols = slice(UNIT_COLS[u][0], CUT[u])
                p = u % P_SLOTS
                nc.gpsimd.tensor_tensor(p_lo[p][:, cols], probs[p][:, cols], p_hi[p][:, cols],
                                        ALU.subtract).then_inc(lo0_done, 1)

            def head(n, slot, use, first, last):
                for u in range(NU):
                    low_first(u, n)
            heads(pool, head)


def finish_inputs(nc, ctx, x, o_scratch, wo, b_o, ident_in, ffn_in, ffn_probe, ffn_mix, own_in, rank_in, center, slope):
    sb = lambda name, shape, dt: ctx.enter_context(nc.sbuf_tensor(name, shape, dt))
    fin = dict(
        ident=sb("ident_bc", [P, P], F32),
        w_raw=sb("wo_raw", [P, WO_RING, D], F32),
        w_hi=sb("wo_hi", [P, KT, D], F16),
        w_lo=sb("wo_lo", [P, KT, D], F16),
        bo_row=sb("bo_row", [P, D], F32),
        ffn_w=sb("ffn_w", [P, KT, FF], F32),
        ffn_hi=sb("ffn_hi", [P, KT, FF], F16),
        ffn_lo=sb("ffn_lo", [P, KT, FF], F16),
        probe=sb("probe", [P, KT, 2 * N_EXP], F32),
        degen=sb("degen", [P, D], F32),
        bias=sb("bias", [P, D], F32),
        bias_hi=sb("bias_hi", [P, D], F16),
        mix_w1=sb("mix_w1", [P, D], F16),
        mix_w2=sb("mix_w2", [P, D], F16),
        own=sb("own", [2 * N_EXP, FF], F32),
        rank=sb("rank", [P, N_EXP], F32),
        center_row=sb("center_row", [P, N_EXP], F32),
        slope_row=sb("slope_row", [P, N_EXP], F32),
        o_in0=sb("o_in0", [P, D], F32),
        x_in0=sb("x_in_c0", [P, D], F32),
        ident_in=ident_in,
        w_view=wo.rearrange("(k p) o -> k p o", p=P),
        x_view=x.rearrange("(b t p) d -> b t p d", b=B, t=QT),
        o_view=o_scratch.rearrange("(b h) p (t f) -> b t p h f", b=B, f=HD))
    fin["loads"] = [(fin["bo_row"][:], b_o.partition_broadcast(P)),
                 (fin["ffn_w"][:], ffn_in.rearrange("(k p) o -> p k o", p=P)),
                 (fin["probe"][:], ffn_probe.rearrange("(k p) o -> p k o", p=P)),
                 (fin["degen"][0:LOWS], ffn_mix[0:LOWS]), (fin["degen"][LOWS:P], ffn_mix[0:LOWS]),
                 (fin["bias"][BIAS_HI:BIAS_HI + N_EXP], ffn_mix[LOWS:]),
                 (fin["bias"][BIAS_LO:BIAS_LO + N_EXP], ffn_mix[LOWS:]),
                 (fin["own"][:], own_in), (fin["rank"][:], rank_in),
                 (fin["center_row"][:], center.partition_broadcast(P)),
                 (fin["slope_row"][:], slope.partition_broadcast(P)),
                 (fin["x_in0"][:], fin["x_view"][0, 0])]
    return fin


def finish_phase(nc, fin, out):
    with ExitStack() as ctx:
        sb = lambda name, shape, dt: ctx.enter_context(nc.sbuf_tensor(name, shape, dt))
        psum = lambda name, shape: ctx.enter_context(nc.psum_tensor(name, shape, F32))
        sem = lambda name: ctx.enter_context(nc.semaphore(name))
        NT = B * QT
        HALF = 512
        halves = [slice(0, HALF), slice(HALF, D)]
        SEL, LOW, DIF = slice(0, 64), slice(64, 128), slice(128, 136)

        ident, w_hi, w_lo, bo_row = fin["ident"], fin["w_hi"], fin["w_lo"], fin["bo_row"]
        ffn_w, probe, own, rank = fin["ffn_w"], fin["probe"], fin["own"], fin["rank"]
        center_row, slope_row = fin["center_row"], fin["slope_row"]
        ones = sb("ones", [2 * N_EXP, P], F32)
        own_dots = sb("own_dots", [2 * N_EXP, FF], F32)
        offsets = sb("offsets", [P, FF], F32)
        eps = sb("eps_c", [P, 1], F32)
        minus_half = sb("minus_half_c", [P, 1], F32)
        o_in = [fin["o_in0"]] + [sb(f"o_in{i}", [P, D], F32) for i in range(1, 4)]
        x_in = [fin["x_in0"]] + [sb(f"x_in_c{i}", [P, D], F32) for i in range(1, 4)]
        ot_hi = [sb(f"ot_hi{i}", [P, KT, P], F16) for i in range(2)]
        ot_lo = [sb(f"ot_lo{i}", [P, KT, P], F16) for i in range(2)]
        attn = [sb(f"attn{i}", [P, D], F32) for i in range(2)]
        x1 = [sb(f"x1_{i}", [P, D], F32) for i in range(4)]
        x2 = [sb(f"x2_{i}", [P, D], F32) for i in range(4)]
        square = sb("square", [P, D], F32)
        x2_norm2 = [sb(f"x2_norm2_{i}", [P, 1], F32) for i in range(4)]
        x2t_hi = sb("x2t_hi", [P, KT, P], F16)
        x2t_lo = sb("x2t_lo", [P, KT, P], F16)
        mixed = [sb(f"mixed{i}", [P, D], F32) for i in range(2)]
        y = [sb(f"y{i}", [P, D], F32) for i in range(2)]
        result = [sb(f"result{i}", [P, D], F32) for i in range(2)]
        stats = sb("stats_c", [P, 3, 2, 6], F32)
        moments = sb("moments_c", [P, 3, 2], F32)
        var_eps = sb("var_eps_c", [P, 3], F32)
        rstd = sb("rstd_c", [P, 3], F32)
        neg_mean = sb("neg_mean", [P, 3], F32)
        shift = sb("shift", [P, 3], F32)
        dots = sb("dots", [P, 2 * 64], F32)
        dots2 = sb("dots2", [P, 64], F32)
        select = sb("select", [P, 10, N_EXP], F32)
        sel_scale = [sb(f"sel_scale{i}", [P, 1], F32) for i in range(2)]
        sel_out = [sb(f"sel_out{i}", [P, 1], F32) for i in range(2)]
        sel_rest = [sb(f"sel_rest{i}", [P, 1], F32) for i in range(2)]
        top_rank = sb("top_rank", [P, 1], F32)
        ident16 = sb("ident16_c", [P, P], F16)
        low_rank = sb("low_rank", [P, LOWS], F32)
        mix = sb("mix", [P, 2 * P], F16)
        mix_t = sb("mix_t", [P, 2 * P], F16)

        ot_ps = [psum(f"ot_ps{i}", [P, HALF]) for i in range(2)]
        proj_ps = [psum(f"proj_ps{i}", [P, HALF]) for i in range(2)]
        ffn_ps = [psum(f"ffn_ps{i}", [P, HALF]) for i in range(2)]
        dots_ps = psum("dots_ps", [P, FF])
        mix_ps = psum("mix_ps", [P, 2 * P])

        set_done = sem("set_done_c")
        fill_done = sem("fill_done")
        own_ps_done = sem("own_ps_done")
        own_done = sem("own_done")
        offsets_ps_done = sem("offsets_ps_done")
        offsets_done = sem("offsets_done")
        tile_loaded = [sem(f"tile_loaded{i}") for i in range(4)]
        ot_ps_done = sem("ot_ps_done")
        ot_hi_done = sem("ot_hi_done")
        ot_lo_done = sem("ot_lo_done")
        proj_done = sem("proj_done")
        attn_done = sem("attn_done")
        stats_done = sem("stats_done_c")
        moments_done = [sem(f"moments_done_c{i}") for i in range(3)]
        var_done = [sem(f"var_done_c{i}") for i in range(3)]
        rstd_done = [sem(f"rstd_done_c{i}") for i in range(3)]
        shift_done = [sem(f"shift_done{i}") for i in range(3)]
        attn_norm_done = sem("attn_norm_done")
        x1_done = sem("x1_done")
        x2_done = sem("x2_done")
        norm2_done = sem("norm2_done")
        x2t_ps_done = sem("x2t_ps_done")
        x2t_hi_done = sem("x2t_hi_done")
        x2t_lo_done = sem("x2t_lo_done")
        dots_ps_done = sem("dots_ps_done")
        gate_step = sem("gate_step")
        logit_done = sem("logit_done")
        gate_exp_done = sem("gate_exp_done")
        mix_done = sem("mix_done")
        mix_ps_done = sem("mix_ps_done")
        mix_t_done = sem("mix_t_done")
        ffn_done = sem("ffn_done")
        mixed_done = sem("mixed_done")
        y_done = sem("y_done")
        y_norm_done = sem("y_norm_done")
        result_done = sem("result_done")
        stored = [sem(f"stored{i}") for i in range(2)]

        x_view, o_view = fin["x_view"], fin["o_view"]
        out_view = out.rearrange("(b t p) d -> b t p d", b=B, t=QT)

        def tiles(eng, step):
            def fixed(m):
                step(m, m // 2, m % 4, lambda d: 0 <= m + d < NT)
            for m in range(4):
                fixed(m)
            with eng.Fori(1, NT // 4 - 1) as i:
                for v in range(4):
                    step(4 * i + v, 2 * i + v // 2, v, lambda d: True)
            for m in range(NT - 4, NT + 4):
                fixed(m)

        block = ctx.enter_context(nc.Block())

        @block.sync
        def _(sp):
            def load(m, t, r):
                sp.dma_start(o_in[r][:].rearrange("p (h f) -> p h f", f=HD), o_view[r % 2, t]).then_inc(
                    tile_loaded[r], 16)
                sp.dma_start(x_in[r][:], x_view[r % 2, t]).then_inc(tile_loaded[r], 16)

            load(1, 0, 1)
            load(2, 1, 2)

            def step(m, t, r, has):
                if has(3):
                    if has(-1):
                        sp.wait_ge(ot_ps_done, 2 * m)
                        sp.wait_ge(x1_done, m)
                    load(m + 3, t + 1 + r % 2, (r + 3) % 4)
                if has(-4):
                    sp.wait_ge(result_done, m - 3)
                    sp.dma_start(out_view[r % 2, t - 2], result[r % 2][:]).then_inc(stored[r % 2], 16)

            tiles(sp, step)
            for i in range(2):
                sp.wait_ge(stored[i], 16 * (NT // 2 + 1))

        @block.tensor
        def _(pe):
            def transpose_attention(m, r):
                for h in range(2):
                    pe.wait_ge(tile_loaded[r], 8 * (m - r) + 32)
                    if not isinstance(m, int) or m > 0:
                        pe.wait_ge(ot_lo_done, 2 * m - 1 + h)
                    for k in range(4):
                        at = slice((4 * h + k) * P, (4 * h + k + 1) * P)
                        tr = nc.tensor.transpose(ot_ps[h][:, k * P:(k + 1) * P], o_in[r][:, at], ident[:])
                    tr.then_inc(ot_ps_done, 1)

            def project(m, r, h):
                if h == 0:
                    pe.wait_ge(ot_lo_done, 2 * m + 2)
                if not isinstance(m, int) or m > 0:
                    pe.wait_ge(attn_done, 2 * m - 1 + h)
                for k in range(KT):
                    nc.tensor.matmul(proj_ps[h][:], ot_lo[r % 2][:, k, :], w_hi[:, k, halves[h]], start=(k == 0),
                                     stop=False)
                    nc.tensor.matmul(proj_ps[h][:], ot_hi[r % 2][:, k, :], w_lo[:, k, halves[h]], start=False,
                                     stop=False)
                    mm = nc.tensor.matmul(proj_ps[h][:], ot_hi[r % 2][:, k, :], w_hi[:, k, halves[h]], start=False,
                                          stop=(k == KT - 1))
                mm.then_inc(proj_done, 1)

            def transpose_x2(m, r):
                pe.wait_ge(x2_done, m + 1)
                for h in range(2):
                    if h == 0 and (not isinstance(m, int) or m > 1):
                        pe.wait_ge(mixed_done, 2 * m - 2)
                    for k in range(4):
                        at = slice((4 * h + k) * P, (4 * h + k + 1) * P)
                        tr = nc.tensor.transpose(ffn_ps[h][:, k * P:(k + 1) * P], x2[r][:, at], ident[:])
                    tr.then_inc(x2t_ps_done, 1)

            def ffn_dots(m):
                pe.wait_ge(x2t_lo_done, 2 * m + 2)
                if isinstance(m, int) and m == 0:
                    pe.wait_ge(offsets_done, 1)
                if not isinstance(m, int) or m > 0:
                    pe.wait_ge(mix_done, m)
                for k in range(KT):
                    nc.tensor.matmul(dots_ps[:], x2t_lo[:, k, :], fin["ffn_hi"][:, k, :], start=(k == 0), stop=False)
                    nc.tensor.matmul(dots_ps[:], x2t_hi[:, k, :], fin["ffn_lo"][:, k, :], start=False, stop=False)
                    mm = nc.tensor.matmul(dots_ps[:], x2t_hi[:, k, :], fin["ffn_hi"][:, k, :], start=False,
                                          stop=(k == KT - 1))
                mm.then_inc(dots_ps_done, 1)

            def mix_transpose(m):
                pe.wait_ge(mix_done, m + 1)
                for i in range(2):
                    block = slice(i * P, (i + 1) * P)
                    mm = nc.tensor.matmul(mix_ps[:, block], mix[:, block], ident16[:], start=True, stop=True)
                mm.then_inc(mix_ps_done, 1)

            def ffn_mix_out(m):
                pe.wait_ge(mix_t_done, m + 1)
                for h in range(2):
                    nc.tensor.matmul(ffn_ps[h][:], mix_t[:, 0:P], fin["mix_w1"][:, halves[h]], start=True, stop=False)
                    nc.tensor.matmul(ffn_ps[h][:], mix_t[:, P:2 * P], fin["mix_w2"][:, halves[h]], start=False,
                                     stop=True).then_inc(ffn_done, 1)

            def step(m, t, r, has):
                if has(-2):
                    transpose_x2(m - 2, (r + 2) % 4)
                if has(-3):
                    mix_transpose(m - 3)
                if has(0) and not has(-1):
                    project(m, r, 0)
                if has(1):
                    transpose_attention(m + 1, (r + 1) % 4)
                if has(-1) and has(0):
                    project(m, r, 0)
                if has(-2):
                    ffn_dots(m - 2)
                if has(-3):
                    ffn_mix_out(m - 3)
                if has(0):
                    project(m, r, 1)

            transpose_attention(0, 0)
            for k in range(KT):
                mm = nc.tensor.matmul(dots_ps[0:2 * N_EXP, :], probe[:, k, :], ffn_w[:, k, :], start=(k == 0),
                                      stop=(k == KT - 1))
            mm.then_inc(own_ps_done, 1)
            pe.wait_ge(own_done, 1)
            pe.wait_ge(fill_done, 3)
            nc.tensor.matmul(dots_ps[:], ones[:], own_dots[:], start=True, stop=True).then_inc(offsets_ps_done, 1)
            tiles(pe, step)

        @block.vector
        def _(dve):
            nc.vector.memset(ones[:], 1.0).then_inc(fill_done, 1)
            nc.vector.memset(mix[:], 0.0).then_inc(fill_done, 1)
            nc.vector.tensor_copy(ident16[:], ident[:]).then_inc(fill_done, 1)
            dve.wait_ge(fill_done, 3)

            def attention_low(m, r):
                for h in range(2):
                    dve.wait_ge(ot_hi_done, 2 * m + 1 + h)
                    nc.vector.tensor_tensor(ot_lo[r % 2][:, 4 * h:4 * h + 4, :].rearrange("p k n -> p (k n)"), ot_ps[h][:],
                                            ot_hi[r % 2][:, 4 * h:4 * h + 4, :].rearrange("p k n -> p (k n)"),
                                            ALU.subtract).then_inc(ot_lo_done, 1)

            def x2_low(m):
                for h in range(2):
                    dve.wait_ge(x2t_hi_done, 2 * m + 1 + h)
                    hi, lo = (x[:, 4 * h:4 * h + 4, :].rearrange("p k n -> p (k n)") for x in (x2t_hi, x2t_lo))
                    nc.vector.scalar_tensor_tensor(lo, ffn_ps[h][:], X_SCALE, hi, ALU.mult, ALU.subtract).then_inc(
                        x2t_lo_done, 1)

            def norm_stats(which, m, tile):
                for h in range(2):
                    bn = nc.vector.bn_stats(stats[:, which, h, :], tile[:, halves[h]])
                bn.then_inc(stats_done, 1)
                dve.wait_ge(stats_done, 1)
                dve.sem_clear(stats_done)
                nc.vector.bn_aggr(moments[:, which, :], stats[:, which].rearrange("p h e -> p (h e)")).then_inc(
                    moments_done[which], 1)

            def attention_out(m, r, h):
                dve.wait_ge(proj_done, 2 * m + 1 + h)
                nc.vector.scalar_tensor_tensor(attn[r % 2][:, halves[h]], proj_ps[h][:], OUT_UNSCALE,
                                               bo_row[:, halves[h]], ALU.mult, ALU.add).then_inc(attn_done, 1)

            def attention_stats(m, r):
                dve.wait_ge(attn_done, 2 * m + 2)
                norm_stats(0, m, attn[r % 2])

            def x1_stats(m, r):
                dve.wait_ge(x1_done, m + 1)
                norm_stats(1, m, x1[r])

            GATE_STEPS = 19

            def gates(m, r):
                count = [0]

                def step(op):
                    count[0] += 1
                    op.then_inc(gate_step, 1)

                def settled():
                    dve.wait_ge(gate_step, GATE_STEPS * m + count[0])
                num, dist, inv, score, off, logit, gate1, gate, first, chosen = (select[:, i, :] for i in range(10))
                dve.wait_ge(dots_ps_done, m + 1)
                dve.wait_ge(norm2_done, m + 1)
                step(nc.vector.scalar_tensor_tensor(dots[:], dots_ps[:, 0:128], DOTS_UNSCALE, offsets[:, 0:128], ALU.mult,
                                                    ALU.subtract))
                step(nc.vector.scalar_tensor_tensor(dist, dots_ps[:, DIF], -2.0 * DOTS_UNSCALE, offsets[:, DIF], ALU.mult,
                                                    ALU.add))
                settled()
                step(nc.vector.tensor_tensor(dots2[:], dots[:, SEL], dots[:, SEL], ALU.mult))
                step(nc.vector.tensor_scalar(dist, dist, x2_norm2[r][:], None, ALU.add))
                settled()
                step(nc.vector.tensor_reduce(num, dots2[:].rearrange("p (n s) -> p n s", n=N_EXP), AX_X, ALU.add))
                step(nc.vector.reciprocal(inv, dist))
                settled()
                step(nc.vector.tensor_tensor(score, num, inv, ALU.mult))
                settled()
                step(nc.vector.tensor_tensor(off, score, center_row[:], ALU.subtract))
                settled()
                nc.vector.tensor_tensor(logit, off, slope_row[:], ALU.mult).then_inc(logit_done, 1)
                dve.wait_ge(gate_exp_done, m + 1)
                step(nc.vector.tensor_scalar(gate1, gate1, 1.0, None, ALU.add))
                settled()
                step(nc.vector.reciprocal(gate, gate1))
                settled()
                if not isinstance(m, int) or m >= 2:
                    dve.wait_ge(y_done, m - 1)
                    dve.wait_ge(mixed_done, 2 * m - 2)
                step(nc.vector.tensor_reduce(sel_scale[r % 2][:], gate, AX_X, ALU.max))
                settled()
                step(nc.vector.tensor_scalar(sel_out[r % 2][:], sel_scale[r % 2][:], 1.0 / W_SCALE, None, ALU.mult))
                step(nc.vector.tensor_scalar(sel_rest[r % 2][:], sel_scale[r % 2][:], -1.0, 1.0, ALU.mult, ALU.add))
                step(nc.vector.scalar_tensor_tensor(first, gate, sel_scale[r % 2][:], rank[:], ALU.is_equal, ALU.mult))
                settled()
                step(nc.vector.tensor_reduce(top_rank[:], first, AX_X, ALU.max))
                settled()
                if not isinstance(m, int) or m >= 1:
                    dve.wait_ge(mix_ps_done, m)
                bias_ones = mix[:, P + BIAS_HI:2 * P].rearrange("p (a n) -> p a n", a=2)[:, :, 0:N_EXP]
                step(nc.vector.tensor_scalar(bias_ones, rank[:].unsqueeze(1).broadcast_to([P, 2, N_EXP]), top_rank[:], None,
                                             ALU.is_equal))
                step(nc.vector.tensor_scalar(chosen, rank[:], top_rank[:], None, ALU.is_equal))
                settled()
                step(nc.vector.tensor_tensor(low_rank[:].rearrange("p (n h) -> p n h", n=N_EXP),
                                             dots[:, LOW].rearrange("p (n h) -> p n h", n=N_EXP),
                                             chosen.unsqueeze(2).broadcast_to([P, N_EXP, N_LOW]), ALU.mult))
                settled()
                low_hi = mix[:].rearrange("p (a n) -> p a n", a=2)[:, :, 0:LOWS]
                step(nc.vector.tensor_copy(low_hi, low_rank[:].unsqueeze(1).broadcast_to([P, 2, LOWS])))
                settled()
                assert count[0] == GATE_STEPS, count
                nc.vector.tensor_tensor(mix[:, LOWS:P], low_rank[:], mix[:, 0:LOWS], ALU.subtract).then_inc(mix_done, 1)

            def ffn_out(m, r):
                dve.wait_ge(mixed_done, 2 * m + 2)
                nc.vector.scalar_tensor_tensor(y[r % 2][:], x2[r][:], sel_rest[r % 2][:], mixed[r % 2][:], ALU.mult,
                                               ALU.add).then_inc(y_done, 1)
                dve.wait_ge(y_done, m + 1)
                norm_stats(2, m, y[r % 2])

            def step(m, t, r, has):
                if has(-1):
                    attention_out(m - 1, (r + 3) % 4, 1)
                    attention_stats(m - 1, (r + 3) % 4)
                if has(-2):
                    x2_low(m - 2)
                if has(-4):
                    ffn_out(m - 4, r)
                if has(1):
                    attention_low(m + 1, (r + 1) % 4)
                if has(-1):
                    x1_stats(m - 1, (r + 3) % 4)
                if has(0):
                    attention_out(m, r, 0)
                if has(-2):
                    gates(m - 2, (r + 2) % 4)

            attention_low(0, 0)
            dve.wait_ge(own_ps_done, 1)
            nc.vector.tensor_tensor(own_dots[:], dots_ps[0:2 * N_EXP, :], own[:], ALU.mult).then_inc(own_done, 1)
            dve.wait_ge(offsets_ps_done, 1)
            nc.vector.tensor_copy(offsets[:], dots_ps[:]).then_inc(offsets_done, 1)
            dve.wait_ge(offsets_done, 1)
            tiles(dve, step)

        @block.scalar
        def _(act):
            def attention_high(m, r):
                for h in range(2):
                    act.wait_ge(ot_ps_done, 2 * m + 1 + h)
                    if h == 0 and (not isinstance(m, int) or m >= 2):
                        act.wait_ge(proj_done, 2 * m - 2)
                    nc.scalar.activation(ot_hi[r % 2][:, 4 * h:4 * h + 4, :].rearrange("p k n -> p (k n)"), ot_ps[h][:],
                                         ACT.Copy).then_inc(ot_hi_done, 1)

            def attention_norm(m, r):
                act.wait_ge(shift_done[0], m + 1)
                nc.scalar.activation(attn[r % 2][:], attn[r % 2][:], ACT.Identity, bias=shift[:, 0:1],
                                     scale=rstd[:, 0:1]).then_inc(attn_norm_done, 1)

            def x2_norm(m, r):
                act.wait_ge(shift_done[1], m + 1)
                nc.scalar.activation(x2[r][:], x1[r][:], ACT.Identity, bias=shift[:, 1:2],
                                     scale=rstd[:, 1:2]).then_inc(x2_done, 1)

            def x2_square(m, r):
                act.wait_ge(x2_done, m + 1)
                nc.scalar.activation(square[:], x2[r][:], ACT.Square, accum_out=x2_norm2[r][:]).then_inc(norm2_done, 1)

            def x2_transposed(m):
                for h in range(2):
                    act.wait_ge(x2t_ps_done, 2 * m + 1 + h)
                    if h == 0 and (not isinstance(m, int) or m >= 1):
                        act.wait_ge(dots_ps_done, m)
                    nc.scalar.activation(x2t_hi[:, 4 * h:4 * h + 4, :].rearrange("p k n -> p (k n)"), ffn_ps[h][:],
                                         ACT.Copy, scale=X_SCALE).then_inc(x2t_hi_done, 1)

            def gate_exp(m):
                act.wait_ge(logit_done, m + 1)
                nc.scalar.activation(select[:, 6, :], select[:, 5, :], ACT.Exp, scale=-1.0).then_inc(gate_exp_done, 1)

            def mix_transposed(m):
                act.wait_ge(mix_ps_done, m + 1)
                if not isinstance(m, int) or m >= 1:
                    act.wait_ge(ffn_done, 2 * m)
                nc.scalar.activation(mix_t[:], mix_ps[:], ACT.Copy).then_inc(mix_t_done, 1)

            def ffn_gated(m, r):
                for h in range(2):
                    act.wait_ge(ffn_done, 2 * m + 1 + h)
                    if h == 0 and (not isinstance(m, int) or m >= 2):
                        act.wait_ge(y_done, m - 1)
                    nc.scalar.activation(mixed[r % 2][:, halves[h]], ffn_ps[h][:], ACT.Copy,
                                         scale=sel_out[r % 2][:]).then_inc(mixed_done, 1)

            def ffn_norm(m, r):
                act.wait_ge(shift_done[2], m + 1)
                nc.scalar.activation(y[r % 2][:], y[r % 2][:], ACT.Identity, bias=shift[:, 2:3],
                                     scale=rstd[:, 2:3]).then_inc(y_norm_done, 1)

            def step(m, t, r, has):
                if has(-2):
                    x2_transposed(m - 2)
                if has(-3):
                    mix_transposed(m - 3)
                if has(1):
                    attention_high(m + 1, (r + 1) % 4)
                if has(-1):
                    attention_norm(m - 1, (r + 3) % 4)
                if has(-4):
                    ffn_norm(m - 4, r)
                if has(-1):
                    x2_norm(m - 1, (r + 3) % 4)
                if has(-2):
                    gate_exp(m - 2)
                if has(-3):
                    ffn_gated(m - 3, (r + 1) % 4)
                if has(-1):
                    x2_square(m - 1, (r + 3) % 4)

            attention_high(0, 0)
            tiles(act, step)

        @block.gpsimd
        def _(pool):
            nc.gpsimd.memset(eps[:], EPS).then_inc(set_done, 1)
            nc.gpsimd.memset(minus_half[:], -0.5).then_inc(set_done, 1)
            pool.wait_ge(set_done, 2)
            for i in range(2):
                pool.sem_inc(stored[i], 16)
            pool.sem_inc(tile_loaded[0], 32)

            def norm_scale(which, m):
                pool.wait_ge(moments_done[which], m + 1)
                w = slice(which, which + 1)
                nc.gpsimd.tensor_tensor(var_eps[:, w], moments[:, which, 1:2], eps[:], ALU.add).then_inc(
                    var_done[which], 1)
                nc.gpsimd.tensor_scalar(neg_mean[:, w], moments[:, which, 0:1], -1.0, None, ALU.mult).then_inc(
                    var_done[which], 1)
                pool.wait_ge(var_done[which], 2 * m + 2)
                nc.gpsimd.tensor_tensor(rstd[:, w], var_eps[:, w], minus_half[:], ALU.pow).then_inc(
                    rstd_done[which], 1)
                pool.wait_ge(rstd_done[which], m + 1)
                nc.gpsimd.tensor_tensor(shift[:, w], neg_mean[:, w], rstd[:, w], ALU.mult).then_inc(
                    shift_done[which], 1)

            def residual(m, r):
                pool.wait_ge(attn_norm_done, m + 1)
                nc.gpsimd.tensor_tensor(x1[r][:], x_in[r][:], attn[r % 2][:], ALU.add).then_inc(x1_done, 1)

            def final(m, r):
                pool.wait_ge(y_norm_done, m + 1)
                pool.wait_ge(stored[r % 2], stores(m, r))
                nc.gpsimd.tensor_tensor(result[r % 2][:], x1[r][:], y[r % 2][:], ALU.add).then_inc(result_done, 1)

            def stores(m, r):
                return 16 * (m // 2 + 1) if isinstance(m, int) else 8 * (m - r % 2) + 16

            def step(m, t, r, has):
                if has(-1):
                    norm_scale(0, m - 1)
                    residual(m - 1, (r + 3) % 4)
                if has(-4):
                    norm_scale(2, m - 4)
                if has(-1):
                    norm_scale(1, m - 1)
                if has(-4):
                    final(m - 4, r)
            tiles(pool, step)


def attention_ffn(nc, x, w_qkv, b_cols, b_v, w_o, b_o, ffn_in, ffn_probe, ffn_mix, center, slope, ident, mask, own, rank,
                  out):
    q_scratch = nc.dram_tensor("q_scratch", (NC, BH, HD, 2, TOK), F16, kind="Internal").ap()
    k_scratch = nc.dram_tensor("k_scratch", (NC, BH, HD, 2, TOK), F16, kind="Internal").ap()
    v_scratch = nc.dram_tensor("v_scratch", (BH, P, QT, 2 * HD), F16, kind="Internal").ap()
    o_scratch = nc.dram_tensor("o_scratch", (BH, P, QT * HD), F32, kind="Internal").ap()
    project_phase(nc, x, w_qkv, b_cols, b_v, ident, q_scratch, k_scratch, v_scratch)
    with ExitStack() as ctx:
        fin = finish_inputs(nc, ctx, x, o_scratch, w_o, b_o, ident, ffn_in, ffn_probe, ffn_mix, own, rank, center, slope)
        attend_phase(nc, q_scratch, k_scratch, v_scratch, o_scratch, mask, fin)
        finish_phase(nc, fin, out)


def kernel(L0_attn_x, L0_attn_wq, L0_attn_bq, L0_attn_wk, L0_attn_bk, L0_attn_wv, L0_attn_bv, L0_attn_wo, L0_attn_bo,
           L0_ffn_select_weight, L0_ffn_select_mean_diff, L0_ffn_imp_center, L0_ffn_imp_slope, L0_ffn_lora_update,
           L0_ffn_lora_degen, L0_ffn_bias_w, L0_ffn_debias_w):
    import ml_dtypes
    import numpy as np
    import concourse.bacc as bacc
    from concourse.bass_utils import run_bass_kernel_spmd

    a = np.asarray
    by_column = lambda w: a(w).transpose(1, 0, 2).reshape(D, -1)
    expert = np.concatenate([np.repeat(np.arange(N_EXP), N_SEL), N_EXP + np.repeat(np.arange(N_EXP), N_LOW),
                             np.arange(N_EXP)])
    arrays = {
        "x": a(L0_attn_x).reshape(B * S, D),
        "w_qkv": np.stack([a(w).T for w in (L0_attn_wq, L0_attn_wk, L0_attn_wv)]),
        "b_cols": np.concatenate([a(L0_attn_bq).reshape(KT, P), a(L0_attn_bk).reshape(KT, P)]).T,
        "b_v": a(L0_attn_bv),
        "w_o": a(L0_attn_wo).T,
        "b_o": a(L0_attn_bo),
        "ffn_in": np.concatenate([by_column(L0_ffn_select_weight), by_column(L0_ffn_lora_update),
                                  a(L0_ffn_select_mean_diff).T], axis=1),
        "ffn_probe": np.concatenate([a(L0_ffn_select_mean_diff).T, a(L0_ffn_debias_w).T], axis=1),
        "ffn_mix": np.concatenate([a(L0_ffn_lora_degen).transpose(0, 2, 1).reshape(-1, D), a(L0_ffn_bias_w)]),
        "center": a(L0_ffn_imp_center),
        "slope": a(L0_ffn_imp_slope),
        "ident": np.eye(P, dtype=np.float32),
        "mask": np.where(np.arange(P)[None, :] > np.arange(P)[:, None], -1e30, 0.0).astype(ml_dtypes.bfloat16),
        "own": (np.arange(2 * N_EXP)[:, None] == expert[None, :]).astype(np.float32),
        "rank": np.broadcast_to(np.arange(N_EXP, 0, -1, dtype=np.float32), (P, N_EXP)),
    }
    nc = bacc.Bacc("TRN2", target_bir_lowering=False, num_devices=1)
    given, aps = {}, []
    for name, array in arrays.items():
        array = np.ascontiguousarray(array)
        given[f"in_{name}"] = array
        aps.append(nc.dram_tensor(f"in_{name}", array.shape, mybir.dt.from_np(array.dtype), kind="ExternalInput").ap())
    aps.append(nc.dram_tensor("out", (B * S, D), F32, kind="ExternalOutput").ap())
    attention_ffn(nc, *aps)
    result = run_bass_kernel_spmd(nc, [given], core_ids=[0])
    return result.results[0]["out"].reshape(B, S, D)
```
